# Optimizing a Trainium2 kernel written in Bass

```python
import numpy as np
import jax
import jax.numpy as jnp

def _softmax(x, axis=-1):
    return jax.nn.softmax(x, axis=axis)

def _gelu(x):
    return jax.nn.gelu(x, approximate=True)

def _silu(x):
    return jax.nn.silu(x)

def _sigmoid(x):
    return jax.nn.sigmoid(x)

def _layernorm(x, axis=-1, eps=1e-05):
    m = jnp.mean(x, axis=axis, keepdims=True)
    v = jnp.var(x, axis=axis, keepdims=True)
    return (x - m) / jnp.sqrt(v + eps)

def _scatter_add(tgt, idx, src, axis=0):
    return tgt.at[idx].add(src)

def _segment_sum(src, seg, n):
    return jax.ops.segment_sum(src, seg, n)
kernel_name = 'mk_conv_attn_hybrid_d2_conv_nchw768_r2_216f9c'

def setup_inputs(seed: int=0):
    np.random.seed(seed)
    _w = jnp.asarray

    def _rec_inputs():
        import jax
        import jax.numpy as jnp
        _gk = jax.random.key(seed)
        x = -0.0001538 + 1 * jax.random.normal(jax.random.fold_in(_gk, 1), (8, 384, 32, 32), jnp.float32)
        return x
    x = _rec_inputs()

    def _L0_conv_setup():
        import jax, jax.numpy as jnp
        import numpy as np
        B, C, H, W = (8, 384, 32, 32)
        CO, KS = (384, 3)

        def _conv(x, w, b):
            y = jax.lax.conv_general_dilated(x, w, (1, 1), [(1, 1), (1, 1)], dimension_numbers=('NCHW', 'OIHW', 'NCHW'))
            return y + b[None, :, None, None]

        def _deform_conv(x, offset, mask, w, b):
            b_, c_, h_, w_ = x.shape
            co, _, kh, kw = w.shape
            K = kh * kw
            off = offset.reshape(b_, K, 2, h_, w_)
            ky = (jnp.arange(K) // kw).astype(x.dtype)
            kx = (jnp.arange(K) % kw).astype(x.dtype)
            py = off[:, :, 0] + (jnp.arange(h_, dtype=x.dtype) - 1.0)[None, None, :, None] + ky[None, :, None, None]
            px = off[:, :, 1] + (jnp.arange(w_, dtype=x.dtype) - 1.0)[None, None, None, :] + kx[None, :, None, None]
            y0 = jnp.floor(py)
            x0 = jnp.floor(px)
            wy1 = py - y0
            wx1 = px - x0
            y0i = y0.astype(jnp.int32)
            x0i = x0.astype(jnp.int32)

            def corner(yi, xi, wt):
                valid = (yi >= 0) & (yi < h_) & (xi >= 0) & (xi < w_)
                yc = jnp.clip(yi, 0, h_ - 1)
                xc = jnp.clip(xi, 0, w_ - 1)
                g = jax.vmap(lambda im, yy, xx: im[:, yy, xx])(x, yc, xc)
                return g * (wt * valid)[:, None]
            p = corner(y0i, x0i, (1.0 - wy1) * (1.0 - wx1) * mask) + corner(y0i, x0i + 1, (1.0 - wy1) * wx1 * mask) + corner(y0i + 1, x0i, wy1 * (1.0 - wx1) * mask) + corner(y0i + 1, x0i + 1, wy1 * wx1 * mask)
            out = jnp.einsum('bckhw,ock->bohw', p, w.reshape(co, c_, K))
            return out + b[None, :, None, None]
        key = jax.random.key(seed)
        ks = jax.random.split(key, 6)
        x = jax.random.normal(ks[0], (B, C, H, W), jnp.float32)
        proj_w = jax.random.normal(ks[1], (CO, C, KS, KS), jnp.float32) * 0.02
        proj_b = jnp.zeros((CO,), jnp.float32)
        off_w = jax.random.normal(ks[2], (2 * KS * KS, C, KS, KS), jnp.float32) * 0.01
        off_b = jax.random.normal(ks[3], (2 * KS * KS,), jnp.float32) * 0.01
        mask_w = jax.random.normal(ks[4], (KS * KS, C, KS, KS), jnp.float32) * 0.01
        mask_b = jax.random.normal(ks[5], (KS * KS,), jnp.float32) * 0.01
        gamma = jnp.ones((CO,), jnp.float32)
        beta = jnp.zeros((CO,), jnp.float32)
        return {'x': x, 'proj_w': proj_w, 'proj_b': proj_b, 'off_w': off_w, 'off_b': off_b, 'mask_w': mask_w, 'mask_b': mask_b, 'gamma': gamma, 'beta': beta}
    _L0_conv_all = _L0_conv_setup()
    _L0_conv_in = {k: v for k, v in _L0_conv_all.items() if k in ('proj_w', 'proj_b', 'off_w', 'off_b', 'mask_w', 'mask_b', 'gamma', 'beta')}
    del _L0_conv_all

    def _L1_attn_setup():
        import jax, jax.numpy as jnp
        import numpy as np
        import math
        N_HEAD = 12
        BLOCK = 128
        EPS = 1e-06

        def _rotate(x):
            a = x[..., 0::2]
            b = x[..., 1::2]
            return jnp.stack([-b, a], axis=-1).reshape(x.shape)
        key = jax.random.key(seed)
        k1, k2, k3 = jax.random.split(key, 3)
        B, T, C = (4, 4096, 384)
        s = 0.02
        return {'x': jax.random.normal(k1, (B, T, C), jnp.float32), 'w_qkv': jax.random.normal(k2, (C, 3 * C), jnp.float32) * s, 'w_ln': jnp.ones((C,), jnp.float32), 'w_proj': jax.random.normal(k3, (C, C), jnp.float32) * s}
    _L1_attn_all = _L1_attn_setup()
    _L1_attn_in = {k: v for k, v in _L1_attn_all.items() if k in ('w_qkv', 'w_ln', 'w_proj')}
    del _L1_attn_all

    def _L1_ffn_setup():
        import jax, jax.numpy as jnp
        import numpy as np
        H = 12
        D = 32
        K = 6
        EPS = 1e-12
        key = jax.random.key(seed)
        ks = jax.random.split(key, 8)
        hid = H * D
        sc = 0.02
        return {'hidden_states': jax.random.normal(ks[0], (8, 512, hid), jnp.float32), 'Wq': jax.random.normal(ks[1], (hid, hid), jnp.float32) * sc, 'bq': jnp.zeros((hid,), jnp.float32), 'Wk': jax.random.normal(ks[2], (hid, hid), jnp.float32) * sc, 'bk': jnp.zeros((hid,), jnp.float32), 'Wv': jax.random.normal(ks[3], (hid, hid), jnp.float32) * sc, 'bv': jnp.zeros((hid,), jnp.float32), 'Wr': jax.random.normal(ks[4], (hid, H), jnp.float32) * sc, 'br': jnp.zeros((H,), jnp.float32), 'Wo': jax.random.normal(ks[5], (hid, hid), jnp.float32) * sc, 'bo': jnp.zeros((hid,), jnp.float32), 'ln_g': jnp.ones((hid,), jnp.float32), 'ln_b': jnp.zeros((hid,), jnp.float32)}
    _L1_ffn_all = _L1_ffn_setup()
    _L1_ffn_in = {k: v for k, v in _L1_ffn_all.items() if k in ('Wq', 'bq', 'Wk', 'bk', 'Wv', 'bv', 'Wr', 'br', 'Wo', 'bo', 'ln_g', 'ln_b')}
    del _L1_ffn_all
    return {'x': x, 'L0_conv_proj_w': _L0_conv_in['proj_w'], 'L0_conv_proj_b': _L0_conv_in['proj_b'], 'L0_conv_off_w': _L0_conv_in['off_w'], 'L0_conv_off_b': _L0_conv_in['off_b'], 'L0_conv_mask_w': _L0_conv_in['mask_w'], 'L0_conv_mask_b': _L0_conv_in['mask_b'], 'L0_conv_gamma': _L0_conv_in['gamma'], 'L0_conv_beta': _L0_conv_in['beta'], 'L1_attn_w_qkv': _L1_attn_in['w_qkv'], 'L1_attn_w_ln': _L1_attn_in['w_ln'], 'L1_attn_w_proj': _L1_attn_in['w_proj'], 'L1_ffn_Wq': _L1_ffn_in['Wq'], 'L1_ffn_bq': _L1_ffn_in['bq'], 'L1_ffn_Wk': _L1_ffn_in['Wk'], 'L1_ffn_bk': _L1_ffn_in['bk'], 'L1_ffn_Wv': _L1_ffn_in['Wv'], 'L1_ffn_bv': _L1_ffn_in['bv'], 'L1_ffn_Wr': _L1_ffn_in['Wr'], 'L1_ffn_br': _L1_ffn_in['br'], 'L1_ffn_Wo': _L1_ffn_in['Wo'], 'L1_ffn_bo': _L1_ffn_in['bo'], 'L1_ffn_ln_g': _L1_ffn_in['ln_g'], 'L1_ffn_ln_b': _L1_ffn_in['ln_b']}

def reference(x, L0_conv_proj_w, L0_conv_proj_b, L0_conv_off_w, L0_conv_off_b, L0_conv_mask_w, L0_conv_mask_b, L0_conv_gamma, L0_conv_beta, L1_attn_w_qkv, L1_attn_w_ln, L1_attn_w_proj, L1_ffn_Wq, L1_ffn_bq, L1_ffn_Wk, L1_ffn_bk, L1_ffn_Wv, L1_ffn_bv, L1_ffn_Wr, L1_ffn_br, L1_ffn_Wo, L1_ffn_bo, L1_ffn_ln_g, L1_ffn_ln_b):
    import jax
    import jax.numpy as jnp

    def _L0_conv_ref(x, proj_w, proj_b, off_w, off_b, mask_w, mask_b, gamma, beta):
        import jax, jax.numpy as jnp
        import numpy as np
        B, C, H, W = (8, 384, 32, 32)
        CO, KS = (384, 3)

        def _conv(x, w, b):
            y = jax.lax.conv_general_dilated(x, w, (1, 1), [(1, 1), (1, 1)], dimension_numbers=('NCHW', 'OIHW', 'NCHW'))
            return y + b[None, :, None, None]

        def _deform_conv(x, offset, mask, w, b):
            b_, c_, h_, w_ = x.shape
            co, _, kh, kw = w.shape
            K = kh * kw
            off = offset.reshape(b_, K, 2, h_, w_)
            ky = (jnp.arange(K) // kw).astype(x.dtype)
            kx = (jnp.arange(K) % kw).astype(x.dtype)
            py = off[:, :, 0] + (jnp.arange(h_, dtype=x.dtype) - 1.0)[None, None, :, None] + ky[None, :, None, None]
            px = off[:, :, 1] + (jnp.arange(w_, dtype=x.dtype) - 1.0)[None, None, None, :] + kx[None, :, None, None]
            y0 = jnp.floor(py)
            x0 = jnp.floor(px)
            wy1 = py - y0
            wx1 = px - x0
            y0i = y0.astype(jnp.int32)
            x0i = x0.astype(jnp.int32)

            def corner(yi, xi, wt):
                valid = (yi >= 0) & (yi < h_) & (xi >= 0) & (xi < w_)
                yc = jnp.clip(yi, 0, h_ - 1)
                xc = jnp.clip(xi, 0, w_ - 1)
                g = jax.vmap(lambda im, yy, xx: im[:, yy, xx])(x, yc, xc)
                return g * (wt * valid)[:, None]
            p = corner(y0i, x0i, (1.0 - wy1) * (1.0 - wx1) * mask) + corner(y0i, x0i + 1, (1.0 - wy1) * wx1 * mask) + corner(y0i + 1, x0i, wy1 * (1.0 - wx1) * mask) + corner(y0i + 1, x0i + 1, wy1 * wx1 * mask)
            out = jnp.einsum('bckhw,ock->bohw', p, w.reshape(co, c_, K))
            return out + b[None, :, None, None]
        h, w = (x.shape[-2], x.shape[-1])
        max_off = float(min(h, w) // 4)
        offset = jnp.clip(_conv(x, off_w, off_b), -max_off, max_off)
        mask = 2.0 * jax.nn.sigmoid(_conv(x, mask_w, mask_b))
        y = _deform_conv(x, offset, mask, proj_w, proj_b)
        mean = y.mean(axis=(0, 2, 3))
        var = y.var(axis=(0, 2, 3))
        yn = (y - mean[None, :, None, None]) * jax.lax.rsqrt(var + 1e-05)[None, :, None, None]
        yn = yn * gamma[None, :, None, None] + beta[None, :, None, None]
        return jax.nn.gelu(yn, approximate=False)

    def _L1_attn_ref(x, w_qkv, w_ln, w_proj):
        import jax, jax.numpy as jnp
        import numpy as np
        import math
        N_HEAD = 12
        BLOCK = 128
        EPS = 1e-06

        def _rotate(x):
            a = x[..., 0::2]
            b = x[..., 1::2]
            return jnp.stack([-b, a], axis=-1).reshape(x.shape)
        B, T, C = x.shape
        nh, ls = (N_HEAD, BLOCK)
        hd = C // nh
        ng = T // ls
        xb = x.reshape(B, ng, ls, C)
        qkv = xb @ w_qkv
        q, k, v = jnp.split(qkv, 3, axis=-1)

        def rms(t):
            return t * jax.lax.rsqrt(jnp.mean(t * t, axis=-1, keepdims=True) + EPS) * w_ln
        q, k = (rms(q), rms(k))

        def heads(t):
            return jnp.swapaxes(t.reshape(B, ng, ls, nh, hd), 2, 3)
        q, k, v = (heads(q), heads(k), heads(v))
        pos = 10000.0 ** ((-2.0 * jnp.arange(0, hd, 2, dtype=jnp.float32) - 1.0) / hd)
        ts = jnp.arange(ls, dtype=jnp.float32)[:, None] * pos[None, :]
        rot = jnp.concatenate([ts, ts], axis=-1)
        cos, sin = (jnp.cos(rot), jnp.sin(rot))
        q = q * cos + _rotate(q) * sin
        k = k * cos + _rotate(k) * sin
        scale = 1.0 / math.sqrt(hd)
        att = jnp.einsum('bgnqd,bgnkd->bgnqk', q, k) * scale
        mask = jnp.tril(jnp.ones((ls, ls), dtype=bool))
        att = jnp.where(mask, att, -jnp.finfo(att.dtype).max)
        att = jax.nn.softmax(att, axis=-1)
        y = jnp.einsum('bgnqk,bgnkd->bgnqd', att, v)
        y = jnp.swapaxes(y, 2, 3).reshape(B, ng, ls, C)
        y = y @ w_proj
        return y.reshape(B, T, C)

    def _L1_ffn_ref(hidden_states, Wq, bq, Wk, bk, Wv, bv, Wr, br, Wo, bo, ln_g, ln_b):
        import jax, jax.numpy as jnp
        import numpy as np
        H = 12
        D = 32
        K = 6
        EPS = 1e-12
        B, S, hid = hidden_states.shape
        router_in = hidden_states.mean(axis=1)
        logits = router_in @ Wr + br
        _, top_idx = jax.lax.top_k(logits, K)
        hard = jax.nn.one_hot(top_idx, H, dtype=logits.dtype).sum(axis=1)
        head_mask = hard + logits - jax.lax.stop_gradient(logits)
        m = head_mask[:, :, None, None]

        def proj(W, b):
            return (hidden_states @ W + b).reshape(B, S, H, D).transpose(0, 2, 1, 3)
        q = proj(Wq, bq) * m
        k = proj(Wk, bk) * m
        v = proj(Wv, bv) * m
        scores = jnp.einsum('bhqd,bhkd->bhqk', q, k) / jnp.sqrt(jnp.float32(D))
        probs = jax.nn.softmax(scores, axis=-1)
        ctx = jnp.einsum('bhqk,bhkd->bhqd', probs, v)
        ctx = ctx.transpose(0, 2, 1, 3).reshape(B, S, hid)
        x = ctx @ Wo + bo + hidden_states
        mu = x.mean(axis=-1, keepdims=True)
        var = ((x - mu) ** 2).mean(axis=-1, keepdims=True)
        return (x - mu) / jnp.sqrt(var + EPS) * ln_g + ln_b

    def _gn(v, G=32, eps=1e-05):
        B_, C_, H_, W_ = v.shape
        g = v.reshape(B_, G, C_ // G, H_, W_)
        m = jnp.mean(g, axis=(2, 3, 4), keepdims=True)
        s = jnp.var(g, axis=(2, 3, 4), keepdims=True)
        return ((g - m) / jnp.sqrt(s + eps)).reshape(v.shape)

    def _ln_c(v, eps=1e-06):
        m = jnp.mean(v, axis=1, keepdims=True)
        s = jnp.var(v, axis=1, keepdims=True)
        return (v - m) / jnp.sqrt(s + eps)

    def _ln_t(v, eps=1e-05):
        m = jnp.mean(v, axis=-1, keepdims=True)
        s = jnp.var(v, axis=-1, keepdims=True)
        return (v - m) / jnp.sqrt(s + eps)

    def _to_tokens(v):
        B_, C_, H_, W_ = v.shape
        return v.reshape(B_, C_, H_ * W_).transpose(0, 2, 1)

    def _from_tokens(t, like):
        B_, C_, H_, W_ = like.shape
        return t.transpose(0, 2, 1).reshape(B_, C_, H_, W_)
    x = x + _L0_conv_ref(_gn(x), L0_conv_proj_w, L0_conv_proj_b, L0_conv_off_w, L0_conv_off_b, L0_conv_mask_w, L0_conv_mask_b, L0_conv_gamma, L0_conv_beta)
    t = _to_tokens(x)
    t = t + _L1_attn_ref(_ln_t(t), L1_attn_w_qkv, L1_attn_w_ln, L1_attn_w_proj)
    t = t + _L1_ffn_ref(_ln_t(t), L1_ffn_Wq, L1_ffn_bq, L1_ffn_Wk, L1_ffn_bk, L1_ffn_Wv, L1_ffn_bv, L1_ffn_Wr, L1_ffn_br, L1_ffn_Wo, L1_ffn_bo, L1_ffn_ln_g, L1_ffn_ln_b)
    x = _from_tokens(t, x)
    return x

_drawn_inputs = setup_inputs


def setup_inputs(seed=0):
    import zlib

    import numpy as np

    out = dict(_drawn_inputs(seed))
    spreads = {'L0_conv_proj_b': (0.0, 2.0),
     'L0_conv_gamma': (1.0, 0.2),
     'L0_conv_beta': (0.0, 0.1),
     'L1_attn_w_ln': (1.0, 0.6),
     'L1_ffn_bq': (0.0, 0.8),
     'L1_ffn_bk': (0.0, 2.0),
     'L1_ffn_bv': (0.0, 0.649),
     'L1_ffn_br': (0.0, 0.636),
     'L1_ffn_bo': (0.0, 0.473),
     'L1_ffn_ln_g': (1.0, 0.2),
     'L1_ffn_ln_b': (0.0, 0.1)}
    factors = {'L0_conv_off_b': 3.213,
     'L1_ffn_Wq': 8.0,
     'L1_ffn_Wk': 8.0,
     'L1_ffn_Wv': 8.0,
     'L1_ffn_Wr': 8.0,
     'L1_ffn_Wo': 4.338}
    for name, (base, spread) in spreads.items():
        noise = np.random.default_rng([zlib.crc32(name.encode()), seed]).standard_normal(out[name].shape)
        drawn = base * np.exp(spread * noise) if base else spread * noise
        out[name] = jnp.asarray(drawn.astype(out[name].dtype))
    for name, factor in factors.items():
        out[name] = (out[name] * factor).astype(out[name].dtype)
    return out
```

```python
from contextlib import ExitStack

import numpy as np
import concourse.bass as bass
from concourse import mybir
from concourse.alu_op_type import AluOpType as ALU

ACT = mybir.ActivationFunctionType
AX = mybir.AxisListType
F32 = mybir.dt.float32
BF16 = mybir.dt.bfloat16
U32 = mybir.dt.uint32

P = 128
BATCH, C, SIDE = 8, 384, 32
PIX = SIDE * SIDE
CH = C // P
TAPS = 9
TILES = PIX // P
BLOCKS = BATCH * TILES
GROUP = 4
GROUPS = BLOCKS // GROUP
PADW = SIDE + 2
MAX_OFF = float(SIDE // 4)
GN_GROUPS = 32
CORNERS = 4
CORNER_SHIFT = [0, 1, SIDE, SIDE + 1]
LEAD = SIDE + 1
IMG_ROWS = PIX + LEAD
HEADS, HD = 12, 32
KEPT = 6
ROUND = float(3 * 2 ** 22)

MASKED = -1e30


def shape_constants():
    f = np.float32
    ch = np.arange(C)
    same = (ch[:, None] // (C // GN_GROUPS) == ch[None, :] // (C // GN_GROUPS)).astype(f) / f(C // GN_GROUPS)
    p = np.arange(P)
    tile = np.arange(TILES)
    tap = np.arange(TAPS)
    row = (tile[None, :, None] * (P // SIDE) + p[:, None, None] // SIDE) - 1 + tap[None, None, :] // 3
    col = (p[:, None, None] % SIDE) - 1 + tap[None, None, :] % 3 + 0 * tile[None, :, None]
    pos = np.concatenate([row, col], axis=2).astype(f)
    rows0 = np.tile((np.arange(BATCH) * IMG_ROWS + LEAD).astype(f), (P, 1))
    freq = np.power(f(10000.0), (f(-2.0) * np.arange(0, HD, 2, dtype=f) - f(1.0)) / f(HD), dtype=f)
    ts = p.astype(f)[:, None] * freq[None, :]
    even = np.arange(0, HD, 2)
    channel = np.concatenate([even, even + 1]) % (HD // 2)
    cos, sin = np.cos(ts)[:, channel], np.sin(ts)[:, channel]
    sin = np.where(np.arange(HD) < HD // 2, -sin, sin)
    dim = np.arange(KEPT * HD)
    slot_of = np.where(dim[None, :] % HD == p[:, None] % HD, dim[None, :] // HD, -1)
    head_of = (np.arange(CH)[None, :, None] * P + p[:, None, None]) // HD == np.arange(HEADS)[None, None, :]
    before = np.arange(HEADS)[None, :] < np.arange(HEADS)[:, None]
    return {
        "slot_of": slot_of.astype(f),
        "head_of": head_of.astype(f),
        "before": np.tile(before.astype(f), (P, 1, 1)),
        "rot_cos": np.tile(cos, (1, HEADS)).astype(f),
        "rot_sin": np.tile(sin, (1, HEADS)).astype(f),
        "causal": np.where(p[None, :] <= p[:, None], f(0), f(MASKED)).astype(f),
        "ident": np.eye(P, dtype=f),
        "same_group": np.ascontiguousarray(same.reshape(CH, P, C).transpose(1, 0, 2)),
        "tap_pos": pos,
        "table_row0": rows0,
    }


STAGE = 3


class Chain:

    def __init__(self, eng, sem, base):
        self.eng, self.sem, self.base, self.n = eng, sem, base, 0

    def step(self, ins, apart=False):
        self.n += 1
        ins.then_inc(self.sem, 1)
        self.eng.wait_ge(self.sem, self.base + self.n)
        if apart:
            self.eng.nop(nofuse=True)


def build(nc, io):
    x_img = io["x"].rearrange("b (o p) h w -> b p o (h w)", p=P)
    out_img = io["out"].rearrange("b (o p) h w -> b p o (h w)", p=P)
    table = nc.dram_tensor("corner_table", (BATCH * IMG_ROWS, CORNERS * C), F32, kind="Internal").ap()

    with ExitStack() as whole:
        def sem(name):
            return whole.enter_context(nc.semaphore(name))

        def sb(stack, name, shape, dt=F32):
            return stack.enter_context(nc.sbuf_tensor(name, [P] + shape, dt))

        def bank(stack, name, dt=F32, width=512):
            return stack.enter_context(nc.psum_tensor(name, [P, width], dt))

        ident = sb(whole, "ident", [P])
        neg_half = sb(whole, "neg_half", [BLOCKS])
        y = sb(whole, "y", [BLOCKS, CH, P])
        conv_stats = sb(whole, "conv_stats", [CH, GROUPS, 6])
        with ExitStack() as conv:
            tap_index = sb(conv, "tap_index", [GROUPS + 1, TAPS, GROUP], U32)
            corner_w = sb(conv, "corner_w", [GROUPS, CORNERS, TAPS, GROUP])
            offsets_and_table(nc, io, sem, sb, bank, x_img, table, ident, tap_index, corner_w, neg_half, y)
            deform_conv(nc, io, sem, sb, bank, table, ident, tap_index, corner_w, y, conv_stats)
        token_stats = sb(whole, "token_stats", [BLOCKS, 2])
        token_rstd = sb(whole, "token_rstd", [BLOCKS])
        if STAGE >= 1:
            batch_norm_gelu(nc, io, sem, sb, bank, x_img, ident, neg_half, y, conv_stats, token_stats, token_rstd)
        if STAGE >= 2:
            block_attention(nc, io, sem, sb, bank, ident, neg_half, y, token_stats, token_rstd)
        if STAGE >= 3:
            head_attention(nc, io, sem, sb, bank, out_img, ident, neg_half, y, token_stats, token_rstd)
        if STAGE < 3:
            dump = sem("dump")
            with nc.Block() as block:
                @block.sync
                def _(sp):
                    if STAGE == 0:
                        o = out_img.rearrange("b p o (t q) -> b t p o q", q=P)
                    else:
                        o = io["out"].rearrange("b c h w -> (b c h w)").rearrange("(n p c) -> n p c", p=P, c=C)
                    for n in range(BLOCKS):
                        dst = o[n // TILES, n % TILES] if STAGE == 0 else o[n]
                        src = y[:, n, :, :] if STAGE == 0 else y[:, n].rearrange("p o q -> p (o q)")
                        sp.dma_start(dst, src).then_inc(dump, 16)
                    sp.wait_ge(dump, 16 * BLOCKS)


def offsets_and_table(nc, io, sem, sb, bank, x_img, table, ident, tap_index, corner_w, neg_half, y):
    NOUT = 3 * TAPS
    with ExitStack() as mem:
        x_in = [sb(mem, f"a_x{u}", [CH, PIX]) for u in range(2)]
        size = 3 * CH * PADW * SIDE
        y_flat = y[:].rearrange("p n o q -> p (n o q)")
        xpad = [y_flat[:, u * size:(u + 1) * size].rearrange("p (d o h w) -> p d o h w", d=3, o=CH, h=PADW)
                for u in range(2)]
        tok = [sb(mem, f"a_tok{u}", [TILES, C]) for u in range(2)]
        w_off = sb(mem, "a_w_off", [CH, TAPS, NOUT])
        b_off = sb(mem, "a_b_off", [NOUT])
        same_group = sb(mem, "a_same_group", [CH, C])
        tap_pos = sb(mem, "a_tap_pos", [TILES, 2 * TAPS])
        table_row0 = sb(mem, "a_table_row0", [BATCH])
        bst = sb(mem, "a_bst", [CH, 2, 6])
        mv = sb(mem, "a_mv", [CH, 2])
        stat = sb(mem, "a_stat", [CH, 2])
        gstat = sb(mem, "a_gstat", [CH, 2])
        gvar = sb(mem, "a_gvar", [CH])
        rstd = sb(mem, "a_rstd", [CH])
        shift = sb(mem, "a_shift", [CH])
        norm_scale = [sb(mem, f"a_ns{u}", [CH]) for u in range(2)]
        norm_shift = [sb(mem, f"a_nb{u}", [CH]) for u in range(2)]
        raw = sb(mem, "a_raw", [TILES, NOUT])
        pos = sb(mem, "a_pos", [TILES, 2 * TAPS])
        base = sb(mem, "a_base", [TILES, 2 * TAPS])
        dist = sb(mem, "a_dist", [2, TILES, 2 * TAPS])
        wgt = sb(mem, "a_wgt", [2, TILES, 2 * TAPS])
        mask = sb(mem, "a_mask", [TILES, TAPS])
        wy = sb(mem, "a_wy", [2, TILES, TAPS])
        row = sb(mem, "a_row", [TILES, TAPS])
        gps = bank(mem, "a_gps")
        offps = [bank(mem, f"a_offps{u}") for u in range(2)]
        tps = [bank(mem, f"a_tps{u}") for u in range(2)]

        consts = sem("a_consts")
        cleared = sem("a_cleared")
        x_loaded = [sem(f"a_x_loaded{u}") for u in range(2)]
        x_free = sem("a_x_free")
        xpad_free = sem("a_xpad_free")
        table_written = [sem(f"a_table_written{u}") for u in range(2)]
        stats_ready = sem("a_stats_ready")
        group_ready = sem("a_group_ready")
        var_ready = sem("a_var_ready")
        rstd_ready = sem("a_rstd_ready")
        norm_ready = sem("a_norm_ready")
        xn_ready = sem("a_xn_ready")
        tp_ready = sem("a_tp_ready")
        tp_free = sem("a_tp_free")
        off_ready = sem("a_off_ready")
        raw_ready = sem("a_raw_ready")
        mask_ready = sem("a_mask_ready")
        fchain = sem("a_fchain")
        bchain = sem("a_bchain")
        gaps_filled = sem("a_gaps_filled")
        NCONST = 6
        GAPS = 2 * (CORNERS - 1)
        img_rows = table.rearrange("(b r) c -> r b c", r=IMG_ROWS)

        with nc.Block() as block:
            @block.sync
            def _(sp):
                def load_x(j, u):
                    sp.wait_ge(x_free, 2 * j + u + 1)
                    sp.dma_start(x_in[u][:], x_img[2 * j + u]).then_inc(x_loaded[u], 16)

                sp.dma_start(ident[:], io["ident"]).then_inc(consts, 16)
                sp.dma_start(w_off[:], io["w_off"]).then_inc(consts, 16)
                sp.dma_start(b_off[:], io["b_off"]).then_inc(consts, 16)
                sp.dma_start(same_group[:], io["same_group"]).then_inc(consts, 16)
                sp.dma_start(tap_pos[:], io["tap_pos"]).then_inc(consts, 16)
                sp.dma_start(table_row0[:], io["table_row0"]).then_inc(consts, 16)
                for u in range(2):
                    load_x(0, u)
                sp.wait_ge(cleared, 5)
                for s, d in enumerate(CORNER_SHIFT):
                    for first, many in ((0, LEAD - d), (LEAD - d + PIX, d)):
                        if many:
                            sp.dma_start(img_rows[first:first + many, :, s * C:(s + 1) * C],
                                         tok[0][0:many]).then_inc(gaps_filled, 16)

                def turn(j, u, more):
                    if more:
                        load_x(j + 1, u)
                    sp.wait_ge(tp_free, TILES * (2 * j + u + 1) + 2)
                    for s, d in enumerate(CORNER_SHIFT):
                        first = (2 * j + u) * IMG_ROWS + LEAD - d
                        dst = table[bass.ds(first, PIX), s * C:(s + 1) * C].rearrange("(t p) c -> p t c", p=P)
                        sp.dma_start(dst, tok[u][:]).then_inc(table_written[u], 16)

                with sp.Fori(0, BATCH // 2 - 1) as j:
                    for u in range(2):
                        turn(j, u, True)
                for u in range(2):
                    turn(BATCH // 2 - 1, u, False)
                for u in range(2):
                    sp.wait_ge(table_written[u], 16 * CORNERS * BATCH // 2 + 1)

            @block.gpsimd
            def _(pool):
                nc.gpsimd.memset(tok[0][:], 0.0).then_inc(cleared, 1)
                nc.gpsimd.memset(neg_half[:], -0.5).then_inc(cleared, 1)
                nc.gpsimd.memset(tap_index[:, GROUPS], 0).then_inc(cleared, 1)
                for u in range(2):
                    nc.gpsimd.memset(xpad[u], 0.0).then_inc(cleared, 1)
                pool.wait_ge(cleared, 5)
                with pool.Fori(0, BATCH) as n:
                    pool.wait_ge(var_ready, n + 1)
                    nc.gpsimd.tensor_tensor(rstd[:], gvar[:], neg_half[:, 0:CH], ALU.pow).then_inc(rstd_ready, 1)

            @block.vector
            def _(dve):
                for u in range(2):
                    dve.sem_inc(table_written[u], 1)
                dve.sem_inc(x_free, 2)
                dve.sem_inc(xpad_free, 2)
                dve.sem_inc(tp_free, 2)
                dve.wait_ge(consts, 16 * NCONST)
                dve.wait_ge(gaps_filled, 16 * GAPS)

                def front(j, u):
                    n = 2 * j + u
                    c = Chain(dve, fchain, 7 * n)
                    dve.wait_ge(x_loaded[u], 16 * (j + 1))
                    for o in range(CH):
                        for h in range(2):
                            last = nc.vector.bn_stats(bst[:, o, h], x_in[u][:, o, h * 512:(h + 1) * 512])
                    c.step(last, apart=True)
                    for o in range(CH):
                        last = nc.vector.bn_aggr(mv[:, o], bst[:, o])
                    c.step(last)
                    nc.vector.tensor_copy(stat[:, :, 0], mv[:, :, 0])
                    c.step(nc.vector.tensor_tensor(stat[:, :, 1], mv[:, :, 0], mv[:, :, 0], ALU.mult))
                    nc.vector.tensor_tensor(stat[:, :, 1], stat[:, :, 1], mv[:, :, 1], ALU.add).then_inc(stats_ready, 1)
                    dve.wait_ge(group_ready, n + 1)
                    c.step(nc.vector.tensor_copy(gstat[:], gps[:, 0:2 * CH].rearrange("p (o s) -> p o s", s=2)))
                    c.step(nc.vector.tensor_tensor(gvar[:], gstat[:, :, 0], gstat[:, :, 0], ALU.mult))
                    c.step(nc.vector.tensor_tensor(gvar[:], gstat[:, :, 1], gvar[:], ALU.subtract))
                    nc.vector.tensor_scalar(gvar[:], gvar[:], 1e-5, None, ALU.add).then_inc(var_ready, 1)
                    dve.wait_ge(rstd_ready, n + 1)
                    dve.wait_ge(x_free, n + 1)
                    c.step(nc.vector.tensor_copy(norm_scale[u][:], rstd[:]))
                    nc.vector.scalar_tensor_tensor(norm_shift[u][:], gstat[:, :, 0], -1.0, rstd[:], ALU.mult,
                                                   ALU.mult).then_inc(norm_ready, 1)
                    assert c.n == 7

                def back(j, u):
                    n = 2 * j + u
                    c = Chain(dve, bchain, 14 * n)
                    dve.wait_ge(table_written[u], 16 * CORNERS * j + 1)
                    for i in range(TILES):
                        dve.wait_ge(tp_ready, TILES * n + i + 1)
                        nc.vector.tensor_copy(tok[u][:, i], tps[i % 2][:, 0:C]).then_inc(tp_free, 1)
                    dve.wait_ge(off_ready, n + 1)
                    c.step(nc.vector.tensor_tensor(
                        raw[:], offps[u][:, 0:TILES * NOUT].rearrange("p (t k) -> p t k", k=NOUT),
                        b_off[:].unsqueeze(1).to_broadcast([P, TILES, NOUT]), ALU.add))
                    dve.sem_inc(raw_ready, 1)
                    c.step(nc.vector.tensor_scalar(pos[:], raw[:, :, 0:2 * TAPS], -MAX_OFF, MAX_OFF, ALU.max, ALU.min))
                    c.step(nc.vector.tensor_tensor(pos[:], pos[:], tap_pos[:], ALU.add))
                    c.step(nc.vector.tensor_scalar(base[:], pos[:], 0.25, SIDE - 1.25, ALU.max, ALU.min))
                    c.step(nc.vector.tensor_scalar(base[:], base[:], -0.5, ROUND, ALU.add, ALU.add))
                    c.step(nc.vector.tensor_scalar(base[:], base[:], -ROUND, None, ALU.add))
                    c.step(nc.vector.tensor_tensor(dist[:, 0], pos[:], base[:], ALU.subtract))
                    c.step(nc.vector.tensor_scalar(dist[:, 1], dist[:, 0], -1.0, None, ALU.add))
                    c.step(nc.vector.tensor_scalar(wgt[:], dist[:], -1.0, 1.0, ALU.mult, ALU.add))
                    flat = "p s t k -> p (s t k)"
                    c.step(nc.vector.scalar_tensor_tensor(wgt[:].rearrange(flat), dist[:].rearrange(flat), 1.0,
                                                          wgt[:].rearrange(flat), ALU.add, ALU.min))
                    c.step(nc.vector.tensor_scalar(wgt[:], wgt[:], 0.0, None, ALU.max))
                    c.step(nc.vector.scalar_tensor_tensor(row[:], base[:, :, 0:TAPS], float(SIDE), base[:, :, TAPS:],
                                                          ALU.mult, ALU.add))
                    halves = "p (g i) k -> p g i k"
                    for g in range(2):
                        nc.vector.tensor_scalar(
                            tap_index[:, bass.ds(2 * n + g, 1)].rearrange("p g k i -> p (g i) k"),
                            row[:, g * GROUP:(g + 1) * GROUP], table_row0[:, bass.ds(n, 1)], None, ALU.add)
                    dve.wait_ge(mask_ready, n + 1)
                    for a in range(2):
                        last = nc.vector.scalar_tensor_tensor(wy[:, a], wgt[:, a, :, 0:TAPS], 2.0, mask[:],
                                                              ALU.mult, ALU.mult)
                    c.step(last)
                    for g in range(2):
                        for a in range(2):
                            for b in range(2):
                                rows = slice(g * GROUP, (g + 1) * GROUP)
                                last = nc.vector.tensor_tensor(
                                    corner_w[:, bass.ds(2 * n + g, 1), 2 * a + b].rearrange("p g k i -> p (g i) k"),
                                    wy[:, a, rows], wgt[:, b, rows, TAPS:], ALU.mult)
                    c.step(last)
                    assert c.n == 14

                front(0, 0)
                with dve.Fori(0, BATCH // 2 - 1) as j:
                    front(j, 1)
                    back(j, 0)
                    front(j + 1, 0)
                    back(j, 1)
                front(BATCH // 2 - 1, 1)
                back(BATCH // 2 - 1, 0)
                back(BATCH // 2 - 1, 1)

            @block.scalar
            def _(act):
                act.wait_ge(cleared, 5)

                def front(j, u):
                    n = 2 * j + u
                    act.wait_ge(norm_ready, n + 1)
                    act.wait_ge(xpad_free, n + 1)
                    for o in range(CH):
                        img = x_in[u][:, o].rearrange("p (h w) -> p h w", w=SIDE)
                        for dx in range(3):
                            to, fro, width = max(0, 1 - dx), max(0, dx - 1), SIDE - abs(dx - 1)
                            last = nc.scalar.activation(
                                xpad[u][:, dx, o, 1:1 + SIDE, to:to + width], img[:, :, fro:fro + width], ACT.Identity,
                                bias=norm_shift[u][:, o:o + 1], scale=norm_scale[u][:, o:o + 1])
                    last.then_inc(xn_ready, 1)
                    act.wait_ge(xn_ready, n + 1)
                    act.sem_inc(x_free, 1)

                def back(n):
                    act.wait_ge(raw_ready, n + 1)
                    nc.scalar.activation(mask[:], raw[:, :, 2 * TAPS:], ACT.Sigmoid).then_inc(mask_ready, 1)

                front(0, 0)
                with act.Fori(0, BATCH // 2 - 1) as j:
                    front(j, 1)
                    back(2 * j)
                    front(j + 1, 0)
                    back(2 * j + 1)
                front(BATCH // 2 - 1, 1)
                back(BATCH - 2)
                back(BATCH - 1)

            @block.tensor
            def _(pe):
                pe.wait_ge(consts, 16 * NCONST)

                def front(n):
                    pe.wait_ge(stats_ready, n + 1)
                    for co in range(CH):
                        for ci in range(CH):
                            last = nc.tensor.matmul(gps[:, 2 * co:2 * co + 2], same_group[:, ci, co * P:(co + 1) * P],
                                                    stat[:, ci, :], start=(ci == 0), stop=(ci == CH - 1))
                    last.then_inc(group_ready, 1)

                def back(j, u):
                    n = 2 * j + u
                    pe.wait_ge(xn_ready, n + 1)
                    flat = xpad[u].rearrange("p d o h w -> p d o (h w)")
                    for i in range(TILES):
                        pe.wait_ge(tp_free, TILES * n + i + 1)
                        for o in range(CH):
                            last = nc.tensor.transpose(tps[i % 2][:, o * P:(o + 1) * P],
                                                       flat[:, 1, o, SIDE + P * i:SIDE + P * (i + 1)],
                                                       ident[:])
                        last.then_inc(tp_ready, 1)
                        for t in range(TAPS):
                            for o in range(CH):
                                at = P * i + SIDE * (t // 3)
                                last = nc.tensor.matmul(offps[u][:, i * NOUT:(i + 1) * NOUT],
                                                        flat[:, t % 3, o, at:at + P],
                                                        w_off[:, o, t, :], start=(t == 0 and o == 0),
                                                        stop=(t == TAPS - 1 and o == CH - 1))
                    last.then_inc(off_ready, 1)
                    pe.wait_ge(off_ready, n + 1)
                    pe.sem_inc(xpad_free, 1)

                front(0)
                with pe.Fori(0, BATCH // 2 - 1) as j:
                    front(2 * j + 1)
                    back(j, 0)
                    front(2 * j + 2)
                    back(j, 1)
                front(BATCH - 1)
                back(BATCH // 2 - 1, 0)
                back(BATCH // 2 - 1, 1)


def deform_conv(nc, io, sem, sb, bank, table, ident, tap_index, corner_w, y, conv_stats):
    STEPS = 2 * TAPS
    TURN = STEPS * GROUP
    SLOTS = 4
    with ExitStack() as mem:
        w_conv = sb(mem, "b_w", [TAPS, CH, C])
        b_conv = sb(mem, "b_b", [CH])
        got = [sb(mem, f"b_got{s}", [CORNERS * C]) for s in range(SLOTS)]
        mix = [sb(mem, f"b_mix{s}", [C]) for s in range(SLOTS)]
        sampled = [sb(mem, f"b_sampled{u}", [CH, GROUP * P]) for u in range(2)]
        index = [sb(mem, f"b_index{g}", [TAPS, GROUP], U32) for g in range(2)]
        weight = sb(mem, "b_weight", [CORNERS, TAPS, GROUP])
        tps = [bank(mem, f"b_tps{u}") for u in range(2)]
        acc = [[bank(mem, f"b_acc{g}{o}") for o in range(CH)] for g in range(2)]

        consts = sem("b_consts")
        index_ready = sem("b_index_ready")
        gathered = [sem(f"b_gathered{s}") for s in range(SLOTS)]
        mixed = sem("b_mixed")
        transposed = sem("b_transposed")
        evacuated = sem("b_evacuated")
        tile_free = sem("b_tile_free")
        tps_free = sem("b_tps_free")
        sampled_free = sem("b_sampled_free")
        acc_ready = sem("b_acc_ready")
        acc_free = sem("b_acc_free")
        chain = sem("b_chain")
        gchain = sem("b_gchain")

        with nc.Block() as block:
            @block.sync
            def _(sp):
                sp.dma_start(w_conv[:], io["w_conv"]).then_inc(consts, 16)
                sp.dma_start(b_conv[:], io["b_conv"]).then_inc(consts, 16)

            @block.gpsimd
            def _(pool):
                with pool.Fori(0, BATCH) as n:
                    for t in range(TURN):
                        s, i = divmod(t, GROUP)
                        g, k = divmod(s, TAPS)
                        if t % (TURN // 2) == 0:
                            pool.wait_ge(index_ready, 2 * n + g + 1)
                        pool.wait_ge(tile_free, TURN * n + t + 1)
                        pool.nop(nofuse=True)
                        nc.gpsimd.indirect_dma_start(
                            out=got[t % SLOTS][:], out_offset=None, in_=table[:, :],
                            in_offset=bass.IndirectOffsetOnAxis(ap=index[g][:, k, i:i + 1], axis=0),
                        ).then_inc(gathered[t % SLOTS], 16)

            @block.vector
            def _(dve):
                dve.sem_inc(tile_free, SLOTS)
                dve.sem_inc(tps_free, 2)
                dve.sem_inc(sampled_free, 2)
                dve.sem_inc(acc_free, 2)
                dve.sem_inc(mixed, 1)
                dve.wait_ge(consts, 32)
                nc.vector.tensor_copy(index[0][:], tap_index[:, 0]).then_inc(index_ready, 1)

                def take(n, g):
                    c = Chain(dve, gchain, 6 * n + 2 * g + 2)
                    dve.wait_ge(acc_ready, 2 * n + g + 1)
                    b0 = TILES * n + GROUP * g
                    for o in range(CH):
                        last = nc.vector.tensor_scalar(
                            y[:, bass.ds(b0, GROUP), o], acc[g][o][:].rearrange("p (b q) -> p b q", q=P),
                            b_conv[:, o:o + 1], None, ALU.add)
                    c.step(last)
                    dve.sem_inc(acc_free, 1)
                    for o in range(CH):
                        last = nc.vector.bn_stats(conv_stats[:, o, bass.ds(2 * n + g, 1)], y[:, bass.ds(b0, GROUP), o])
                    c.step(last)

                with dve.Fori(0, BATCH) as n:
                    for t in range(TURN):
                        s, i = divmod(t, GROUP)
                        g, k = divmod(s, TAPS)
                        if t % (TURN // 2) == 0:
                            dve.wait_ge(mixed, TURN * n + t + 1)
                            nc.vector.tensor_copy(index[1 - g][:], tap_index[:, bass.ds(2 * n + g + 1, 1)]).then_inc(
                                index_ready, 1)
                            nc.vector.tensor_copy(weight[:], corner_w[:, bass.ds(2 * n + g, 1)]).then_inc(gchain, 1)
                            dve.wait_ge(gchain, 6 * n + g + 1)
                        if g == 1 and k == 2 and i == 0:
                            take(n, 0)
                        c = Chain(dve, chain, 3 * (TURN * n + t))
                        dve.wait_ge(gathered[t % SLOTS], 16 * (TURN // SLOTS * n + t // SLOTS + 1))
                        src, dst = got[t % SLOTS], mix[t % SLOTS]
                        c.step(nc.vector.tensor_scalar(dst[:], src[:, 0:C], weight[:, 0, k, i:i + 1], None, ALU.mult))
                        for q in range(1, CORNERS):
                            ins = nc.vector.scalar_tensor_tensor(dst[:], src[:, q * C:(q + 1) * C],
                                                                 weight[:, q, k, i:i + 1], dst[:], ALU.mult, ALU.add)
                            if q < CORNERS - 1:
                                c.step(ins)
                        ins.then_inc(mixed, 1)
                    take(n, 1)

            @block.scalar
            def _(act):
                with act.Fori(0, BATCH) as n:
                    for t in range(TURN):
                        s, i = divmod(t, GROUP)
                        if i == 0:
                            act.wait_ge(sampled_free, STEPS * n + s + 1)
                        act.wait_ge(transposed, TURN * n + t + 1)
                        nc.scalar.activation(sampled[s % 2][:, :, i * P:(i + 1) * P],
                                             tps[t % 2][:, 0:C].rearrange("p (o q) -> p o q", q=P),
                                             ACT.Copy).then_inc(evacuated, 1)
                        act.wait_ge(evacuated, TURN * n + t + 1)
                        act.sem_inc(tile_free, 1)
                        act.sem_inc(tps_free, 1)

            @block.tensor
            def _(pe):
                pe.wait_ge(consts, 32)

                def product(n, s):
                    g, k = divmod(s, TAPS)
                    if k == 0:
                        pe.wait_ge(acc_free, 2 * n + g + 1)
                    pe.wait_ge(evacuated, GROUP * (STEPS * n + s + 1))
                    for co in range(CH):
                        for ci in range(CH):
                            last = nc.tensor.matmul(acc[g][co][:], w_conv[:, k, ci, co * P:(co + 1) * P],
                                                    sampled[s % 2][:, ci], start=(k == 0 and ci == 0),
                                                    stop=(k == TAPS - 1 and ci == CH - 1))
                    if k == TAPS - 1:
                        last.then_inc(acc_ready, 1)
                        pe.wait_ge(acc_ready, 2 * n + g + 1)
                        pe.sem_inc(sampled_free, 1)
                    else:
                        last.then_inc(sampled_free, 1)

                with pe.Fori(0, BATCH) as n:
                    for s in range(STEPS):
                        for i in range(GROUP):
                            t = s * GROUP + i
                            pe.wait_ge(mixed, TURN * n + t + 2)
                            pe.wait_ge(tps_free, TURN * n + t + 1)
                            for o in range(CH):
                                last = nc.tensor.transpose(tps[t % 2][:, o * P:(o + 1) * P],
                                                           mix[t % SLOTS][:, o * P:(o + 1) * P], ident[:])
                            last.then_inc(transposed, 1)
                        if s:
                            product(n, s - 1)
                    product(n, STEPS - 1)


def batch_norm_gelu(nc, io, sem, sb, bank, x_img, ident, neg_half, y, conv_stats, token_stats, token_rstd):
    WIDE = GROUP * P
    with ExitStack() as mem:
        x_in = [sb(mem, f"c_x{u}", [CH, WIDE]) for u in range(2)]
        act_out = [sb(mem, f"c_act{u}", [CH, WIDE]) for u in range(2)]
        gamma = sb(mem, "c_gamma", [CH])
        beta = sb(mem, "c_beta", [CH])
        mv = sb(mem, "c_mv", [CH, 2])
        var = sb(mem, "c_var", [CH])
        rstd = sb(mem, "c_rstd", [CH])
        scale = sb(mem, "c_scale", [CH])
        shift = sb(mem, "c_shift", [CH])
        tst = sb(mem, "c_tst", [GROUP, 6])
        tmv = sb(mem, "c_tmv", [GROUP, 2])
        tvar = sb(mem, "c_tvar", [BLOCKS])
        tps = [bank(mem, f"c_tps{i}") for i in range(2 * GROUP)]

        consts = sem("c_consts")
        x_loaded = [sem(f"c_x_loaded{u}") for u in range(2)]
        x_free = sem("c_x_free")
        var_ready = sem("c_var_ready")
        rstd_ready = sem("c_rstd_ready")
        coef_ready = sem("c_coef_ready")
        act_ready = sem("c_act_ready")
        summed = sem("c_summed")
        transposed = sem("c_transposed")
        tps_free = sem("c_tps_free")
        chain = sem("c_chain")
        lchain = sem("c_lchain")
        token_var = sem("c_token_var")
        token_done = sem("c_token_done")

        with nc.Block() as block:
            @block.sync
            def _(sp):
                sp.dma_start(gamma[:], io["gamma"]).then_inc(consts, 16)
                sp.dma_start(beta[:], io["beta"]).then_inc(consts, 16)
                with sp.Fori(0, BATCH) as n:
                    for u in range(2):
                        sp.wait_ge(x_free, 2 * n + u + 1)
                        sp.dma_start(x_in[u][:], x_img[n, :, :, u * WIDE:(u + 1) * WIDE]).then_inc(x_loaded[u], 16)

            @block.gpsimd
            def _(pool):
                pool.wait_ge(var_ready, 1)
                nc.gpsimd.tensor_tensor(rstd[:], var[:], neg_half[:, 0:CH], ALU.pow).then_inc(rstd_ready, 1)
                with pool.Fori(0, BATCH) as n:
                    for u in range(2):
                        pool.wait_ge(act_ready, 2 * n + u + 1)
                        pool.wait_ge(x_loaded[u], 16 * (n + 1))
                        nc.gpsimd.tensor_tensor(x_in[u][:], x_in[u][:], act_out[u][:], ALU.add).then_inc(summed, 1)
                pool.wait_ge(token_var, 1)
                nc.gpsimd.tensor_tensor(token_rstd[:], tvar[:], neg_half[:], ALU.pow).then_inc(token_done, 1)

            @block.vector
            def _(dve):
                dve.sem_inc(x_free, 2)
                dve.sem_inc(summed, 2)
                dve.sem_inc(tps_free, 2 * GROUP)
                dve.wait_ge(consts, 32)
                c = Chain(dve, chain, 0)
                for o in range(CH):
                    last = nc.vector.bn_aggr(mv[:, o], conv_stats[:, o])
                c.step(last)
                nc.vector.tensor_scalar(var[:], mv[:, :, 1], 1e-5, None, ALU.add).then_inc(var_ready, 1)
                dve.wait_ge(rstd_ready, 1)
                c.step(nc.vector.tensor_tensor(scale[:], rstd[:], gamma[:], ALU.mult))
                c.step(nc.vector.tensor_tensor(shift[:], mv[:, :, 0], scale[:], ALU.mult))
                nc.vector.tensor_tensor(shift[:], beta[:], shift[:], ALU.subtract).then_inc(coef_ready, 1)
                with dve.Fori(0, BATCH) as n:
                    for u in range(2):
                        for i in range(GROUP):
                            count = TILES * n + u * GROUP + i
                            blk = bass.ds(count, 1)
                            c = Chain(dve, lchain, 3 * count)
                            dve.wait_ge(transposed, count + 1)
                            tile = tps[u * GROUP + i][:, 0:C]
                            nc.vector.tensor_copy(y[:, blk].rearrange("p n o q -> p (n o q)"), tile)
                            c.step(nc.vector.bn_stats(tst[:, i], tile), apart=True)
                            c.step(nc.vector.bn_aggr(tmv[:, i], tst[:, i]))
                            c.step(nc.vector.tensor_copy(token_stats[:, blk], tmv[:, i:i + 1]))
                            dve.sem_inc(tps_free, 1)
                        dve.sem_inc(x_free, 1)
                nc.vector.tensor_scalar(tvar[:], token_stats[:, :, 1], 1e-5, None, ALU.add).then_inc(token_var, 1)

            @block.scalar
            def _(act):
                act.wait_ge(coef_ready, 1)
                with act.Fori(0, BATCH) as n:
                    for u in range(2):
                        act.wait_ge(summed, 2 * n + u + 1)
                        act.nop(nofuse=True)
                        for o in range(CH):
                            last = nc.scalar.activation(
                                act_out[u][:, o].rearrange("p (b q) -> p b q", q=P),
                                y[:, bass.ds(TILES * n + u * GROUP, GROUP), o], ACT.Gelu,
                                bias=shift[:, o:o + 1], scale=scale[:, o:o + 1])
                        last.then_inc(act_ready, 1)

            @block.tensor
            def _(pe):
                with pe.Fori(0, BATCH) as n:
                    for u in range(2):
                        pe.wait_ge(summed, 2 * n + u + 3)
                        for i in range(GROUP):
                            count = TILES * n + u * GROUP + i
                            pe.wait_ge(tps_free, count + 1)
                            for o in range(CH):
                                last = nc.tensor.transpose(tps[u * GROUP + i][:, o * P:(o + 1) * P],
                                                           x_in[u][:, o, i * P:(i + 1) * P], ident[:])
                            last.then_inc(transposed, 1)


def block_attention(nc, io, sem, sb, bank, ident, neg_half, y, token_stats, token_rstd):
    SCALE = 1.0 / float(np.sqrt(np.float32(HD)))
    with ExitStack() as mem:
        w_qkv = sb(mem, "d_w_qkv", [CH, 3 * C])
        w_proj = sb(mem, "d_w_proj", [CH, C])
        rot_a = sb(mem, "d_rot_a", [C])
        rot_b = sb(mem, "d_rot_b", [C])
        w_ln = sb(mem, "d_w_ln", [2, C])
        ident_lo = sb(mem, "d_ident_lo", [P], BF16)
        causal = sb(mem, "d_causal", [P])
        causal_lo = sb(mem, "d_causal_lo", [CH, P], BF16)
        h = sb(mem, "d_h", [C])
        h_t = sb(mem, "d_h_t", [CH, P])
        v = [sb(mem, f"d_v{u}", [C]) for u in range(2)]
        square = sb(mem, "d_square", [2, C])
        ssq = sb(mem, "d_ssq", [2])
        ms = sb(mem, "d_ms", [2])
        rqk = sb(mem, "d_rqk", [2])
        part_a = sb(mem, "d_part_a", [2, C])
        part_b = sb(mem, "d_part_b", [2, C])
        qk = sb(mem, "d_qk", [2, C])
        q_t = [sb(mem, f"d_q_t{u}", [CH, P]) for u in range(2)]
        k_t = [sb(mem, f"d_k_t{u}", [CH, P]) for u in range(2)]
        top = sb(mem, "d_top", [HEADS])
        neg_top = sb(mem, "d_neg_top", [HEADS])
        prob = sb(mem, "d_prob", [HEADS, P])
        psum = sb(mem, "d_psum", [HEADS])
        prob_t = sb(mem, "d_prob_t", [HEADS, P])
        inv = sb(mem, "d_inv", [HEADS])
        mixed = sb(mem, "d_mixed", [C])
        mixed_t = sb(mem, "d_mixed_t", [CH, P])
        tst = sb(mem, "d_tst", [6])
        tmv = sb(mem, "d_tmv", [1, 2])
        tvar = sb(mem, "d_tvar", [BLOCKS])
        b_ht, b_q, b_k, b_v = [bank(mem, f"d_front{i}") for i in range(4)]
        b_s = [bank(mem, f"d_back{i}") for i in range(4)]

        consts = sem("d_consts")
        tables = sem("d_tables")
        h_ready = sem("d_h_ready")
        ht_psum = sem("d_ht_psum")
        ht_ready = sem("d_ht_ready")
        qkv_psum = sem("d_qkv_psum")
        squared = sem("d_squared")
        v_ready = sem("d_v_ready")
        ms_ready = sem("d_ms_ready")
        rqk_ready = sem("d_rqk_ready")
        parts = sem("d_parts")
        rotated = sem("d_rotated")
        qkt_psum = sem("d_qkt_psum")
        qkt_ready = sem("d_qkt_ready")
        s_psum = sem("d_s_psum")
        top_ready = sem("d_top_ready")
        prob_ready = sem("d_prob_ready")
        pt_psum = sem("d_pt_psum")
        pt_ready = sem("d_pt_ready")
        av_psum = sem("d_av_psum")
        mixed_ready = sem("d_mixed_ready")
        mt_psum = sem("d_mt_psum")
        mt_ready = sem("d_mt_ready")
        out_psum = sem("d_out_psum")
        out_done = sem("d_out_done")
        fchain = sem("d_fchain")
        bchain = sem("d_bchain")
        token_var = sem("d_token_var")
        token_done = sem("d_token_done")
        CONSTS = 6

        with nc.Block() as block:
            @block.sync
            def _(sp):
                sp.dma_start(w_qkv[:], io["w_qkv"]).then_inc(consts, 16)
                sp.dma_start(w_proj[:], io["w_proj"]).then_inc(consts, 16)
                sp.dma_start(rot_a[:], io["rot_cos"]).then_inc(consts, 16)
                sp.dma_start(rot_b[:], io["rot_sin"]).then_inc(consts, 16)
                sp.dma_start(w_ln[:], io["w_ln"]).then_inc(consts, 16)
                sp.dma_start(causal[:], io["causal"]).then_inc(consts, 16)

            @block.gpsimd
            def _(pool):
                pool.wait_ge(consts, 16 * CONSTS)
                nc.gpsimd.tensor_tensor(rot_a[:], rot_a[:], w_ln[:, 0], ALU.mult).then_inc(tables, 1)
                nc.gpsimd.tensor_tensor(rot_b[:], rot_b[:], w_ln[:, 1], ALU.mult).then_inc(tables, 1)
                nc.gpsimd.tensor_copy(ident_lo[:], ident[:]).then_inc(tables, 1)
                for c in range(CH):
                    nc.gpsimd.tensor_copy(causal_lo[:, c], causal[:]).then_inc(tables, 1)
                with pool.Fori(0, BLOCKS) as n:
                    pool.wait_ge(ms_ready, n + 1)
                    nc.gpsimd.tensor_tensor(rqk[:], ms[:], neg_half[:, 0:2], ALU.pow).then_inc(rqk_ready, 1)
                    for w in range(2):
                        pool.wait_ge(parts, 2 * n + w + 1)
                        nc.gpsimd.tensor_tensor(qk[:, w], part_a[:, w], part_b[:, w], ALU.add).then_inc(rotated, 1)
                pool.wait_ge(token_var, 1)
                nc.gpsimd.tensor_tensor(token_rstd[:], tvar[:], neg_half[:], ALU.pow).then_inc(token_done, 1)

            @block.vector
            def _(dve):
                dve.sem_inc(qkt_ready, 1)
                dve.sem_inc(s_psum, 2)
                dve.sem_inc(av_psum, 2)
                dve.sem_inc(out_done, 1)
                dve.wait_ge(tables, 3 + CH)

                def front_norm(n):
                    blk = bass.ds(n, 1)
                    dve.wait_ge(qkt_ready, n + 1)
                    nc.vector.tensor_scalar(h[:], y[:, blk].rearrange("p n o q -> p (n o q)"),
                                            token_stats[:, blk, 0], token_rstd[:, blk], ALU.subtract,
                                            ALU.mult).then_inc(h_ready, 1)

                def front_rotate(n):
                    dve.wait_ge(squared, n + 1)
                    nc.vector.tensor_scalar(ms[:], ssq[:], 1.0 / C, 1e-6, ALU.mult, ALU.add).then_inc(ms_ready, 1)
                    dve.wait_ge(rqk_ready, n + 1)
                    half = "p (h s d) -> p h s d"
                    for w, src in enumerate((b_q, b_k)):
                        nc.vector.scalar_tensor_tensor(part_a[:, w], src[:, 0:C], rqk[:, w:w + 1], rot_a[:],
                                                       ALU.mult, ALU.mult)
                        s4 = src[:, 0:C].rearrange(half, s=2, d=HD // 2)
                        o4 = part_b[:, w].rearrange(half, s=2, d=HD // 2)
                        b4 = rot_b[:].rearrange(half, s=2, d=HD // 2)
                        for side in range(2):
                            last = nc.vector.scalar_tensor_tensor(o4[:, :, side], s4[:, :, 1 - side], rqk[:, w:w + 1],
                                                                  b4[:, :, side], ALU.mult, ALU.mult)
                        last.then_inc(parts, 1)

                def back_top(n):
                    dve.wait_ge(s_psum, n + 3)
                    for r in range(4):
                        last = nc.vector.tensor_reduce(top[:, r::4], b_s[r][:, 0:C].rearrange("p (c k) -> p c k", k=P),
                                                       AX.X, ALU.max)
                    last.then_inc(bchain, 1)
                    dve.wait_ge(bchain, 3 * n + 1)
                    nc.vector.tensor_scalar(neg_top[:], top[:], -SCALE, None, ALU.mult).then_inc(top_ready, 1)

                def back_rest(n):
                    blk = bass.ds(n, 1)
                    dve.wait_ge(pt_psum, n + 1)
                    for q in (1, 2):
                        last = nc.vector.tensor_copy(prob_t[:, 4 * q:4 * q + 4],
                                                     b_s[q][:].rearrange("p (h k) -> p h k", k=P))
                    last.then_inc(pt_ready, 1)
                    nc.vector.reciprocal(inv[:], psum[:]).then_inc(bchain, 1)
                    dve.wait_ge(bchain, 3 * n + 2)
                    dve.wait_ge(av_psum, n + 3)
                    hd = "p (h d) -> p h d"
                    nc.vector.tensor_tensor(mixed[:].rearrange(hd, d=HD), b_s[3][:, 0:C].rearrange(hd, d=HD),
                                            inv[:].unsqueeze(2).to_broadcast([P, HEADS, HD]),
                                            ALU.mult).then_inc(mixed_ready, 1)
                    dve.wait_ge(out_psum, n + 1)
                    tok = y[:, blk].rearrange("p n o q -> p (n o q)")
                    nc.vector.tensor_tensor(tok, tok, b_s[1][:, 0:C], ALU.add).then_inc(bchain, 1)
                    dve.wait_ge(bchain, 3 * n + 3)
                    dve.sem_inc(out_done, 1)
                    c = Chain(dve, fchain, 3 * n)
                    c.step(nc.vector.bn_stats(tst[:], tok), apart=True)
                    c.step(nc.vector.bn_aggr(tmv[:, 0], tst[:]))
                    c.step(nc.vector.tensor_copy(token_stats[:, blk], tmv[:]))

                front_norm(0)
                front_rotate(0)
                with dve.Fori(0, BLOCKS - 1) as n:
                    front_norm(n + 1)
                    back_top(n)
                    front_rotate(n + 1)
                    back_rest(n)
                back_top(BLOCKS - 1)
                back_rest(BLOCKS - 1)
                nc.vector.tensor_scalar(tvar[:], token_stats[:, :, 1], 1e-5, None, ALU.add).then_inc(token_var, 1)

            @block.scalar
            def _(act):
                def three(out, src):
                    return nc.scalar.activation(out, src[:, 0:C].rearrange("p (o q) -> p o q", q=P), ACT.Copy)

                def front_h(n):
                    act.wait_ge(ht_psum, n + 1)
                    three(h_t[:], b_ht).then_inc(ht_ready, 1)

                def front_rest(n, u):
                    act.wait_ge(qkv_psum, n + 1)
                    for w, src in enumerate((b_q, b_k)):
                        last = nc.scalar.activation(square[:, w], src[:, 0:C], ACT.Square, accum_out=ssq[:, w:w + 1])
                    last.then_inc(squared, 1)
                    act.wait_ge(av_psum, n + 1)
                    nc.scalar.activation(v[u][:], b_v[:, 0:C], ACT.Copy).then_inc(v_ready, 1)
                    act.wait_ge(qkt_psum, n + 1)
                    act.wait_ge(s_psum, n + 1)
                    three(q_t[u][:], b_ht)
                    three(k_t[u][:], b_v).then_inc(qkt_ready, 1)

                def back_exp(n):
                    act.wait_ge(top_ready, n + 1)
                    for head in range(HEADS):
                        c, r = divmod(head, 4)
                        last = nc.scalar.activation(prob[:, head], b_s[r][:, c * P:(c + 1) * P], ACT.Exp,
                                                    bias=neg_top[:, head:head + 1], scale=SCALE,
                                                    accum_out=psum[:, head:head + 1])
                    last.then_inc(prob_ready, 1)

                def back_prob(n):
                    act.wait_ge(pt_psum, n + 1)
                    nc.scalar.activation(prob_t[:, 0:4], b_s[0][:].rearrange("p (h k) -> p h k", k=P),
                                         ACT.Copy).then_inc(pt_ready, 1)

                def back_mixed(n):
                    act.wait_ge(mt_psum, n + 1)
                    three(mixed_t[:], b_s[0]).then_inc(mt_ready, 1)

                def turn(n, u, more=True):
                    if more:
                        front_h(n + 1)
                    back_exp(n)
                    if more:
                        front_rest(n + 1, 1 - u)
                    back_prob(n)
                    back_mixed(n)

                front_h(0)
                front_rest(0, 0)
                with act.Fori(0, BLOCKS // 2 - 1) as j:
                    turn(2 * j, 0)
                    turn(2 * j + 1, 1)
                turn(BLOCKS - 2, 0)
                turn(BLOCKS - 1, 1, more=False)

            @block.tensor
            def _(pe):
                pe.wait_ge(tables, 3 + CH)

                def three(dst, src):
                    for o in range(CH):
                        last = nc.tensor.transpose(dst[:, o * P:(o + 1) * P], src[:, o * P:(o + 1) * P], ident[:])
                    return last

                def front_h(n):
                    pe.wait_ge(h_ready, n + 1)
                    pe.wait_ge(qkt_ready, n + 1)
                    three(b_ht, h).then_inc(ht_psum, 1)

                def front_qkv(n):
                    pe.wait_ge(ht_ready, n + 1)
                    for w, dst in enumerate((b_q, b_k, b_v)):
                        for o in range(CH):
                            last = nc.tensor.matmul(dst[:, 0:C], h_t[:, o], w_qkv[:, o, w * C:(w + 1) * C],
                                                    start=(o == 0), stop=(o == CH - 1))
                    last.then_inc(qkv_psum, 1)

                def front_turn(n):
                    pe.wait_ge(rotated, 2 * n + 1)
                    three(b_ht, qk[:, 0])
                    pe.wait_ge(v_ready, n + 1)
                    pe.wait_ge(rotated, 2 * n + 2)
                    three(b_v, qk[:, 1]).then_inc(qkt_psum, 1)

                def back_scores(n, u):
                    pe.wait_ge(qkt_ready, n + 2)
                    pe.wait_ge(out_done, n + 1)
                    for c in range(CH):
                        for r in range(4):
                            rows = slice(HD * r, HD * (r + 1))
                            nc.tensor.matmul(b_s[r][:, c * P:(c + 1) * P], q_t[u][rows, c], k_t[u][rows, c],
                                             start=(c == 0), stop=False, skip_group_check=True)
                    for r in range(4):
                        last = nc.tensor.matmul(b_s[r][:, 0:C], ident_lo[:], causal_lo[:].rearrange("p c k -> p (c k)"),
                                                start=False, stop=True, skip_group_check=True)
                    last.then_inc(s_psum, 1)

                def back_prob(n):
                    pe.wait_ge(prob_ready, n + 1)
                    for head in range(HEADS):
                        last = nc.tensor.transpose(b_s[head // 4][:, head % 4 * P:(head % 4 + 1) * P], prob[:, head],
                                                   ident[:])
                    last.then_inc(pt_psum, 1)

                def back_mix(n, u):
                    pe.wait_ge(pt_ready, 2 * n + 2)
                    for head in range(HEADS):
                        d = slice(head * HD, (head + 1) * HD)
                        last = nc.tensor.matmul(b_s[3][:, d], prob_t[:, head], v[u][:, d], start=True, stop=True)
                    last.then_inc(av_psum, 1)

                def back_project(n):
                    pe.wait_ge(mixed_ready, n + 1)
                    three(b_s[0], mixed).then_inc(mt_psum, 1)
                    pe.wait_ge(mt_ready, n + 1)
                    for o in range(CH):
                        last = nc.tensor.matmul(b_s[1][:, 0:C], mixed_t[:, o], w_proj[:, o], start=(o == 0),
                                                stop=(o == CH - 1))
                    last.then_inc(out_psum, 1)

                def turn(n, u, more=True):
                    if more:
                        front_h(n + 1)
                    back_scores(n, u)
                    if more:
                        front_qkv(n + 1)
                    back_prob(n)
                    if more:
                        front_turn(n + 1)
                    back_mix(n, u)
                    back_project(n)

                front_h(0)
                front_qkv(0)
                front_turn(0)
                with pe.Fori(0, BLOCKS // 2 - 1) as j:
                    turn(2 * j, 0)
                    turn(2 * j + 1, 1)
                turn(BLOCKS - 2, 0)
                turn(BLOCKS - 1, 1, more=False)


def head_attention(nc, io, sem, sb, bank, out_img, ident, neg_half, y, token_stats, token_rstd):
    WIDE = KEPT * HD
    SIDES = 2
    LOT = WIDE // SIDES
    SCALE = 1.0 / float(np.sqrt(np.float32(HD)))
    with ExitStack() as mem:
        w_t = sb(mem, "e_w_t", [3, CH, C])
        w_o = sb(mem, "e_w_o", [CH, C])
        w_r = sb(mem, "e_w_r", [CH, HEADS])
        b_r = sb(mem, "e_b_r", [HEADS])
        b_qk = sb(mem, "e_b_qk", [CH, 2])
        b_v = sb(mem, "e_b_v", [CH, P])
        rows = sb(mem, "e_rows", [3, C])
        slot_of = sb(mem, "e_slot_of", [WIDE])
        head_of = sb(mem, "e_head_of", [CH, HEADS])
        before = sb(mem, "e_before", [HEADS, HEADS])
        h = sb(mem, "e_h", [TILES, C])
        h_t = sb(mem, "e_h_t", [CH, PIX])
        mean_h = sb(mem, "e_mean_h", [CH])
        mean_b = sb(mem, "e_mean_b", [CH, P])
        logit = sb(mem, "e_logit", [HEADS])
        beats = sb(mem, "e_beats", [HEADS, HEADS])
        ties = sb(mem, "e_ties", [HEADS, HEADS])
        rank = sb(mem, "e_rank", [HEADS])
        keep = sb(mem, "e_keep", [HEADS])
        by_ch = sb(mem, "e_by_ch", [2, CH, HEADS])
        ch_rank = sb(mem, "e_ch_rank", [2, CH])
        select = sb(mem, "e_select", [2, CH, WIDE])
        w_kept = sb(mem, "e_w_kept", [3, CH, WIDE])
        wo_kept = sb(mem, "e_wo_kept", [SIDES, C])
        bqk_kept = sb(mem, "e_bqk_kept", [SIDES, 2])
        bv_kept = sb(mem, "e_bv_kept", [WIDE])
        k_t = sb(mem, "e_k_t", [SIDES, PIX])
        v = sb(mem, "e_v", [TILES, WIDE])
        q_t = sb(mem, "e_q_t", [SIDES, P])
        top = [sb(mem, f"e_top{u}", [1]) for u in range(2)]
        neg_top = [sb(mem, f"e_neg_top{u}", [1]) for u in range(2)]
        prob = [sb(mem, f"e_prob{u}", [PIX]) for u in range(2)]
        prob_t = [sb(mem, f"e_prob_t{u}", [PIX]) for u in range(2)]
        psum = sb(mem, "e_psum", [KEPT])
        inv = sb(mem, "e_inv", [KEPT])
        mixed = sb(mem, "e_mixed", [WIDE])
        mixed_t = sb(mem, "e_mixed_t", [SIDES, P])
        z = sb(mem, "e_z", [C])
        tst = sb(mem, "e_tst", [6])
        tmv = sb(mem, "e_tmv", [2])
        zvar = sb(mem, "e_zvar", [1])
        zrstd = sb(mem, "e_zrstd", [1])
        fin = sb(mem, "e_fin", [CH, P])
        b_s = [bank(mem, f"e_s{u}", width=PIX) for u in range(2)]
        b_pt = bank(mem, "e_pt", width=PIX)
        b_mix = bank(mem, "e_mix")
        b_x = bank(mem, "e_x")

        consts = sem("e_consts")
        h_ready = sem("e_h_ready")
        ht_psum = sem("e_ht_psum")
        ht_ready = sem("e_ht_ready")
        mean_ready = sem("e_mean_ready")
        logit_psum = sem("e_logit_psum")
        select_ready = sem("e_select_ready")
        kept_psum = sem("e_kept_psum")
        kept_ready = sem("e_kept_ready")
        kept2_psum = sem("e_kept2_psum")
        kept2_ready = sem("e_kept2_ready")
        kv_psum = sem("e_kv_psum")
        kv_ready = sem("e_kv_ready")
        q_psum = sem("e_q_psum")
        q_ready = sem("e_q_ready")
        s_psum = sem("e_s_psum")
        top_ready = sem("e_top_ready")
        prob_ready = sem("e_prob_ready")
        pt_psum = sem("e_pt_psum")
        pt_ready = sem("e_pt_ready")
        unit_mixed = sem("e_unit_mixed")
        inv_ready = sem("e_inv_ready")
        mixed_ready = sem("e_mixed_ready")
        mt_psum = sem("e_mt_psum")
        mt_ready = sem("e_mt_ready")
        out_psum = sem("e_out_psum")
        zvar_ready = sem("e_zvar_ready")
        zrstd_ready = sem("e_zrstd_ready")
        z_ready = sem("e_z_ready")
        fin_psum = sem("e_fin_psum")
        fin_ready = sem("e_fin_ready")
        written = sem("e_written")
        pchain = sem("e_pchain")
        uchain = sem("e_uchain")
        tchain = sem("e_tchain")
        image_done = sem("e_image_done")
        CONSTS = 10
        LAST = TILES - 1

        with nc.Block() as block:
            @block.sync
            def _(sp):
                for dst, name in ((w_t, "w_t"), (w_o, "w_o"), (w_r, "w_r"), (b_r, "b_r"), (b_qk, "b_qk"), (b_v, "b_v"),
                                  (rows, "rows"), (slot_of, "slot_of"), (head_of, "head_of"), (before, "before")):
                    sp.dma_start(dst[:], io[name]).then_inc(consts, 16)
                with sp.Fori(0, BATCH) as n:
                    with sp.Fori(0, TILES) as t:
                        sp.wait_ge(fin_ready, TILES * n + t + 2)
                        sp.dma_start(out_img[n, :, :, bass.ds(t * P, P)], fin[:]).then_inc(written, 16)
                sp.wait_ge(written, 16 * BLOCKS + 16)

            @block.gpsimd
            def _(pool):
                with pool.Fori(0, BLOCKS) as t:
                    pool.wait_ge(zvar_ready, t + 1)
                    nc.gpsimd.tensor_tensor(zrstd[:], zvar[:], neg_half[:, 0:1], ALU.pow).then_inc(zrstd_ready, 1)

            @block.vector
            def _(dve):
                dve.sem_inc(ht_ready, 2)
                dve.sem_inc(prob_ready, 2)
                dve.sem_inc(pt_ready, 2)
                dve.sem_inc(unit_mixed, 2)
                dve.sem_inc(mixed_ready, 1)
                dve.sem_inc(fin_ready, 1)
                dve.sem_inc(written, 16)
                dve.wait_ge(consts, 16 * CONSTS)

                def begin(n):
                    c = Chain(dve, pchain, 17 * n)
                    for t in range(TILES):
                        blk = bass.ds(TILES * n + t, 1)
                        nc.vector.tensor_scalar(h[:, t], y[:, blk].rearrange("p n o q -> p (n o q)"),
                                                token_stats[:, blk, 0], token_rstd[:, blk], ALU.subtract,
                                                ALU.mult).then_inc(h_ready, 1)
                    dve.wait_ge(ht_ready, TILES * (n + 1) + 2)
                    c.step(nc.vector.reduce_sum(mean_h[:], h_t[:], AX.X))
                    nc.vector.tensor_scalar(mean_b[:], mean_h[:].unsqueeze(2).to_broadcast([P, CH, P]), 1.0 / PIX, None,
                                            ALU.mult).then_inc(mean_ready, 1)
                    dve.wait_ge(logit_psum, n + 1)
                    c.step(nc.vector.tensor_tensor(logit[:], b_x[:, 0:HEADS], b_r[:], ALU.add))
                    square = [P, HEADS, HEADS]
                    mine = logit[:].unsqueeze(2).to_broadcast(square)
                    other = logit[:].unsqueeze(1).to_broadcast(square)
                    nc.vector.tensor_tensor(beats[:], other, mine, ALU.is_gt)
                    c.step(nc.vector.tensor_tensor(ties[:], other, mine, ALU.is_equal))
                    c.step(nc.vector.tensor_tensor(ties[:], ties[:], before[:], ALU.mult))
                    c.step(nc.vector.tensor_tensor(beats[:], beats[:], ties[:], ALU.add))
                    c.step(nc.vector.reduce_sum(rank[:], beats[:], AX.X))
                    c.step(nc.vector.tensor_scalar(keep[:], rank[:], KEPT - 0.5, None, ALU.is_lt))
                    c.step(nc.vector.tensor_tensor(keep[:], keep[:], logit[:], ALU.add))
                    c.step(nc.vector.tensor_tensor(keep[:], keep[:], logit[:], ALU.subtract))
                    wide = [P, CH, HEADS]
                    nc.vector.tensor_tensor(by_ch[:, 0], head_of[:], rank[:].unsqueeze(1).to_broadcast(wide), ALU.mult)
                    c.step(nc.vector.tensor_tensor(by_ch[:, 1], head_of[:], keep[:].unsqueeze(1).to_broadcast(wide),
                                                   ALU.mult))
                    c.step(nc.vector.reduce_sum(ch_rank[:], by_ch[:], AX.X))
                    for o in range(CH):
                        nc.vector.tensor_scalar(select[:, 0, o], slot_of[:], ch_rank[:, 0, o:o + 1], None, ALU.is_equal)
                        last = nc.vector.tensor_scalar(select[:, 1, o], slot_of[:], ch_rank[:, 0, o:o + 1],
                                                       ch_rank[:, 1, o:o + 1], ALU.is_equal, ALU.mult)
                    last.then_inc(select_ready, 1)
                    dve.wait_ge(kept_psum, n + 1)
                    for w, src in enumerate((b_s[0], b_s[1], b_pt)):
                        last = nc.vector.tensor_copy(
                            w_kept[:, w, 0:2], src[:, 0:512].rearrange("p (o k) -> p o k", k=256)[:, :, 0:WIDE])
                        last = nc.vector.tensor_copy(w_kept[:, w, 2], src[:, 512:512 + WIDE])
                    nc.vector.tensor_copy(bv_kept[:], b_x[:, 0:WIDE])
                    last = nc.vector.tensor_copy(bqk_kept[0:LOT],
                                                 b_mix[0:LOT, 0:2 * SIDES].rearrange("p (g w) -> p g w", w=2))
                    c.step(last)
                    dve.sem_inc(kept_ready, 1)
                    dve.wait_ge(kept2_psum, n + 1)
                    c.step(nc.vector.tensor_copy(wo_kept[0:LOT],
                                                 b_s[0][0:LOT].rearrange("p (g c) -> p g c", g=SIDES)[:, :, 0:C]))
                    dve.sem_inc(kept2_ready, 1)
                    for g in range(SIDES):
                        dve.wait_ge(kv_psum, 4 * n + g + 1)
                        c.step(nc.vector.tensor_scalar(k_t[0:LOT, g], b_s[g][0:LOT], bqk_kept[0:LOT, g, 1:2], None,
                                                       ALU.add))
                        dve.sem_inc(kv_ready, 1)
                    for f in range(2):
                        dve.wait_ge(kv_psum, 4 * n + f + 3)
                        c.step(nc.vector.tensor_tensor(
                            v[:, 4 * f:4 * f + 4], b_pt[:].rearrange("p (t k) -> p t k", k=256)[:, :, 0:WIDE],
                            bv_kept[:].unsqueeze(1).to_broadcast([P, 4, WIDE]), ALU.add))
                        dve.sem_inc(kv_ready, 1)
                    assert c.n == 17

                def tail_mixed(tt):
                    dve.wait_ge(unit_mixed, KEPT * (tt + 1) + 2)
                    dve.wait_ge(inv_ready, tt + 1)
                    hd = "p (h d) -> p h d"
                    nc.vector.tensor_tensor(mixed[:].rearrange(hd, d=HD), b_mix[:, 0:WIDE].rearrange(hd, d=HD),
                                            inv[:].unsqueeze(2).to_broadcast([P, KEPT, HD]),
                                            ALU.mult).then_inc(mixed_ready, 1)

                def tail_norm(tt, t):
                    c = Chain(dve, tchain, 8 * tt)
                    dve.wait_ge(out_psum, tt + 1)
                    c.step(nc.vector.tensor_tensor(z[:], b_x[:, 0:C], rows[:, 0], ALU.add))
                    c.step(nc.vector.tensor_tensor(z[:], z[:], h[:, bass.ds(t, 1)].rearrange("p t c -> p (t c)"), ALU.add))
                    c.step(nc.vector.bn_stats(tst[:], z[:]), apart=True)
                    c.step(nc.vector.bn_aggr(tmv[:], tst[:]))
                    nc.vector.tensor_scalar(zvar[:], tmv[:, 1:2], 1e-12, None, ALU.add).then_inc(zvar_ready, 1)
                    dve.wait_ge(zrstd_ready, tt + 1)
                    c.step(nc.vector.tensor_scalar(z[:], z[:], tmv[:, 0:1], zrstd[:], ALU.subtract, ALU.mult))
                    c.step(nc.vector.tensor_tensor(z[:], z[:], rows[:, 1], ALU.mult))
                    c.step(nc.vector.tensor_tensor(z[:], z[:], rows[:, 2], ALU.add))
                    c.step(nc.vector.tensor_tensor(z[:], z[:], y[:, bass.ds(tt, 1)].rearrange("p n o q -> p (n o q)"),
                                                   ALU.add))
                    dve.sem_inc(z_ready, 1)
                    assert c.n == 8

                def unit(m, s, first):
                    dve.wait_ge(s_psum, m + 1)
                    nc.vector.tensor_reduce(top[s % 2][:], b_s[s % 2][:], AX.X, ALU.max).then_inc(uchain, 1)
                    dve.wait_ge(uchain, m + 1)
                    if s == 0 and not first:
                        dve.wait_ge(prob_ready, m + 2)
                        nc.vector.reciprocal(inv[:], psum[:]).then_inc(inv_ready, 1)
                    nc.vector.tensor_scalar(neg_top[s % 2][:], top[s % 2][:], -SCALE, None, ALU.mult).then_inc(top_ready, 1)

                def copy_t(m, s):
                    dve.wait_ge(pt_psum, m)
                    dve.wait_ge(unit_mixed, m)
                    nc.vector.tensor_copy(prob_t[(s - 1) % 2][:, 0:512], b_pt[:, 0:512]).then_inc(pt_ready, 1)

                def tile(n, t, first=False):
                    tt = TILES * n + t
                    for s in range(KEPT):
                        m = KEPT * tt + s
                        unit(m, s, first)
                        if s or not first:
                            copy_t(m, s)
                        if s == 1 and not first:
                            tail_mixed(tt - 1)
                        if s == 3 and not first:
                            tail_norm(tt - 1, t - 1)

                with dve.Fori(0, BATCH) as n:
                    begin(n)
                    tile(n, 0, first=True)
                    with dve.Fori(1, TILES) as t:
                        tile(n, t)
                    m = KEPT * TILES * (n + 1)
                    copy_t(m, 0)
                    dve.wait_ge(prob_ready, m + 2)
                    nc.vector.reciprocal(inv[:], psum[:]).then_inc(inv_ready, 1)
                    tail_mixed(TILES * n + LAST)
                    tail_norm(TILES * n + LAST, LAST)

            @block.scalar
            def _(act):
                def begin(n):
                    for t in range(TILES):
                        act.wait_ge(ht_psum, TILES * n + t + 1)
                        nc.scalar.activation(h_t[:, :, t * P:(t + 1) * P],
                                             b_s[t % 2][:, 0:C].rearrange("p (o q) -> p o q", q=P),
                                             ACT.Copy).then_inc(ht_ready, 1)
                    q_copy(n, 0)

                def q_copy(n, t):
                    act.wait_ge(q_psum, TILES * n + t + 1)
                    for g in range(SIDES):
                        last = nc.scalar.activation(q_t[0:LOT, g], b_x[0:LOT, g * P:(g + 1) * P], ACT.Identity,
                                                    bias=bqk_kept[0:LOT, g, 0:1])
                    last.then_inc(q_ready, 1)

                def copy_t(m, s):
                    act.wait_ge(pt_psum, m)
                    act.wait_ge(unit_mixed, m)
                    nc.scalar.activation(prob_t[(s - 1) % 2][:, 512:PIX], b_pt[:, 512:PIX], ACT.Copy).then_inc(pt_ready, 1)

                def tail(tt):
                    act.wait_ge(mt_psum, tt + 1)
                    nc.scalar.activation(mixed_t[0:LOT], b_x[0:LOT, 0:2 * P].rearrange("p (g q) -> p g q", q=P),
                                         ACT.Copy).then_inc(mt_ready, 1)

                def finish(tt):
                    act.wait_ge(fin_psum, tt + 1)
                    act.wait_ge(written, 16 * tt + 16)
                    nc.scalar.activation(fin[:], b_x[:, 0:C].rearrange("p (o q) -> p o q", q=P),
                                         ACT.Copy).then_inc(fin_ready, 1)

                def tile(n, t, first=False, last=False):
                    tt = TILES * n + t
                    for s in range(KEPT):
                        m = KEPT * tt + s
                        act.wait_ge(top_ready, m + 1)
                        if s >= 2 or not first:
                            act.wait_ge(pt_psum, m - 1)
                        nc.scalar.activation(prob[s % 2][:], b_s[s % 2][:], ACT.Exp, bias=neg_top[s % 2][:], scale=SCALE,
                                             accum_out=psum[:, s:s + 1]).then_inc(prob_ready, 1)
                        if s or not first:
                            copy_t(m, s)
                        if s == 2 and not first:
                            tail(tt - 1)
                        if s == 4 and not first:
                            finish(tt - 1)
                    if not last:
                        q_copy(n, t + 1)

                with act.Fori(0, BATCH) as n:
                    begin(n)
                    tile(n, 0, first=True)
                    with act.Fori(1, LAST) as t:
                        tile(n, t)
                    tile(n, LAST, last=True)
                    copy_t(KEPT * TILES * (n + 1), 0)
                    tail(TILES * n + LAST)
                    finish(TILES * n + LAST)

            @block.tensor
            def _(pe):
                pe.wait_ge(consts, 16 * CONSTS)

                def begin(n):
                    for t in range(TILES):
                        pe.wait_ge(h_ready, TILES * n + t + 1)
                        pe.wait_ge(ht_ready, TILES * n + t + 1)
                        for o in range(CH):
                            last = nc.tensor.transpose(b_s[t % 2][:, o * P:(o + 1) * P], h[:, t, o * P:(o + 1) * P],
                                                       ident[:])
                        last.then_inc(ht_psum, 1)
                    pe.wait_ge(mean_ready, n + 1)
                    for o in range(CH):
                        last = nc.tensor.matmul(b_x[:, 0:HEADS], mean_b[:, o], w_r[:, o], start=(o == 0),
                                                stop=(o == CH - 1))
                    last.then_inc(logit_psum, 1)
                    pe.wait_ge(select_ready, n + 1)
                    for w, dst in enumerate((b_s[0], b_s[1], b_pt)):
                        for ci in range(CH):
                            for co in range(CH):
                                nc.tensor.matmul(dst[:, 256 * ci:256 * ci + WIDE], w_t[:, w, co, ci * P:(ci + 1) * P],
                                                 select[:, 1, co], start=(co == 0), stop=(co == CH - 1))
                    for co in range(CH):
                        nc.tensor.matmul(b_x[:, 0:WIDE], b_v[:, co], select[:, 1, co], start=(co == 0), stop=(co == CH - 1))
                    for g in range(SIDES):
                        for co in range(CH):
                            last = nc.tensor.matmul(b_mix[0:LOT, 2 * g:2 * g + 2], select[:, 1, co, g * LOT:(g + 1) * LOT],
                                                    b_qk[:, co], start=(co == 0), stop=(co == CH - 1))
                    last.then_inc(kept_psum, 1)
                    pe.wait_ge(kept_ready, n + 1)
                    for g in range(SIDES):
                        for co in range(CH):
                            last = nc.tensor.matmul(b_s[0][0:LOT, 512 * g:512 * g + C],
                                                    select[:, 0, co, g * LOT:(g + 1) * LOT], w_o[:, co],
                                                    start=(co == 0), stop=(co == CH - 1))
                    last.then_inc(kept2_psum, 1)
                    pe.wait_ge(kept2_ready, n + 1)
                    for g in range(SIDES):
                        for f in range(2):
                            for ci in range(CH):
                                last = nc.tensor.matmul(b_s[g][0:LOT, 512 * f:512 * (f + 1)],
                                                        w_kept[:, 1, ci, g * LOT:(g + 1) * LOT],
                                                        h_t[:, ci, 512 * f:512 * (f + 1)], start=(ci == 0),
                                                        stop=(ci == CH - 1))
                        last.then_inc(kv_psum, 1)
                    for f in range(2):
                        if f:
                            pe.wait_ge(kv_ready, 4 * n + 3)
                        for t in range(4):
                            for ci in range(CH):
                                last = nc.tensor.matmul(b_pt[:, 256 * t:256 * t + WIDE],
                                                        h_t[:, ci, (4 * f + t) * P:(4 * f + t + 1) * P],
                                                        w_kept[:, 2, ci], start=(ci == 0), stop=(ci == CH - 1))
                        last.then_inc(kv_psum, 1)
                    query(n, 0)
                    pe.wait_ge(kv_ready, 4 * n + 4)

                def query(n, t):
                    for g in range(SIDES):
                        for ci in range(CH):
                            last = nc.tensor.matmul(b_x[0:LOT, g * P:(g + 1) * P], w_kept[:, 0, ci, g * LOT:(g + 1) * LOT],
                                                    h_t[:, ci, bass.ds(t * P, P)], start=(ci == 0), stop=(ci == CH - 1))
                    last.then_inc(q_psum, 1)

                def scores(m, s):
                    pe.wait_ge(prob_ready, m + 1)
                    g, r = divmod(s, KEPT // SIDES)
                    part = slice(HD * r, HD * (r + 1))
                    for f in range(2):
                        last = nc.tensor.matmul(b_s[s % 2][:, 512 * f:512 * (f + 1)], q_t[part, g],
                                                k_t[part, g, 512 * f:512 * (f + 1)], start=True, stop=True)
                    last.then_inc(s_psum, 1)

                def transposes(m, s):
                    pe.wait_ge(prob_ready, m + 3)
                    pe.wait_ge(pt_ready, 2 * m + 2)
                    for t in range(TILES):
                        last = nc.tensor.transpose(b_pt[:, t * P:(t + 1) * P], prob[s % 2][:, t * P:(t + 1) * P], ident[:])
                    last.then_inc(pt_psum, 1)

                def mix(m, s, tt):
                    pe.wait_ge(pt_ready, 2 * m + 4)
                    if s == 0:
                        pe.wait_ge(mixed_ready, tt + 1)
                    for t in range(TILES):
                        last = nc.tensor.matmul(b_mix[:, s * HD:(s + 1) * HD], prob_t[s % 2][:, t * P:(t + 1) * P],
                                                v[:, t, s * HD:(s + 1) * HD], start=(t == 0), stop=(t == LAST))
                    last.then_inc(unit_mixed, 1)

                def project(tt):
                    pe.wait_ge(mixed_ready, tt + 2)
                    for g in range(SIDES):
                        last = nc.tensor.transpose(b_x[0:LOT, g * P:(g + 1) * P], mixed[:, g * LOT:(g + 1) * LOT], ident[:])
                    last.then_inc(mt_psum, 1)

                def project2(tt):
                    pe.wait_ge(mt_ready, tt + 1)
                    for g in range(SIDES):
                        last = nc.tensor.matmul(b_x[:, 0:C], mixed_t[0:LOT, g], wo_kept[0:LOT, g], start=(g == 0),
                                                stop=(g == SIDES - 1))
                    last.then_inc(out_psum, 1)

                def finish(tt):
                    pe.wait_ge(z_ready, tt + 1)
                    for o in range(CH):
                        last = nc.tensor.transpose(b_x[:, o * P:(o + 1) * P], z[:, o * P:(o + 1) * P], ident[:])
                    last.then_inc(fin_psum, 1)

                def tile(n, t, first=False, last=False):
                    tt = TILES * n + t
                    for s in range(KEPT):
                        m = KEPT * tt + s
                        if s == 0:
                            pe.wait_ge(q_ready, tt + 1)
                        if s == KEPT - 1 and not last:
                            if not first:
                                pe.wait_ge(fin_ready, tt + 1)
                            query(n, t + 1)
                        scores(m, s)
                        if s >= 1 or not first:
                            transposes(m - 1, (s - 1) % 2)
                        if s >= 2 or not first:
                            mix(m - 2, (s - 2) % KEPT, tt if s >= 2 else tt - 1)
                        if not first:
                            if s == 2:
                                project(tt - 1)
                                project2(tt - 1)
                            if s == 4:
                                finish(tt - 1)

                with pe.Fori(0, BATCH) as n:
                    begin(n)
                    tile(n, 0, first=True)
                    with pe.Fori(1, LAST) as t:
                        tile(n, t)
                    tile(n, LAST, last=True)
                    tt = TILES * n + LAST
                    m = KEPT * (tt + 1)
                    transposes(m - 1, 1)
                    mix(m - 2, KEPT - 2, tt)
                    mix(m - 1, KEPT - 1, tt)
                    project(tt)
                    project2(tt)
                    finish(tt)
                    pe.wait_ge(fin_ready, tt + 2)


def kernel(**inputs):
    import numpy as _np
    import concourse.bacc as _bacc
    from concourse import mybir as _mybir
    from concourse.bass_utils import run_bass_kernel_spmd as _run

    a = {k: _np.asarray(v) for k, v in inputs.items()}
    ow = a["L0_conv_off_w"].reshape(2 * TAPS, C, TAPS)
    ob = a["L0_conv_off_b"]
    off_w = _np.concatenate([ow[0::2], ow[1::2], a["L0_conv_mask_w"].reshape(TAPS, C, TAPS)])
    off_b = _np.concatenate([ob[0::2], ob[1::2], a["L0_conv_mask_b"]])

    def chunks(w):
        return w.reshape(CH, P, *w.shape[1:]).swapaxes(0, 1)

    arrays = dict(shape_constants())
    arrays["x"] = a["x"]
    arrays["w_off"] = chunks(off_w.transpose(1, 2, 0))
    arrays["b_off"] = _np.tile(off_b, (P, 1))
    arrays["w_conv"] = chunks(a["L0_conv_proj_w"].reshape(C, C, TAPS).transpose(1, 2, 0)).swapaxes(1, 2)
    arrays["gamma"] = chunks(a["L0_conv_gamma"])
    arrays["beta"] = chunks(a["L0_conv_beta"])
    half = _np.concatenate([_np.arange(0, HD, 2), _np.arange(1, HD, 2)])
    order = (_np.arange(HEADS)[:, None] * HD + half).reshape(-1)
    partner = _np.roll(order.reshape(HEADS, HD), HD // 2, axis=1).reshape(-1)
    w = a["L1_attn_w_qkv"]
    arrays["w_qkv"] = chunks(_np.concatenate([w[:, order], w[:, C + order], w[:, 2 * C:]], axis=1))
    arrays["w_proj"] = chunks(a["L1_attn_w_proj"])
    ln = a["L1_attn_w_ln"]
    arrays["w_ln"] = _np.tile(_np.stack([ln[order], ln[partner]]), (P, 1, 1))
    arrays["w_t"] = _np.stack([chunks(a["L1_ffn_W" + k].T) for k in "qkv"], axis=1)
    arrays["w_o"] = chunks(a["L1_ffn_Wo"])
    arrays["w_r"] = chunks(a["L1_ffn_Wr"])
    arrays["b_r"] = _np.tile(a["L1_ffn_br"], (P, 1))
    arrays["b_qk"] = chunks(_np.stack([a["L1_ffn_bq"], a["L1_ffn_bk"]], axis=1))
    arrays["b_v"] = chunks(_np.tile(a["L1_ffn_bv"][:, None], (1, P)))
    arrays["rows"] = _np.tile(_np.stack([a["L1_ffn_bo"], a["L1_ffn_ln_g"], a["L1_ffn_ln_b"]]), (P, 1, 1))
    arrays["b_conv"] = chunks(a["L0_conv_proj_b"])

    nc = _bacc.Bacc("TRN2", target_bir_lowering=False, num_devices=1)
    io, fed = {}, {}
    for name, v in arrays.items():
        v = _np.ascontiguousarray(v)
        fed["in_" + name] = v
        io[name] = nc.dram_tensor("in_" + name, v.shape, _mybir.dt.from_np(v.dtype), kind="ExternalInput").ap()
    io["out"] = nc.dram_tensor("out_0", (BATCH, C, SIDE, SIDE), F32, kind="ExternalOutput").ap()
    build(nc, io)
    r = _run(nc, [fed], core_ids=[0])
    return r.results[0]["out_0"]
```

```python
from contextlib import ExitStack

import numpy as np
import concourse.bass as bass
from concourse import mybir
from concourse.alu_op_type import AluOpType as ALU

ACT = mybir.ActivationFunctionType
AX = mybir.AxisListType
F32 = mybir.dt.float32
BF16 = mybir.dt.bfloat16
U32 = mybir.dt.uint32

P = 128
BATCH, C, SIDE = 8, 384, 32
PIX = SIDE * SIDE
CH = C // P
TAPS = 9
TILES = PIX // P
BLOCKS = BATCH * TILES
GROUP = 4
GROUPS = BLOCKS // GROUP
PADW = SIDE + 2
MAX_OFF = float(SIDE // 4)
GN_GROUPS = 32
CORNERS = 4
CORNER_SHIFT = [0, 1, SIDE, SIDE + 1]
LEAD = SIDE + 1
IMG_ROWS = PIX + LEAD
HEADS, HD = 12, 32
KEPT = 6
ROUND = float(3 * 2 ** 22)

MASKED = -1e30


def shape_constants():
    f = np.float32
    ch = np.arange(C)
    same = (ch[:, None] // (C // GN_GROUPS) == ch[None, :] // (C // GN_GROUPS)).astype(f) / f(C // GN_GROUPS)
    p = np.arange(P)
    tile = np.arange(TILES)
    tap = np.arange(TAPS)
    row = (tile[None, :, None] * (P // SIDE) + p[:, None, None] // SIDE) - 1 + tap[None, None, :] // 3
    col = (p[:, None, None] % SIDE) - 1 + tap[None, None, :] % 3 + 0 * tile[None, :, None]
    pos = np.concatenate([row, col], axis=2).astype(f)
    rows0 = np.tile((np.arange(BATCH) * IMG_ROWS + LEAD).astype(f), (P, 1))
    freq = np.power(f(10000.0), (f(-2.0) * np.arange(0, HD, 2, dtype=f) - f(1.0)) / f(HD), dtype=f)
    ts = p.astype(f)[:, None] * freq[None, :]
    even = np.arange(0, HD, 2)
    channel = np.concatenate([even, even + 1]) % (HD // 2)
    cos, sin = np.cos(ts)[:, channel], np.sin(ts)[:, channel]
    sin = np.where(np.arange(HD) < HD // 2, -sin, sin)
    dim = np.arange(KEPT * HD)
    slot_of = np.where(dim[None, :] % HD == p[:, None] % HD, dim[None, :] // HD, -1)
    head_of = (np.arange(CH)[None, :, None] * P + p[:, None, None]) // HD == np.arange(HEADS)[None, None, :]
    before = np.arange(HEADS)[None, :] < np.arange(HEADS)[:, None]
    return {
        "slot_of": slot_of.astype(f),
        "head_of": head_of.astype(f),
        "before": np.tile(before.astype(f), (P, 1, 1)),
        "rot_cos": np.tile(cos, (1, HEADS)).astype(f),
        "rot_sin": np.tile(sin, (1, HEADS)).astype(f),
        "causal": np.where(p[None, :] <= p[:, None], f(0), f(MASKED)).astype(f),
        "ident": np.eye(P, dtype=f),
        "same_group": np.ascontiguousarray(same.reshape(CH, P, C).transpose(1, 0, 2)),
        "tap_pos": pos,
        "table_row0": rows0,
    }


class Chain:

    def __init__(self, eng, sem, base):
        self.eng, self.sem, self.base, self.n = eng, sem, base, 0

    def step(self, ins, apart=False):
        self.n += 1
        ins.then_inc(self.sem, 1)
        self.eng.wait_ge(self.sem, self.base + self.n)
        if apart:
            self.eng.nop(nofuse=True)


def build(nc, io):
    x_img = io["x"].rearrange("b (o p) h w -> b p o (h w)", p=P)
    out_img = io["out"].rearrange("b (o p) h w -> b p o (h w)", p=P)
    table = nc.dram_tensor("corner_table", (BATCH * IMG_ROWS, CORNERS * C), F32, kind="Internal").ap()

    tokens = nc.dram_tensor("tokens", (BLOCKS, P, C), F32, kind="Internal").ap()

    with ExitStack() as whole:
        def sem(name):
            return whole.enter_context(nc.semaphore(name))

        def sb(stack, name, shape, dt=F32):
            return stack.enter_context(nc.sbuf_tensor(name, [P] + shape, dt))

        def bank(stack, name, dt=F32, width=512):
            return stack.enter_context(nc.psum_tensor(name, [P, width], dt))

        ident = sb(whole, "ident", [P])
        neg_half = sb(whole, "neg_half", [BLOCKS])
        token_stats = sb(whole, "token_stats", [BLOCKS, 2])
        token_rstd = sb(whole, "token_rstd", [BLOCKS])
        with ExitStack() as layers:
            y = sb(layers, "y", [BLOCKS, CH, P])
            conv_stats = sb(layers, "conv_stats", [CH, GROUPS, 6])
            with ExitStack() as conv:
                tap_index = sb(conv, "tap_index", [GROUPS + 1, TAPS, GROUP], U32)
                corner_w = sb(conv, "corner_w", [GROUPS, CORNERS, TAPS, GROUP])
                offsets_and_table(nc, io, sem, sb, bank, x_img, table, ident, tap_index, corner_w, neg_half, y)
                deform_conv(nc, io, sem, sb, bank, table, ident, tap_index, corner_w, y, conv_stats)
            batch_norm_gelu(nc, io, sem, sb, bank, x_img, ident, neg_half, y, conv_stats, token_stats, token_rstd)
            block_attention(nc, io, sem, sb, bank, ident, neg_half, y, tokens, token_stats, token_rstd)
        head_attention(nc, io, sem, sb, bank, out_img, tokens, ident, neg_half, token_stats, token_rstd)


def offsets_and_table(nc, io, sem, sb, bank, x_img, table, ident, tap_index, corner_w, neg_half, y):
    NOUT = 3 * TAPS
    with ExitStack() as mem:
        x_in = [sb(mem, f"a_x{u}", [CH, PIX]) for u in range(2)]
        size = 3 * CH * PADW * SIDE
        y_flat = y[:].rearrange("p n o q -> p (n o q)")
        xpad = [y_flat[:, u * size:(u + 1) * size].rearrange("p (d o h w) -> p d o h w", d=3, o=CH, h=PADW)
                for u in range(2)]
        tok = [sb(mem, f"a_tok{u}", [TILES, C]) for u in range(2)]
        w_off = sb(mem, "a_w_off", [CH, TAPS, NOUT])
        b_off = sb(mem, "a_b_off", [NOUT])
        same_group = sb(mem, "a_same_group", [CH, C])
        tap_pos = sb(mem, "a_tap_pos", [TILES, 2 * TAPS])
        table_row0 = sb(mem, "a_table_row0", [BATCH])
        bst = sb(mem, "a_bst", [CH, 2, 6])
        mv = sb(mem, "a_mv", [CH, 2])
        stat = sb(mem, "a_stat", [CH, 2])
        gstat = sb(mem, "a_gstat", [CH, 2])
        gvar = sb(mem, "a_gvar", [CH])
        rstd = sb(mem, "a_rstd", [CH])
        shift = sb(mem, "a_shift", [CH])
        norm_scale = [sb(mem, f"a_ns{u}", [CH]) for u in range(2)]
        norm_shift = [sb(mem, f"a_nb{u}", [CH]) for u in range(2)]
        raw = sb(mem, "a_raw", [TILES, NOUT])
        pos = sb(mem, "a_pos", [TILES, 2 * TAPS])
        base = sb(mem, "a_base", [TILES, 2 * TAPS])
        dist = sb(mem, "a_dist", [2, TILES, 2 * TAPS])
        wgt = sb(mem, "a_wgt", [2, TILES, 2 * TAPS])
        mask = sb(mem, "a_mask", [TILES, TAPS])
        wy = sb(mem, "a_wy", [2, TILES, TAPS])
        row = sb(mem, "a_row", [TILES, TAPS])
        gps = bank(mem, "a_gps")
        offps = [bank(mem, f"a_offps{u}") for u in range(2)]
        tps = [bank(mem, f"a_tps{u}") for u in range(2)]

        consts = sem("a_consts")
        cleared = sem("a_cleared")
        x_loaded = [sem(f"a_x_loaded{u}") for u in range(2)]
        x_free = sem("a_x_free")
        xpad_free = sem("a_xpad_free")
        table_written = [sem(f"a_table_written{u}") for u in range(2)]
        stats_ready = sem("a_stats_ready")
        group_ready = sem("a_group_ready")
        var_ready = sem("a_var_ready")
        rstd_ready = sem("a_rstd_ready")
        norm_ready = sem("a_norm_ready")
        xn_ready = sem("a_xn_ready")
        tp_ready = sem("a_tp_ready")
        tp_free = sem("a_tp_free")
        off_ready = sem("a_off_ready")
        raw_ready = sem("a_raw_ready")
        mask_ready = sem("a_mask_ready")
        fchain = sem("a_fchain")
        bchain = sem("a_bchain")
        gaps_filled = sem("a_gaps_filled")
        NCONST = 6
        GAPS = 2 * (CORNERS - 1)
        img_rows = table.rearrange("(b r) c -> r b c", r=IMG_ROWS)

        with nc.Block() as block:
            @block.sync
            def _(sp):
                def load_x(j, u):
                    sp.wait_ge(x_free, 2 * j + u + 1)
                    sp.dma_start(x_in[u][:], x_img[2 * j + u]).then_inc(x_loaded[u], 16)

                sp.dma_start(ident[:], io["ident"]).then_inc(consts, 16)
                sp.dma_start(w_off[:], io["w_off"]).then_inc(consts, 16)
                sp.dma_start(b_off[:], io["b_off"]).then_inc(consts, 16)
                sp.dma_start(same_group[:], io["same_group"]).then_inc(consts, 16)
                sp.dma_start(tap_pos[:], io["tap_pos"]).then_inc(consts, 16)
                sp.dma_start(table_row0[:], io["table_row0"]).then_inc(consts, 16)
                for u in range(2):
                    load_x(0, u)
                sp.wait_ge(cleared, 5)
                for s, d in enumerate(CORNER_SHIFT):
                    for first, many in ((0, LEAD - d), (LEAD - d + PIX, d)):
                        if many:
                            sp.dma_start(img_rows[first:first + many, :, s * C:(s + 1) * C],
                                         tok[0][0:many]).then_inc(gaps_filled, 16)

                def turn(j, u, more):
                    if more:
                        load_x(j + 1, u)
                    sp.wait_ge(tp_free, TILES * (2 * j + u + 1) + 2)
                    for s, d in enumerate(CORNER_SHIFT):
                        first = (2 * j + u) * IMG_ROWS + LEAD - d
                        dst = table[bass.ds(first, PIX), s * C:(s + 1) * C].rearrange("(t p) c -> p t c", p=P)
                        sp.dma_start(dst, tok[u][:]).then_inc(table_written[u], 16)

                with sp.Fori(0, BATCH // 2 - 1) as j:
                    for u in range(2):
                        turn(j, u, True)
                for u in range(2):
                    turn(BATCH // 2 - 1, u, False)
                for u in range(2):
                    sp.wait_ge(table_written[u], 16 * CORNERS * BATCH // 2 + 1)

            @block.gpsimd
            def _(pool):
                nc.gpsimd.memset(tok[0][:], 0.0).then_inc(cleared, 1)
                nc.gpsimd.memset(neg_half[:], -0.5).then_inc(cleared, 1)
                nc.gpsimd.memset(tap_index[:, GROUPS], 0).then_inc(cleared, 1)
                for u in range(2):
                    nc.gpsimd.memset(xpad[u], 0.0).then_inc(cleared, 1)
                pool.wait_ge(cleared, 5)
                with pool.Fori(0, BATCH) as n:
                    pool.wait_ge(var_ready, n + 1)
                    nc.gpsimd.tensor_tensor(rstd[:], gvar[:], neg_half[:, 0:CH], ALU.pow).then_inc(rstd_ready, 1)

            @block.vector
            def _(dve):
                for u in range(2):
                    dve.sem_inc(table_written[u], 1)
                dve.sem_inc(x_free, 2)
                dve.sem_inc(xpad_free, 2)
                dve.sem_inc(tp_free, 2)
                dve.wait_ge(consts, 16 * NCONST)
                dve.wait_ge(gaps_filled, 16 * GAPS)

                def front(j, u):
                    n = 2 * j + u
                    c = Chain(dve, fchain, 7 * n)
                    dve.wait_ge(x_loaded[u], 16 * (j + 1))
                    for o in range(CH):
                        for h in range(2):
                            last = nc.vector.bn_stats(bst[:, o, h], x_in[u][:, o, h * 512:(h + 1) * 512])
                    c.step(last, apart=True)
                    for o in range(CH):
                        last = nc.vector.bn_aggr(mv[:, o], bst[:, o])
                    c.step(last)
                    nc.vector.tensor_copy(stat[:, :, 0], mv[:, :, 0])
                    c.step(nc.vector.tensor_tensor(stat[:, :, 1], mv[:, :, 0], mv[:, :, 0], ALU.mult))
                    nc.vector.tensor_tensor(stat[:, :, 1], stat[:, :, 1], mv[:, :, 1], ALU.add).then_inc(stats_ready, 1)
                    dve.wait_ge(group_ready, n + 1)
                    c.step(nc.vector.tensor_copy(gstat[:], gps[:, 0:2 * CH].rearrange("p (o s) -> p o s", s=2)))
                    c.step(nc.vector.tensor_tensor(gvar[:], gstat[:, :, 0], gstat[:, :, 0], ALU.mult))
                    c.step(nc.vector.tensor_tensor(gvar[:], gstat[:, :, 1], gvar[:], ALU.subtract))
                    nc.vector.tensor_scalar(gvar[:], gvar[:], 1e-5, None, ALU.add).then_inc(var_ready, 1)
                    dve.wait_ge(rstd_ready, n + 1)
                    dve.wait_ge(x_free, n + 1)
                    c.step(nc.vector.tensor_copy(norm_scale[u][:], rstd[:]))
                    nc.vector.scalar_tensor_tensor(norm_shift[u][:], gstat[:, :, 0], -1.0, rstd[:], ALU.mult,
                                                   ALU.mult).then_inc(norm_ready, 1)
                    assert c.n == 7

                def back(j, u):
                    n = 2 * j + u
                    c = Chain(dve, bchain, 14 * n)
                    dve.wait_ge(table_written[u], 16 * CORNERS * j + 1)
                    for i in range(TILES):
                        dve.wait_ge(tp_ready, TILES * n + i + 1)
                        nc.vector.tensor_copy(tok[u][:, i], tps[i % 2][:, 0:C]).then_inc(tp_free, 1)
                    dve.wait_ge(off_ready, n + 1)
                    c.step(nc.vector.tensor_tensor(
                        raw[:], offps[u][:, 0:TILES * NOUT].rearrange("p (t k) -> p t k", k=NOUT),
                        b_off[:].unsqueeze(1).to_broadcast([P, TILES, NOUT]), ALU.add))
                    dve.sem_inc(raw_ready, 1)
                    c.step(nc.vector.tensor_scalar(pos[:], raw[:, :, 0:2 * TAPS], -MAX_OFF, MAX_OFF, ALU.max, ALU.min))
                    c.step(nc.vector.tensor_tensor(pos[:], pos[:], tap_pos[:], ALU.add))
                    c.step(nc.vector.tensor_scalar(base[:], pos[:], 0.25, SIDE - 1.25, ALU.max, ALU.min))
                    c.step(nc.vector.tensor_scalar(base[:], base[:], -0.5, ROUND, ALU.add, ALU.add))
                    c.step(nc.vector.tensor_scalar(base[:], base[:], -ROUND, None, ALU.add))
                    c.step(nc.vector.tensor_tensor(dist[:, 0], pos[:], base[:], ALU.subtract))
                    c.step(nc.vector.tensor_scalar(dist[:, 1], dist[:, 0], -1.0, None, ALU.add))
                    c.step(nc.vector.tensor_scalar(wgt[:], dist[:], -1.0, 1.0, ALU.mult, ALU.add))
                    flat = "p s t k -> p (s t k)"
                    c.step(nc.vector.scalar_tensor_tensor(wgt[:].rearrange(flat), dist[:].rearrange(flat), 1.0,
                                                          wgt[:].rearrange(flat), ALU.add, ALU.min))
                    c.step(nc.vector.tensor_scalar(wgt[:], wgt[:], 0.0, None, ALU.max))
                    c.step(nc.vector.scalar_tensor_tensor(row[:], base[:, :, 0:TAPS], float(SIDE), base[:, :, TAPS:],
                                                          ALU.mult, ALU.add))
                    halves = "p (g i) k -> p g i k"
                    for g in range(2):
                        nc.vector.tensor_scalar(
                            tap_index[:, bass.ds(2 * n + g, 1)].rearrange("p g k i -> p (g i) k"),
                            row[:, g * GROUP:(g + 1) * GROUP], table_row0[:, bass.ds(n, 1)], None, ALU.add)
                    dve.wait_ge(mask_ready, n + 1)
                    for a in range(2):
                        last = nc.vector.scalar_tensor_tensor(wy[:, a], wgt[:, a, :, 0:TAPS], 2.0, mask[:],
                                                              ALU.mult, ALU.mult)
                    c.step(last)
                    for g in range(2):
                        for a in range(2):
                            for b in range(2):
                                rows = slice(g * GROUP, (g + 1) * GROUP)
                                last = nc.vector.tensor_tensor(
                                    corner_w[:, bass.ds(2 * n + g, 1), 2 * a + b].rearrange("p g k i -> p (g i) k"),
                                    wy[:, a, rows], wgt[:, b, rows, TAPS:], ALU.mult)
                    c.step(last)
                    assert c.n == 14

                front(0, 0)
                with dve.Fori(0, BATCH // 2 - 1) as j:
                    front(j, 1)
                    back(j, 0)
                    front(j + 1, 0)
                    back(j, 1)
                front(BATCH // 2 - 1, 1)
                back(BATCH // 2 - 1, 0)
                back(BATCH // 2 - 1, 1)

            @block.scalar
            def _(act):
                act.wait_ge(cleared, 5)

                def front(j, u):
                    n = 2 * j + u
                    act.wait_ge(norm_ready, n + 1)
                    act.wait_ge(xpad_free, n + 1)
                    for o in range(CH):
                        img = x_in[u][:, o].rearrange("p (h w) -> p h w", w=SIDE)
                        for dx in range(3):
                            to, fro, width = max(0, 1 - dx), max(0, dx - 1), SIDE - abs(dx - 1)
                            last = nc.scalar.activation(
                                xpad[u][:, dx, o, 1:1 + SIDE, to:to + width], img[:, :, fro:fro + width], ACT.Identity,
                                bias=norm_shift[u][:, o:o + 1], scale=norm_scale[u][:, o:o + 1])
                    last.then_inc(xn_ready, 1)
                    act.wait_ge(xn_ready, n + 1)
                    act.sem_inc(x_free, 1)

                def back(n):
                    act.wait_ge(raw_ready, n + 1)
                    nc.scalar.activation(mask[:], raw[:, :, 2 * TAPS:], ACT.Sigmoid).then_inc(mask_ready, 1)

                front(0, 0)
                with act.Fori(0, BATCH // 2 - 1) as j:
                    front(j, 1)
                    back(2 * j)
                    front(j + 1, 0)
                    back(2 * j + 1)
                front(BATCH // 2 - 1, 1)
                back(BATCH - 2)
                back(BATCH - 1)

            @block.tensor
            def _(pe):
                pe.wait_ge(consts, 16 * NCONST)

                def front(n):
                    pe.wait_ge(stats_ready, n + 1)
                    for co in range(CH):
                        for ci in range(CH):
                            last = nc.tensor.matmul(gps[:, 2 * co:2 * co + 2], same_group[:, ci, co * P:(co + 1) * P],
                                                    stat[:, ci, :], start=(ci == 0), stop=(ci == CH - 1))
                    last.then_inc(group_ready, 1)

                def back(j, u):
                    n = 2 * j + u
                    pe.wait_ge(xn_ready, n + 1)
                    flat = xpad[u].rearrange("p d o h w -> p d o (h w)")
                    for i in range(TILES):
                        pe.wait_ge(tp_free, TILES * n + i + 1)
                        for o in range(CH):
                            last = nc.tensor.transpose(tps[i % 2][:, o * P:(o + 1) * P],
                                                       flat[:, 1, o, SIDE + P * i:SIDE + P * (i + 1)],
                                                       ident[:])
                        last.then_inc(tp_ready, 1)
                        for t in range(TAPS):
                            for o in range(CH):
                                at = P * i + SIDE * (t // 3)
                                last = nc.tensor.matmul(offps[u][:, i * NOUT:(i + 1) * NOUT],
                                                        flat[:, t % 3, o, at:at + P],
                                                        w_off[:, o, t, :], start=(t == 0 and o == 0),
                                                        stop=(t == TAPS - 1 and o == CH - 1))
                    last.then_inc(off_ready, 1)
                    pe.wait_ge(off_ready, n + 1)
                    pe.sem_inc(xpad_free, 1)

                front(0)
                with pe.Fori(0, BATCH // 2 - 1) as j:
                    front(2 * j + 1)
                    back(j, 0)
                    front(2 * j + 2)
                    back(j, 1)
                front(BATCH - 1)
                back(BATCH // 2 - 1, 0)
                back(BATCH // 2 - 1, 1)


def deform_conv(nc, io, sem, sb, bank, table, ident, tap_index, corner_w, y, conv_stats):
    STEPS = 2 * TAPS
    TURN = STEPS * GROUP
    SLOTS = 4
    with ExitStack() as mem:
        w_conv = sb(mem, "b_w", [TAPS, CH, C])
        b_conv = sb(mem, "b_b", [CH])
        got = [sb(mem, f"b_got{s}", [CORNERS * C]) for s in range(SLOTS)]
        mix = [sb(mem, f"b_mix{s}", [C]) for s in range(SLOTS)]
        sampled = [sb(mem, f"b_sampled{u}", [CH, GROUP * P]) for u in range(2)]
        index = [sb(mem, f"b_index{g}", [TAPS, GROUP], U32) for g in range(2)]
        weight = sb(mem, "b_weight", [CORNERS, TAPS, GROUP])
        tps = [bank(mem, f"b_tps{u}") for u in range(2)]
        acc = [[bank(mem, f"b_acc{g}{o}") for o in range(CH)] for g in range(2)]

        consts = sem("b_consts")
        index_ready = sem("b_index_ready")
        gathered = [sem(f"b_gathered{s}") for s in range(SLOTS)]
        mixed = sem("b_mixed")
        transposed = sem("b_transposed")
        evacuated = sem("b_evacuated")
        tile_free = sem("b_tile_free")
        tps_free = sem("b_tps_free")
        sampled_free = sem("b_sampled_free")
        acc_ready = sem("b_acc_ready")
        acc_free = sem("b_acc_free")
        chain = sem("b_chain")
        gchain = sem("b_gchain")

        with nc.Block() as block:
            @block.sync
            def _(sp):
                sp.dma_start(w_conv[:], io["w_conv"]).then_inc(consts, 16)
                sp.dma_start(b_conv[:], io["b_conv"]).then_inc(consts, 16)

            @block.gpsimd
            def _(pool):
                with pool.Fori(0, BATCH) as n:
                    for t in range(TURN):
                        s, i = divmod(t, GROUP)
                        g, k = divmod(s, TAPS)
                        if t % (TURN // 2) == 0:
                            pool.wait_ge(index_ready, 2 * n + g + 1)
                        pool.wait_ge(tile_free, TURN * n + t + 1)
                        pool.nop(nofuse=True)
                        nc.gpsimd.indirect_dma_start(
                            out=got[t % SLOTS][:], out_offset=None, in_=table[:, :],
                            in_offset=bass.IndirectOffsetOnAxis(ap=index[g][:, k, i:i + 1], axis=0),
                        ).then_inc(gathered[t % SLOTS], 16)

            @block.vector
            def _(dve):
                dve.sem_inc(tile_free, SLOTS)
                dve.sem_inc(tps_free, 2)
                dve.sem_inc(sampled_free, 2)
                dve.sem_inc(acc_free, 2)
                dve.sem_inc(mixed, 1)
                dve.wait_ge(consts, 32)
                nc.vector.tensor_copy(index[0][:], tap_index[:, 0]).then_inc(index_ready, 1)

                def take(n, g):
                    c = Chain(dve, gchain, 6 * n + 2 * g + 2)
                    dve.wait_ge(acc_ready, 2 * n + g + 1)
                    b0 = TILES * n + GROUP * g
                    for o in range(CH):
                        last = nc.vector.tensor_scalar(
                            y[:, bass.ds(b0, GROUP), o], acc[g][o][:].rearrange("p (b q) -> p b q", q=P),
                            b_conv[:, o:o + 1], None, ALU.add)
                    c.step(last)
                    dve.sem_inc(acc_free, 1)
                    for o in range(CH):
                        last = nc.vector.bn_stats(conv_stats[:, o, bass.ds(2 * n + g, 1)], y[:, bass.ds(b0, GROUP), o])
                    c.step(last)

                with dve.Fori(0, BATCH) as n:
                    for t in range(TURN):
                        s, i = divmod(t, GROUP)
                        g, k = divmod(s, TAPS)
                        if t % (TURN // 2) == 0:
                            dve.wait_ge(mixed, TURN * n + t + 1)
                            nc.vector.tensor_copy(index[1 - g][:], tap_index[:, bass.ds(2 * n + g + 1, 1)]).then_inc(
                                index_ready, 1)
                            nc.vector.tensor_copy(weight[:], corner_w[:, bass.ds(2 * n + g, 1)]).then_inc(gchain, 1)
                            dve.wait_ge(gchain, 6 * n + g + 1)
                        if g == 1 and k == 2 and i == 0:
                            take(n, 0)
                        c = Chain(dve, chain, 3 * (TURN * n + t))
                        dve.wait_ge(gathered[t % SLOTS], 16 * (TURN // SLOTS * n + t // SLOTS + 1))
                        src, dst = got[t % SLOTS], mix[t % SLOTS]
                        c.step(nc.vector.tensor_scalar(dst[:], src[:, 0:C], weight[:, 0, k, i:i + 1], None, ALU.mult))
                        for q in range(1, CORNERS):
                            ins = nc.vector.scalar_tensor_tensor(dst[:], src[:, q * C:(q + 1) * C],
                                                                 weight[:, q, k, i:i + 1], dst[:], ALU.mult, ALU.add)
                            if q < CORNERS - 1:
                                c.step(ins)
                        ins.then_inc(mixed, 1)
                    take(n, 1)

            @block.scalar
            def _(act):
                with act.Fori(0, BATCH) as n:
                    for t in range(TURN):
                        s, i = divmod(t, GROUP)
                        if i == 0:
                            act.wait_ge(sampled_free, STEPS * n + s + 1)
                        act.wait_ge(transposed, TURN * n + t + 1)
                        nc.scalar.activation(sampled[s % 2][:, :, i * P:(i + 1) * P],
                                             tps[t % 2][:, 0:C].rearrange("p (o q) -> p o q", q=P),
                                             ACT.Copy).then_inc(evacuated, 1)
                        act.wait_ge(evacuated, TURN * n + t + 1)
                        act.sem_inc(tile_free, 1)
                        act.sem_inc(tps_free, 1)

            @block.tensor
            def _(pe):
                pe.wait_ge(consts, 32)

                def product(n, s):
                    g, k = divmod(s, TAPS)
                    if k == 0:
                        pe.wait_ge(acc_free, 2 * n + g + 1)
                    pe.wait_ge(evacuated, GROUP * (STEPS * n + s + 1))
                    for co in range(CH):
                        for ci in range(CH):
                            last = nc.tensor.matmul(acc[g][co][:], w_conv[:, k, ci, co * P:(co + 1) * P],
                                                    sampled[s % 2][:, ci], start=(k == 0 and ci == 0),
                                                    stop=(k == TAPS - 1 and ci == CH - 1))
                    if k == TAPS - 1:
                        last.then_inc(acc_ready, 1)
                        pe.wait_ge(acc_ready, 2 * n + g + 1)
                        pe.sem_inc(sampled_free, 1)
                    else:
                        last.then_inc(sampled_free, 1)

                with pe.Fori(0, BATCH) as n:
                    for s in range(STEPS):
                        for i in range(GROUP):
                            t = s * GROUP + i
                            pe.wait_ge(mixed, TURN * n + t + 2)
                            pe.wait_ge(tps_free, TURN * n + t + 1)
                            for o in range(CH):
                                last = nc.tensor.transpose(tps[t % 2][:, o * P:(o + 1) * P],
                                                           mix[t % SLOTS][:, o * P:(o + 1) * P], ident[:])
                            last.then_inc(transposed, 1)
                        if s:
                            product(n, s - 1)
                    product(n, STEPS - 1)


def batch_norm_gelu(nc, io, sem, sb, bank, x_img, ident, neg_half, y, conv_stats, token_stats, token_rstd):
    WIDE = GROUP * P
    with ExitStack() as mem:
        x_in = [sb(mem, f"c_x{u}", [CH, WIDE]) for u in range(2)]
        act_out = [sb(mem, f"c_act{u}", [CH, WIDE]) for u in range(2)]
        gamma = sb(mem, "c_gamma", [CH])
        beta = sb(mem, "c_beta", [CH])
        mv = sb(mem, "c_mv", [CH, 2])
        var = sb(mem, "c_var", [CH])
        rstd = sb(mem, "c_rstd", [CH])
        scale = sb(mem, "c_scale", [CH])
        shift = sb(mem, "c_shift", [CH])
        tst = sb(mem, "c_tst", [GROUP, 6])
        tmv = sb(mem, "c_tmv", [GROUP, 2])
        tvar = sb(mem, "c_tvar", [BLOCKS])
        tps = [bank(mem, f"c_tps{i}") for i in range(2 * GROUP)]

        consts = sem("c_consts")
        x_loaded = [sem(f"c_x_loaded{u}") for u in range(2)]
        x_free = sem("c_x_free")
        var_ready = sem("c_var_ready")
        rstd_ready = sem("c_rstd_ready")
        coef_ready = sem("c_coef_ready")
        act_ready = sem("c_act_ready")
        summed = sem("c_summed")
        transposed = sem("c_transposed")
        tps_free = sem("c_tps_free")
        chain = sem("c_chain")
        lchain = sem("c_lchain")
        token_var = sem("c_token_var")
        token_done = sem("c_token_done")

        with nc.Block() as block:
            @block.sync
            def _(sp):
                sp.dma_start(gamma[:], io["gamma"]).then_inc(consts, 16)
                sp.dma_start(beta[:], io["beta"]).then_inc(consts, 16)
                with sp.Fori(0, BATCH) as n:
                    for u in range(2):
                        sp.wait_ge(x_free, 2 * n + u + 1)
                        sp.dma_start(x_in[u][:], x_img[n, :, :, u * WIDE:(u + 1) * WIDE]).then_inc(x_loaded[u], 16)

            @block.gpsimd
            def _(pool):
                pool.wait_ge(var_ready, 1)
                nc.gpsimd.tensor_tensor(rstd[:], var[:], neg_half[:, 0:CH], ALU.pow).then_inc(rstd_ready, 1)
                with pool.Fori(0, BATCH) as n:
                    for u in range(2):
                        pool.wait_ge(act_ready, 2 * n + u + 1)
                        pool.wait_ge(x_loaded[u], 16 * (n + 1))
                        nc.gpsimd.tensor_tensor(x_in[u][:], x_in[u][:], act_out[u][:], ALU.add).then_inc(summed, 1)
                pool.wait_ge(token_var, 1)
                nc.gpsimd.tensor_tensor(token_rstd[:], tvar[:], neg_half[:], ALU.pow).then_inc(token_done, 1)

            @block.vector
            def _(dve):
                dve.sem_inc(x_free, 2)
                dve.sem_inc(summed, 2)
                dve.sem_inc(tps_free, 2 * GROUP)
                dve.wait_ge(consts, 32)
                c = Chain(dve, chain, 0)
                for o in range(CH):
                    last = nc.vector.bn_aggr(mv[:, o], conv_stats[:, o])
                c.step(last)
                nc.vector.tensor_scalar(var[:], mv[:, :, 1], 1e-5, None, ALU.add).then_inc(var_ready, 1)
                dve.wait_ge(rstd_ready, 1)
                c.step(nc.vector.tensor_tensor(scale[:], rstd[:], gamma[:], ALU.mult))
                c.step(nc.vector.tensor_tensor(shift[:], mv[:, :, 0], scale[:], ALU.mult))
                nc.vector.tensor_tensor(shift[:], beta[:], shift[:], ALU.subtract).then_inc(coef_ready, 1)
                with dve.Fori(0, BATCH) as n:
                    for u in range(2):
                        for i in range(GROUP):
                            count = TILES * n + u * GROUP + i
                            blk = bass.ds(count, 1)
                            c = Chain(dve, lchain, 3 * count)
                            dve.wait_ge(transposed, count + 1)
                            tile = tps[u * GROUP + i][:, 0:C]
                            nc.vector.tensor_copy(y[:, blk].rearrange("p n o q -> p (n o q)"), tile)
                            c.step(nc.vector.bn_stats(tst[:, i], tile), apart=True)
                            c.step(nc.vector.bn_aggr(tmv[:, i], tst[:, i]))
                            c.step(nc.vector.tensor_copy(token_stats[:, blk], tmv[:, i:i + 1]))
                            dve.sem_inc(tps_free, 1)
                        dve.sem_inc(x_free, 1)
                nc.vector.tensor_scalar(tvar[:], token_stats[:, :, 1], 1e-5, None, ALU.add).then_inc(token_var, 1)

            @block.scalar
            def _(act):
                act.wait_ge(coef_ready, 1)
                with act.Fori(0, BATCH) as n:
                    for u in range(2):
                        act.wait_ge(summed, 2 * n + u + 1)
                        act.nop(nofuse=True)
                        for o in range(CH):
                            last = nc.scalar.activation(
                                act_out[u][:, o].rearrange("p (b q) -> p b q", q=P),
                                y[:, bass.ds(TILES * n + u * GROUP, GROUP), o], ACT.Gelu,
                                bias=shift[:, o:o + 1], scale=scale[:, o:o + 1])
                        last.then_inc(act_ready, 1)

            @block.tensor
            def _(pe):
                with pe.Fori(0, BATCH) as n:
                    for u in range(2):
                        pe.wait_ge(summed, 2 * n + u + 3)
                        for i in range(GROUP):
                            count = TILES * n + u * GROUP + i
                            pe.wait_ge(tps_free, count + 1)
                            for o in range(CH):
                                last = nc.tensor.transpose(tps[u * GROUP + i][:, o * P:(o + 1) * P],
                                                           x_in[u][:, o, i * P:(i + 1) * P], ident[:])
                            last.then_inc(transposed, 1)


def block_attention(nc, io, sem, sb, bank, ident, neg_half, y, tokens, token_stats, token_rstd):
    SCALE = 1.0 / float(np.sqrt(np.float32(HD)))
    with ExitStack() as mem:
        w_qkv = sb(mem, "d_w_qkv", [CH, 3 * C])
        w_proj = sb(mem, "d_w_proj", [CH, C])
        rot_a = sb(mem, "d_rot_a", [C])
        rot_b = sb(mem, "d_rot_b", [C])
        w_ln = sb(mem, "d_w_ln", [2, C])
        ident_lo = sb(mem, "d_ident_lo", [P], BF16)
        causal = sb(mem, "d_causal", [P])
        causal_lo = sb(mem, "d_causal_lo", [CH, P], BF16)
        h = sb(mem, "d_h", [C])
        h_t = sb(mem, "d_h_t", [CH, P])
        v = [sb(mem, f"d_v{u}", [C]) for u in range(2)]
        square = sb(mem, "d_square", [2, C])
        ssq = sb(mem, "d_ssq", [2])
        ms = sb(mem, "d_ms", [2])
        rqk = sb(mem, "d_rqk", [2])
        part_a = sb(mem, "d_part_a", [2, C])
        part_b = sb(mem, "d_part_b", [2, C])
        qk = sb(mem, "d_qk", [2, C])
        q_t = [sb(mem, f"d_q_t{u}", [CH, P]) for u in range(2)]
        k_t = [sb(mem, f"d_k_t{u}", [CH, P]) for u in range(2)]
        top = sb(mem, "d_top", [HEADS])
        neg_top = sb(mem, "d_neg_top", [HEADS])
        prob = sb(mem, "d_prob", [HEADS, P])
        psum = sb(mem, "d_psum", [HEADS])
        prob_t = sb(mem, "d_prob_t", [HEADS, P])
        inv = sb(mem, "d_inv", [HEADS])
        mixed = sb(mem, "d_mixed", [C])
        mixed_t = sb(mem, "d_mixed_t", [CH, P])
        tst = sb(mem, "d_tst", [6])
        tmv = sb(mem, "d_tmv", [1, 2])
        tvar = sb(mem, "d_tvar", [BLOCKS])
        b_ht, b_q, b_k, b_v = [bank(mem, f"d_front{i}") for i in range(4)]
        b_s = [bank(mem, f"d_back{i}") for i in range(4)]

        consts = sem("d_consts")
        tables = sem("d_tables")
        h_ready = sem("d_h_ready")
        ht_psum = sem("d_ht_psum")
        ht_ready = sem("d_ht_ready")
        qkv_psum = sem("d_qkv_psum")
        squared = sem("d_squared")
        v_ready = sem("d_v_ready")
        ms_ready = sem("d_ms_ready")
        rqk_ready = sem("d_rqk_ready")
        parts = sem("d_parts")
        rotated = sem("d_rotated")
        qkt_psum = sem("d_qkt_psum")
        qkt_ready = sem("d_qkt_ready")
        s_psum = sem("d_s_psum")
        top_ready = sem("d_top_ready")
        prob_ready = sem("d_prob_ready")
        pt_psum = sem("d_pt_psum")
        pt_ready = sem("d_pt_ready")
        av_psum = sem("d_av_psum")
        mixed_ready = sem("d_mixed_ready")
        mt_psum = sem("d_mt_psum")
        mt_ready = sem("d_mt_ready")
        out_psum = sem("d_out_psum")
        out_done = sem("d_out_done")
        stored = sem("d_stored")
        fchain = sem("d_fchain")
        bchain = sem("d_bchain")
        token_var = sem("d_token_var")
        token_done = sem("d_token_done")
        CONSTS = 6

        with nc.Block() as block:
            @block.sync
            def _(sp):
                sp.dma_start(w_qkv[:], io["w_qkv"]).then_inc(consts, 16)
                sp.dma_start(w_proj[:], io["w_proj"]).then_inc(consts, 16)
                sp.dma_start(rot_a[:], io["rot_cos"]).then_inc(consts, 16)
                sp.dma_start(rot_b[:], io["rot_sin"]).then_inc(consts, 16)
                sp.dma_start(w_ln[:], io["w_ln"]).then_inc(consts, 16)
                sp.dma_start(causal[:], io["causal"]).then_inc(consts, 16)
                with sp.Fori(0, BLOCKS) as n:
                    sp.wait_ge(out_done, n + 2)
                    sp.dma_start(tokens[n], y[:, bass.ds(n, 1)].rearrange("p n o q -> p (n o q)")).then_inc(stored, 16)
                sp.wait_ge(stored, 16 * BLOCKS)

            @block.gpsimd
            def _(pool):
                pool.wait_ge(consts, 16 * CONSTS)
                nc.gpsimd.tensor_tensor(rot_a[:], rot_a[:], w_ln[:, 0], ALU.mult).then_inc(tables, 1)
                nc.gpsimd.tensor_tensor(rot_b[:], rot_b[:], w_ln[:, 1], ALU.mult).then_inc(tables, 1)
                nc.gpsimd.tensor_copy(ident_lo[:], ident[:]).then_inc(tables, 1)
                for c in range(CH):
                    nc.gpsimd.tensor_copy(causal_lo[:, c], causal[:]).then_inc(tables, 1)
                with pool.Fori(0, BLOCKS) as n:
                    pool.wait_ge(ms_ready, n + 1)
                    nc.gpsimd.tensor_tensor(rqk[:], ms[:], neg_half[:, 0:2], ALU.pow).then_inc(rqk_ready, 1)
                    for w in range(2):
                        pool.wait_ge(parts, 2 * n + w + 1)
                        nc.gpsimd.tensor_tensor(qk[:, w], part_a[:, w], part_b[:, w], ALU.add).then_inc(rotated, 1)
                pool.wait_ge(token_var, 1)
                nc.gpsimd.tensor_tensor(token_rstd[:], tvar[:], neg_half[:], ALU.pow).then_inc(token_done, 1)

            @block.vector
            def _(dve):
                dve.sem_inc(qkt_ready, 1)
                dve.sem_inc(s_psum, 2)
                dve.sem_inc(av_psum, 2)
                dve.sem_inc(out_done, 1)
                dve.wait_ge(tables, 3 + CH)

                def front_norm(n):
                    blk = bass.ds(n, 1)
                    dve.wait_ge(qkt_ready, n + 1)
                    nc.vector.tensor_scalar(h[:], y[:, blk].rearrange("p n o q -> p (n o q)"),
                                            token_stats[:, blk, 0], token_rstd[:, blk], ALU.subtract,
                                            ALU.mult).then_inc(h_ready, 1)

                def front_rotate(n):
                    dve.wait_ge(squared, n + 1)
                    nc.vector.tensor_scalar(ms[:], ssq[:], 1.0 / C, 1e-6, ALU.mult, ALU.add).then_inc(ms_ready, 1)
                    dve.wait_ge(rqk_ready, n + 1)
                    half = "p (h s d) -> p h s d"
                    for w, src in enumerate((b_q, b_k)):
                        nc.vector.scalar_tensor_tensor(part_a[:, w], src[:, 0:C], rqk[:, w:w + 1], rot_a[:],
                                                       ALU.mult, ALU.mult)
                        s4 = src[:, 0:C].rearrange(half, s=2, d=HD // 2)
                        o4 = part_b[:, w].rearrange(half, s=2, d=HD // 2)
                        b4 = rot_b[:].rearrange(half, s=2, d=HD // 2)
                        for side in range(2):
                            last = nc.vector.scalar_tensor_tensor(o4[:, :, side], s4[:, :, 1 - side], rqk[:, w:w + 1],
                                                                  b4[:, :, side], ALU.mult, ALU.mult)
                        last.then_inc(parts, 1)

                def back_top(n):
                    dve.wait_ge(s_psum, n + 3)
                    for r in range(4):
                        last = nc.vector.tensor_reduce(top[:, r::4], b_s[r][:, 0:C].rearrange("p (c k) -> p c k", k=P),
                                                       AX.X, ALU.max)
                    last.then_inc(bchain, 1)
                    dve.wait_ge(bchain, 3 * n + 1)
                    nc.vector.tensor_scalar(neg_top[:], top[:], -SCALE, None, ALU.mult).then_inc(top_ready, 1)

                def back_rest(n):
                    blk = bass.ds(n, 1)
                    dve.wait_ge(pt_psum, n + 1)
                    for q in (1, 2):
                        last = nc.vector.tensor_copy(prob_t[:, 4 * q:4 * q + 4],
                                                     b_s[q][:].rearrange("p (h k) -> p h k", k=P))
                    last.then_inc(pt_ready, 1)
                    nc.vector.reciprocal(inv[:], psum[:]).then_inc(bchain, 1)
                    dve.wait_ge(bchain, 3 * n + 2)
                    dve.wait_ge(av_psum, n + 3)
                    hd = "p (h d) -> p h d"
                    nc.vector.tensor_tensor(mixed[:].rearrange(hd, d=HD), b_s[3][:, 0:C].rearrange(hd, d=HD),
                                            inv[:].unsqueeze(2).to_broadcast([P, HEADS, HD]),
                                            ALU.mult).then_inc(mixed_ready, 1)
                    dve.wait_ge(out_psum, n + 1)
                    tok = y[:, blk].rearrange("p n o q -> p (n o q)")
                    nc.vector.tensor_tensor(tok, tok, b_s[1][:, 0:C], ALU.add).then_inc(bchain, 1)
                    dve.wait_ge(bchain, 3 * n + 3)
                    dve.sem_inc(out_done, 1)
                    c = Chain(dve, fchain, 3 * n)
                    c.step(nc.vector.bn_stats(tst[:], tok), apart=True)
                    c.step(nc.vector.bn_aggr(tmv[:, 0], tst[:]))
                    c.step(nc.vector.tensor_copy(token_stats[:, blk], tmv[:]))

                front_norm(0)
                front_rotate(0)
                with dve.Fori(0, BLOCKS - 1) as n:
                    front_norm(n + 1)
                    back_top(n)
                    front_rotate(n + 1)
                    back_rest(n)
                back_top(BLOCKS - 1)
                back_rest(BLOCKS - 1)
                nc.vector.tensor_scalar(tvar[:], token_stats[:, :, 1], 1e-5, None, ALU.add).then_inc(token_var, 1)

            @block.scalar
            def _(act):
                def three(out, src):
                    return nc.scalar.activation(out, src[:, 0:C].rearrange("p (o q) -> p o q", q=P), ACT.Copy)

                def front_h(n):
                    act.wait_ge(ht_psum, n + 1)
                    three(h_t[:], b_ht).then_inc(ht_ready, 1)

                def front_rest(n, u):
                    act.wait_ge(qkv_psum, n + 1)
                    for w, src in enumerate((b_q, b_k)):
                        last = nc.scalar.activation(square[:, w], src[:, 0:C], ACT.Square, accum_out=ssq[:, w:w + 1])
                    last.then_inc(squared, 1)
                    act.wait_ge(av_psum, n + 1)
                    nc.scalar.activation(v[u][:], b_v[:, 0:C], ACT.Copy).then_inc(v_ready, 1)
                    act.wait_ge(qkt_psum, n + 1)
                    act.wait_ge(s_psum, n + 1)
                    three(q_t[u][:], b_ht)
                    three(k_t[u][:], b_v).then_inc(qkt_ready, 1)

                def back_exp(n):
                    act.wait_ge(top_ready, n + 1)
                    for head in range(HEADS):
                        c, r = divmod(head, 4)
                        last = nc.scalar.activation(prob[:, head], b_s[r][:, c * P:(c + 1) * P], ACT.Exp,
                                                    bias=neg_top[:, head:head + 1], scale=SCALE,
                                                    accum_out=psum[:, head:head + 1])
                    last.then_inc(prob_ready, 1)

                def back_prob(n):
                    act.wait_ge(pt_psum, n + 1)
                    nc.scalar.activation(prob_t[:, 0:4], b_s[0][:].rearrange("p (h k) -> p h k", k=P),
                                         ACT.Copy).then_inc(pt_ready, 1)

                def back_mixed(n):
                    act.wait_ge(mt_psum, n + 1)
                    three(mixed_t[:], b_s[0]).then_inc(mt_ready, 1)

                def turn(n, u, more=True):
                    if more:
                        front_h(n + 1)
                    back_exp(n)
                    if more:
                        front_rest(n + 1, 1 - u)
                    back_prob(n)
                    back_mixed(n)

                front_h(0)
                front_rest(0, 0)
                with act.Fori(0, BLOCKS // 2 - 1) as j:
                    turn(2 * j, 0)
                    turn(2 * j + 1, 1)
                turn(BLOCKS - 2, 0)
                turn(BLOCKS - 1, 1, more=False)

            @block.tensor
            def _(pe):
                pe.wait_ge(tables, 3 + CH)

                def three(dst, src):
                    for o in range(CH):
                        last = nc.tensor.transpose(dst[:, o * P:(o + 1) * P], src[:, o * P:(o + 1) * P], ident[:])
                    return last

                def front_h(n):
                    pe.wait_ge(h_ready, n + 1)
                    pe.wait_ge(qkt_ready, n + 1)
                    three(b_ht, h).then_inc(ht_psum, 1)

                def front_qkv(n):
                    pe.wait_ge(ht_ready, n + 1)
                    for w, dst in enumerate((b_q, b_k, b_v)):
                        for o in range(CH):
                            last = nc.tensor.matmul(dst[:, 0:C], h_t[:, o], w_qkv[:, o, w * C:(w + 1) * C],
                                                    start=(o == 0), stop=(o == CH - 1))
                    last.then_inc(qkv_psum, 1)

                def front_turn(n):
                    pe.wait_ge(rotated, 2 * n + 1)
                    three(b_ht, qk[:, 0])
                    pe.wait_ge(v_ready, n + 1)
                    pe.wait_ge(rotated, 2 * n + 2)
                    three(b_v, qk[:, 1]).then_inc(qkt_psum, 1)

                def back_scores(n, u):
                    pe.wait_ge(qkt_ready, n + 2)
                    pe.wait_ge(out_done, n + 1)
                    for c in range(CH):
                        for r in range(4):
                            rows = slice(HD * r, HD * (r + 1))
                            nc.tensor.matmul(b_s[r][:, c * P:(c + 1) * P], q_t[u][rows, c], k_t[u][rows, c],
                                             start=(c == 0), stop=False, skip_group_check=True)
                    for r in range(4):
                        last = nc.tensor.matmul(b_s[r][:, 0:C], ident_lo[:], causal_lo[:].rearrange("p c k -> p (c k)"),
                                                start=False, stop=True, skip_group_check=True)
                    last.then_inc(s_psum, 1)

                def back_prob(n):
                    pe.wait_ge(prob_ready, n + 1)
                    for head in range(HEADS):
                        last = nc.tensor.transpose(b_s[head // 4][:, head % 4 * P:(head % 4 + 1) * P], prob[:, head],
                                                   ident[:])
                    last.then_inc(pt_psum, 1)

                def back_mix(n, u):
                    pe.wait_ge(pt_ready, 2 * n + 2)
                    for head in range(HEADS):
                        d = slice(head * HD, (head + 1) * HD)
                        last = nc.tensor.matmul(b_s[3][:, d], prob_t[:, head], v[u][:, d], start=True, stop=True)
                    last.then_inc(av_psum, 1)

                def back_project(n):
                    pe.wait_ge(mixed_ready, n + 1)
                    three(b_s[0], mixed).then_inc(mt_psum, 1)
                    pe.wait_ge(mt_ready, n + 1)
                    for o in range(CH):
                        last = nc.tensor.matmul(b_s[1][:, 0:C], mixed_t[:, o], w_proj[:, o], start=(o == 0),
                                                stop=(o == CH - 1))
                    last.then_inc(out_psum, 1)

                def turn(n, u, more=True):
                    if more:
                        front_h(n + 1)
                    back_scores(n, u)
                    if more:
                        front_qkv(n + 1)
                    back_prob(n)
                    if more:
                        front_turn(n + 1)
                    back_mix(n, u)
                    back_project(n)

                front_h(0)
                front_qkv(0)
                front_turn(0)
                with pe.Fori(0, BLOCKS // 2 - 1) as j:
                    turn(2 * j, 0)
                    turn(2 * j + 1, 1)
                turn(BLOCKS - 2, 0)
                turn(BLOCKS - 1, 1, more=False)


def head_attention(nc, io, sem, sb, bank, out_img, tokens, ident, neg_half, token_stats, token_rstd):
    WIDE = KEPT * HD
    SIDES = 2
    LOT = WIDE // SIDES
    SCALE = 1.0 / float(np.sqrt(np.float32(HD)))
    HALF = PIX // 2
    STEPS = TILES
    LAST = BATCH - 1
    STACKS = 3
    UNITS = 2 * STEPS
    F32R = mybir.dt.float32r
    NEXT_TILES = [[0], [1, 2], [3], [4], [5], [6], [7], []]
    ROW_STEP = [4, 7]
    PREP = [("w", 0), ("w", 1), ("w", 2), ("bias", 0), ("w", 3), ("wbv", 4), ("v", 0), ("v", 1),
            ("v", 2), ("v", 3), ("wo", 0), ("wo", 1)]

    def fills(s, c, tail, prep):
        out = []
        if tail and c in (0, 4) and 1 <= s <= 4:
            out.append(("out", 2 * (s - 1) + c // 4))
        if tail and c in (3, 7):
            k = 2 * (s - 1) + (c + 1) // 4 - 2
            if 0 <= k < TILES:
                out.append(("turned", k))
        if prep and s == 0:
            out.append(("h", c))
        if prep and s == 1 and c == 5:
            out.append(("logit", 0))
        if prep and 2 <= s <= 4 and c % 4 in (1, 2):
            out.append(PREP[4 * (s - 2) + 2 * (c // 4) + c % 4 - 1])
        return out

    def residual_of(s, c):
        k = 2 * s if c == 7 else 2 * s - 1
        return k if c in (3, 7) and 0 <= k < TILES else None

    def ordered(tail, prep):
        return [f for s in range(KEPT) for c in range(STEPS) for f in fills(s, c, tail, prep)]

    PREPS, BOTH, TAILS = (len(ordered(*kind)) for kind in ((False, True), (True, True), (True, False)))

    class Fills:

        def __init__(self, n, tail, prep):
            if n is None:
                self.base = 0
            elif tail:
                self.base = 2 * PREPS + BOTH * (n - 1)
                if isinstance(n, int) and n == BATCH:
                    self.base += TAILS - BOTH
            else:
                self.base = PREPS
            self.order = ordered(tail, prep)

        def of(self, fill):
            return self.base + self.order.index(fill) + 1

    with ExitStack() as mem:
        w_t = sb(mem, "e_w_t", [3, CH, C])
        w_o = sb(mem, "e_w_o", [CH, C])
        w_r = sb(mem, "e_w_r", [CH, HEADS])
        b_r = sb(mem, "e_b_r", [HEADS])
        b_qk = sb(mem, "e_b_qk", [CH, 2])
        b_v = sb(mem, "e_b_v", [CH, P])
        rows = sb(mem, "e_rows", [3, C])
        slot_of = sb(mem, "e_slot_of", [WIDE])
        head_of = sb(mem, "e_head_of", [CH, HEADS])
        before = sb(mem, "e_before", [HEADS, HEADS])
        tok = sb(mem, "e_tok", [TILES, C])
        img_mean = sb(mem, "e_img_mean", [TILES])
        img_rstd = sb(mem, "e_img_rstd", [TILES])
        img_shift = sb(mem, "e_img_shift", [TILES])
        minus_one = sb(mem, "e_minus_one", [TILES])
        h = [sb(mem, f"e_h{t}", [C]) for t in range(2)]
        h_t = [sb(mem, f"e_h_t{u}", [CH, PIX]) for u in range(2)]
        mean_h = sb(mem, "e_mean_h", [CH])
        mean_b = sb(mem, "e_mean_b", [CH, P])
        logit = sb(mem, "e_logit", [HEADS])
        beats = sb(mem, "e_beats", [HEADS, HEADS])
        ties = sb(mem, "e_ties", [HEADS, HEADS])
        rank = sb(mem, "e_rank", [HEADS])
        keep = sb(mem, "e_keep", [HEADS])
        by_ch = sb(mem, "e_by_ch", [2, CH, HEADS])
        ch_rank = sb(mem, "e_ch_rank", [2, CH])
        select = sb(mem, "e_select", [2, CH, WIDE])
        w_kept = [sb(mem, f"e_w_kept{u}", [3 * CH, WIDE]) for u in range(2)]
        wo_kept = [sb(mem, f"e_wo_kept{u}", [SIDES, C]) for u in range(2)]
        bias = [sb(mem, f"e_bias{u}", [KEPT]) for u in range(2)]
        bv_kept = sb(mem, "e_bv_kept", [WIDE])
        v = [sb(mem, f"e_v{u}", [TILES, KEPT, 2 * HD]) for u in range(2)]
        high = sb(mem, "e_high", [HALF], F32R)
        low = sb(mem, "e_low", [HALF], F32R)
        stack = [sb(mem, f"e_stack{i}", [2, PIX], F32R) for i in range(STACKS)]
        part_top = sb(mem, "e_part_top", [TILES, 2])
        top = sb(mem, "e_top", [TILES])
        prob = [sb(mem, f"e_prob{i}", [HALF]) for i in range(4)]
        den = sb(mem, "e_den", [HALF])
        ctx = [sb(mem, f"e_ctx{u}", [SIDES, PIX]) for u in range(2)]
        t_tok = [sb(mem, f"e_t_tok{i}", [C]) for i in range(2)]
        t_mean = sb(mem, "e_t_mean", [TILES])
        t_rstd = sb(mem, "e_t_rstd", [TILES])
        t_shift = sb(mem, "e_t_shift", [TILES])
        hb = [sb(mem, f"e_hb{i}", [C]) for i in range(2)]
        z = [sb(mem, f"e_z{i}", [C]) for i in range(2)]
        tst = sb(mem, "e_tst", [6])
        tmv = [sb(mem, f"e_tmv{i}", [2]) for i in range(2)]
        zvar = [sb(mem, f"e_zvar{i}", [1]) for i in range(2)]
        zrstd = [sb(mem, f"e_zrstd{i}", [1]) for i in range(2)]
        fin = [sb(mem, f"e_fin{i}", [CH, P]) for i in range(2)]
        b_next = [bank(mem, f"e_next{f}") for f in range(2)]
        b_s = [bank(mem, f"e_s{f}") for f in range(2)]
        b_acc = [bank(mem, f"e_acc{i}") for i in range(2)]
        b_x = bank(mem, "e_x")
        b_z = bank(mem, "e_z")

        consts = sem("e_consts")
        ones_set = sem("e_ones_set")
        tok_loaded = sem("e_tok_loaded")
        img_stats = sem("e_img_stats")
        h_ready = sem("e_h_ready")
        z_full = sem("e_z_full")
        z_free = sem("e_z_free")
        mean_ready = sem("e_mean_ready")
        select_ready = sem("e_select_ready")
        qk_psum = sem("e_qk_psum")
        high_ready = sem("e_high_ready")
        split_done = sem("e_split_done")
        stacked = [sem(f"e_stacked{i}") for i in range(STACKS)]
        next_psum = sem("e_next_psum")
        part_ready = sem("e_part_ready")
        top_ready = sem("e_top_ready")
        row_psum = sem("e_row_psum")
        row_ready = sem("e_row_ready")
        s_psum = sem("e_s_psum")
        prob_ready = sem("e_prob_ready")
        prob_used = sem("e_prob_used")
        den_ready = sem("e_den_ready")
        inverted = sem("e_inverted")
        acc_free = sem("e_acc_free")
        t_tok_loaded = [sem(f"e_t_tok_loaded{i}") for i in range(2)]
        t_stats = sem("e_t_stats")
        residual_made = sem("e_residual_made")
        hb_ready = sem("e_hb_ready")
        zvar_ready = sem("e_zvar_ready")
        zrstd_ready = sem("e_zrstd_ready")
        znorm_ready = sem("e_znorm_ready")
        z_ready = sem("e_z_ready")
        fin_ready = sem("e_fin_ready")
        written = [sem(f"e_written{i}") for i in range(2)]
        pchain = sem("e_pchain")
        tchain = sem("e_tchain")
        zchain = sem("e_zchain")
        rchain = sem("e_rchain")
        CONSTS = 10
        STACK_DMA = 16 * 12
        img_tokens = tokens.rearrange("(b t) p c -> b p t c", t=TILES)

        def head(n, s):
            return KEPT * n + s

        def stacked_count(n, s):
            return STACK_DMA * (2 * n + s // STACKS + 1)

        def turns(eng, turn):
            turn(0, 0, tail=False)
            with eng.Fori(0, BATCH // 2 - 1) as j:
                turn(2 * j + 1, 1)
                turn(2 * j + 2, 0)
            turn(LAST, 1, prep=False)

        with nc.Block() as block:
            @block.sync
            def _(sp):
                def load_image(n):
                    sp.dma_start(tok[:], img_tokens[n]).then_inc(tok_loaded, 16)

                def stack_up(n, s):
                    g, k = head(n, s), s % STACKS
                    sp.wait_ge(split_done, g + 1)
                    sp.nop(nofuse=True)
                    if not isinstance(g, int) or g >= STACKS:
                        sp.wait_ge(s_psum, UNITS * (g - STACKS + 1))
                        sp.nop(nofuse=True)

                    for w, order in enumerate(((high, high, low), (high, low, high))):
                        for at, src in enumerate(order):
                            for f in range(2):
                                part = slice(HD * (2 * w + f), HD * (2 * w + f + 1))
                                sp.dma_start(
                                    stack[k][HD * at:HD * (at + 1), w, f * HALF:(f + 1) * HALF].bitcast(F32),
                                    src[part].bitcast(F32)).then_inc(stacked[k], 16)

                def load_tile(n, k):
                    sp.wait_ge(z_ready, TILES * n + k + 1)
                    sp.nop(nofuse=True)
                    sp.dma_start(t_tok[k % 2][:], img_tokens[n, :, k]).then_inc(t_tok_loaded[k % 2], 16)

                def store(n, k):
                    sp.wait_ge(fin_ready, TILES * n + k + 1)
                    sp.nop(nofuse=True)
                    sp.dma_start(out_img[n, :, :, k * P:(k + 1) * P], fin[k % 2][:]).then_inc(written[k % 2], 16)

                def turn(n, tail=True, prep=True, load=True):
                    for s in range(KEPT):
                        if tail and s == 0:
                            load_tile(n - 1, 0)
                            load_tile(n - 1, 1)
                        if tail and 2 <= s <= 4:
                            load_tile(n - 1, 2 * s - 1)
                        if s + 2 < KEPT or prep:
                            stack_up(n if s + 2 < KEPT else n + 1, (s + 2) % KEPT)
                        if tail and s >= 2:
                            store(n - 1, 2 * s - 3)
                        if tail and 1 <= s <= 3:
                            load_tile(n - 1, 2 * s)
                        if tail and 1 <= s <= 4:
                            store(n - 1, 2 * s - 2)
                        if load and s == 1:
                            sp.wait_ge(h_ready, TILES * (n + 2))
                            sp.nop(nofuse=True)
                            load_image(n + 2)

                for dst, name in ((w_t, "w_t"), (w_o, "w_o"), (w_r, "w_r"), (b_r, "b_r"), (b_qk, "b_qk"), (b_v, "b_v"),
                                  (rows, "rows"), (slot_of, "slot_of"), (head_of, "head_of"), (before, "before")):
                    sp.dma_start(dst[:], io[name]).then_inc(consts, 16)
                load_image(0)
                sp.wait_ge(h_ready, TILES)
                load_image(1)
                stack_up(0, 0)
                stack_up(0, 1)
                turn(0, tail=False)
                with sp.Fori(1, LAST - 1) as n:
                    turn(n)
                turn(LAST - 1, load=False)
                turn(LAST, prep=False, load=False)
                load_tile(LAST, 0)
                load_tile(LAST, 1)
                for k in range(TILES):
                    if k + 2 < TILES:
                        load_tile(LAST, k + 2)
                    store(LAST, k)
                for i in range(2):
                    sp.wait_ge(written[i], 16 * (BLOCKS // 2 + 1))

            @block.gpsimd
            def _(pool):
                for u in range(2):
                    nc.gpsimd.memset(v[u][:], 1.0).then_inc(ones_set, 1)

                def statistics(n, counter, mean, rstd, shift):
                    blk = bass.ds(TILES * n, TILES)
                    c = Chain(pool, counter, 4 * n)
                    pool.nop(nofuse=True)
                    c.step(nc.gpsimd.tensor_copy(mean[:], token_stats[:, blk, 0]), apart=True)
                    c.step(nc.gpsimd.tensor_copy(rstd[:], token_rstd[:, blk]))
                    c.step(nc.gpsimd.tensor_tensor(shift[:], mean[:], rstd[:], ALU.mult))
                    nc.gpsimd.tensor_tensor(shift[:], shift[:], minus_one[:], ALU.mult).then_inc(counter, 1)

                def image_statistics(n):
                    if not isinstance(n, int) or n:
                        pool.wait_ge(h_ready, TILES * n)
                    statistics(n, img_stats, img_mean, img_rstd, img_shift)

                def tail_statistics(n):
                    if not isinstance(n, int) or n:
                        pool.wait_ge(residual_made, TILES * n)
                    statistics(n, t_stats, t_mean, t_rstd, t_shift)

                def add_bias(n, k):
                    pool.wait_ge(residual_made, TILES * n + k + 1)
                    nc.gpsimd.tensor_tensor(hb[k % 2][:], hb[k % 2][:], rows[:, 0], ALU.add).then_inc(hb_ready, 1)

                def root(n, k):
                    pool.wait_ge(zvar_ready, TILES * n + k + 1)
                    nc.gpsimd.tensor_tensor(zrstd[k % 2][:], zvar[k % 2][:], neg_half[:, 0:1], ALU.pow).then_inc(
                        zrstd_ready, 1)

                def finish(n, k):
                    i = k % 2
                    c = Chain(pool, zchain, 2 * (TILES * n + k))
                    pool.wait_ge(znorm_ready, TILES * n + k + 1)
                    c.step(nc.gpsimd.tensor_tensor(z[i][:], z[i][:], rows[:, 1], ALU.mult))
                    c.step(nc.gpsimd.tensor_tensor(z[i][:], z[i][:], rows[:, 2], ALU.add))
                    nc.gpsimd.tensor_tensor(z[i][:], z[i][:], t_tok[i][:], ALU.add).then_inc(z_ready, 1)

                def turn(n, u, tail=True, prep=True):
                    if prep:
                        image_statistics(n + 1)
                    if tail:
                        tail_statistics(n - 1)
                    for s in range(KEPT):
                        for c in range(STEPS):
                            if tail and 1 <= s <= 4 and c in (1, 5):
                                root(n - 1, 2 * (s - 1) + c // 4)
                            if tail and 1 <= s <= 4 and c in (2, 6):
                                finish(n - 1, 2 * (s - 1) + c // 4)
                            if tail and residual_of(s, c) is not None:
                                add_bias(n - 1, residual_of(s, c))

                nc.gpsimd.memset(minus_one[:], -1.0).then_inc(ones_set, 1)
                nc.gpsimd.memset(den[:], 1.0).then_inc(ones_set, 1)
                pool.wait_ge(ones_set, 4)
                pool.wait_ge(consts, 16 * CONSTS)
                image_statistics(0)
                turns(pool, turn)
                tail_statistics(LAST)
                add_bias(LAST, 0)
                for k in range(TILES):
                    root(LAST, k)
                    finish(LAST, k)
                    if k + 1 < TILES:
                        add_bias(LAST, k + 1)

            @block.vector
            def _(dve):
                dve.sem_inc(z_free, 1)
                dve.sem_inc(part_ready, 2)
                dve.sem_inc(prob_ready, 2)
                dve.sem_inc(prob_used, 4)
                dve.sem_inc(acc_free, 2)
                dve.sem_inc(z_ready, 2)
                for i in range(2):
                    dve.sem_inc(written[i], 16)
                dve.wait_ge(consts, 16 * CONSTS)
                dve.wait_ge(ones_set, 4)
                for i in range(STACKS):
                    nc.vector.tensor_scalar(stack[i][96:97, 1], v[0][96:97].rearrange("p t k d -> p (t k d)")[:, 0:PIX],
                                            -1.0, None, ALU.mult).then_inc(ones_set, 1)
                dve.wait_ge(ones_set, 4 + STACKS)

                def router(n, count):
                    c = Chain(dve, pchain, 11 * n)
                    dve.wait_ge(z_full, count.of(("logit", 0)))
                    c.step(nc.vector.tensor_tensor(logit[:], b_z[:, 0:HEADS], b_r[:], ALU.add))
                    dve.sem_inc(z_free, 1)
                    square = [P, HEADS, HEADS]
                    mine = logit[:].unsqueeze(2).to_broadcast(square)
                    other = logit[:].unsqueeze(1).to_broadcast(square)
                    nc.vector.tensor_tensor(beats[:], other, mine, ALU.is_gt)
                    c.step(nc.vector.tensor_tensor(ties[:], other, mine, ALU.is_equal))
                    c.step(nc.vector.tensor_tensor(ties[:], ties[:], before[:], ALU.mult))
                    c.step(nc.vector.tensor_tensor(beats[:], beats[:], ties[:], ALU.add))
                    c.step(nc.vector.reduce_sum(rank[:], beats[:], AX.X))
                    c.step(nc.vector.tensor_scalar(keep[:], rank[:], KEPT - 0.5, None, ALU.is_lt))
                    c.step(nc.vector.tensor_tensor(keep[:], keep[:], logit[:], ALU.add))
                    c.step(nc.vector.tensor_tensor(keep[:], keep[:], logit[:], ALU.subtract))
                    wide = [P, CH, HEADS]
                    nc.vector.tensor_tensor(by_ch[:, 0], head_of[:], rank[:].unsqueeze(1).to_broadcast(wide), ALU.mult)
                    c.step(nc.vector.tensor_tensor(by_ch[:, 1], head_of[:], keep[:].unsqueeze(1).to_broadcast(wide),
                                                   ALU.mult))
                    c.step(nc.vector.reduce_sum(ch_rank[:], by_ch[:], AX.X))
                    for o in range(CH):
                        nc.vector.tensor_scalar(select[:, 0, o], slot_of[:], ch_rank[:, 0, o:o + 1], None, ALU.is_equal)
                        last = nc.vector.tensor_scalar(select[:, 1, o], slot_of[:], ch_rank[:, 0, o:o + 1],
                                                       ch_rank[:, 1, o:o + 1], ALU.is_equal, ALU.mult)
                    c.step(last)
                    dve.sem_inc(select_ready, 1)
                    assert c.n == 11

                def mean(n, u, count):
                    dve.wait_ge(z_free, count.of(("h", TILES - 1)) + 1)
                    nc.vector.reduce_sum(mean_h[:], h_t[u][:], AX.X).then_inc(rchain, 1)
                    dve.wait_ge(rchain, n + 1)
                    nc.vector.tensor_scalar(mean_b[:], mean_h[:].unsqueeze(2).to_broadcast([P, CH, P]), 1.0 / PIX, None,
                                            ALU.mult).then_inc(mean_ready, 1)

                def take(n, u, fill, count):
                    kind, k = fill
                    if kind == "bias":
                        dve.wait_ge(z_full, count.of(fill))
                        for w in range(2):
                            part = slice(2 * HD * w, 2 * HD * (w + 1))
                            last = nc.vector.tensor_copy(
                                bias[u][part], b_z[part, 0:2 * KEPT].rearrange("p (s w) -> p s w", w=2)[:, :, w])
                        last.then_inc(z_free, 1)
                    elif kind == "v":
                        dve.wait_ge(z_full, count.of(fill))
                        nc.vector.tensor_tensor(
                            v[u][:, 2 * k:2 * k + 2, :, 0:HD],
                            b_z[:, 0:2 * WIDE].rearrange("p (t s d) -> p t s d", t=2, d=HD),
                            bv_kept[:].rearrange("p (s d) -> p s d", d=HD).unsqueeze(1).to_broadcast([P, 2, KEPT, HD]),
                            ALU.add).then_inc(z_free, 1)
                    elif kind == "logit":
                        router(n, count)
                    elif kind == "out":
                        i = k % 2
                        dve.wait_ge(hb_ready, TILES * n + k + 1)
                        dve.wait_ge(z_full, count.of(fill))
                        c = Chain(dve, tchain, 3 * (TILES * n + k))
                        c.step(nc.vector.tensor_tensor(z[i][:], b_z[:, 0:C], hb[i][:], ALU.add))
                        dve.sem_inc(z_free, 1)
                        c.step(nc.vector.bn_stats(tst[:], z[i][:]), apart=True)
                        c.step(nc.vector.bn_aggr(tmv[i][:], tst[:]))
                        nc.vector.tensor_scalar(zvar[i][:], tmv[i][:, 1:2], 1e-12, None, ALU.add).then_inc(zvar_ready, 1)

                def norm(n, k):
                    i = k % 2
                    dve.wait_ge(zrstd_ready, TILES * n + k + 1)
                    nc.vector.tensor_scalar(z[i][:], z[i][:], tmv[i][:, 0:1], zrstd[i][:], ALU.subtract,
                                            ALU.mult).then_inc(znorm_ready, 1)

                def split(n, s, u):
                    g = head(n, s)
                    dve.wait_ge(high_ready, g + 1)
                    nc.vector.scalar_tensor_tensor(low[:], b_x[:], bias[u][:, s:s + 1], high[:], ALU.add,
                                                   ALU.subtract).then_inc(split_done, 1)

                def maxima(n, s, t):
                    g = head(n, s)
                    if t % 4 == 0:
                        half = t // 4
                        if s or not isinstance(n, int) or n:
                            dve.wait_ge(top_ready, 2 * g + half - 1)
                    for f in range(2):
                        i = UNITS * g + 2 * t + f
                        dve.wait_ge(next_psum, i + 1)
                        nc.vector.reduce_max(part_top[:, t, f:f + 1], b_next[f][:], AX.X).then_inc(part_ready, 1)

                def join(n, s, half):
                    g = head(n, s)
                    dve.wait_ge(part_ready, UNITS * g + 8 * (half + 1) + 2)
                    part = slice(4 * half, 4 * half + 4)
                    nc.vector.reduce_max(top[:, part], part_top[:, part], AX.X).then_inc(top_ready, 1)

                def divide(n, s, u):
                    g = head(n, s)
                    dve.wait_ge(den_ready, g + 1)
                    nc.vector.reciprocal(den[0:96], den[0:96]).then_inc(inverted, 1)
                    dve.wait_ge(inverted, g + 1)
                    to = slice(HD * (s % 3), HD * (s % 3 + 1))
                    for f in range(2):
                        part = slice(2 * HD * f, 2 * HD * f + HD)
                        last = nc.vector.tensor_tensor(ctx[u][to, s // 3, f * HALF:(f + 1) * HALF],
                                                       b_acc[s % 2][part], den[part], ALU.mult)
                    last.then_inc(acc_free, 1)

                def turn(n, u, tail=True, prep=True):
                    count = Fills(n, tail, prep)
                    for s in range(KEPT):
                        for c in range(STEPS):
                            if s + 1 < KEPT or prep:
                                at = (n, s + 1) if s + 1 < KEPT else (n + 1, 0)
                                for t in NEXT_TILES[c]:
                                    maxima(*at, t)
                                if c in ROW_STEP:
                                    join(*at, ROW_STEP.index(c))
                            if c == 1 and s + 2 < KEPT:
                                split(n, s + 2, u)
                            elif c == 1 and prep:
                                split(n + 1, s + 2 - KEPT, 1 - u)
                            if c == 2 and s:
                                divide(n, s - 1, u)
                            elif c == 2 and tail:
                                divide(n - 1, KEPT - 1, 1 - u)
                            if tail and 1 <= s <= 4 and c in (2, 6):
                                norm(n - 1, 2 * (s - 1) + c // 4)
                            for f in fills(s - (c == 0), (c - 1) % STEPS, tail, prep):
                                of_before = f[0] in ("out", "turned")
                                take(n - 1 if of_before else n + 1, 1 - u, f, count)
                            if prep and s == 1 and c == 0:
                                mean(n + 1, 1 - u, count)

                first = Fills(None, False, True)
                for f in first.order:
                    if f[0] == "logit":
                        mean(0, 0, first)
                    take(0, 0, f, first)
                split(0, 0, 0)
                for t in range(TILES):
                    maxima(0, 0, t)
                    if t % 4 == 3:
                        join(0, 0, t // 4)
                split(0, 1, 0)
                turns(dve, turn)
                divide(LAST, KEPT - 1, 1)
                last = Fills(BATCH, True, False)
                for f in last.order:
                    take(LAST, 1, f, last)
                    if f[0] == "out":
                        norm(LAST, f[1])

            @block.scalar
            def _(act):
                def take(n, u, fill, count):
                    kind, k = fill
                    if kind in ("h", "w", "wbv", "wo", "turned"):
                        act.wait_ge(z_full, count.of(fill))
                    if kind == "h":
                        nc.scalar.activation(h_t[u][:, :, k * P:(k + 1) * P],
                                             b_z[:, 0:C].rearrange("p (o q) -> p o q", q=P), ACT.Copy).then_inc(z_free, 1)
                    elif kind == "w":
                        nc.scalar.activation(w_kept[u][:, 2 * k:2 * k + 2],
                                             b_z[:, 0:2 * WIDE].rearrange("p (g k) -> p g k", g=2),
                                             ACT.Copy).then_inc(z_free, 1)
                    elif kind == "wbv":
                        nc.scalar.activation(w_kept[u][:, 2 * k], b_z[:, 0:WIDE], ACT.Copy)
                        nc.scalar.activation(bv_kept[:], b_z[:, WIDE:2 * WIDE], ACT.Copy).then_inc(z_free, 1)
                    elif kind == "wo":
                        nc.scalar.activation(wo_kept[u][0:LOT, k], b_z[0:LOT, 0:C], ACT.Copy).then_inc(z_free, 1)
                    elif kind == "turned":
                        act.wait_ge(written[k % 2], 16 * (TILES // 2 * n + k // 2 + 1))
                        nc.scalar.activation(fin[k % 2][:], b_z[:, 0:C].rearrange("p (o q) -> p o q", q=P),
                                             ACT.Copy).then_inc(fin_ready, 1)
                        act.wait_ge(fin_ready, TILES * n + k + 1)
                        act.sem_inc(z_free, 1)

                def normalise(n, t, z_of):
                    if t == 0:
                        act.wait_ge(tok_loaded, 16 * (n + 1))
                        act.wait_ge(img_stats, 4 * (n + 1))
                    if z_of is not None:
                        act.wait_ge(z_full, z_of)
                    nc.scalar.activation(h[t % 2][:], tok[:, t], ACT.Identity, bias=img_shift[:, t:t + 1],
                                         scale=img_rstd[:, t:t + 1]).then_inc(h_ready, 1)

                def residual(n, k):
                    i = k % 2
                    act.wait_ge(t_stats, 4 * (n + 1))
                    act.wait_ge(t_tok_loaded[i], 16 * (TILES // 2 * n + k // 2 + 1))
                    act.wait_ge(z_ready, TILES * n + k + 1)
                    nc.scalar.activation(hb[i][:], t_tok[i][:], ACT.Identity, bias=t_shift[:, k:k + 1],
                                         scale=t_rstd[:, k:k + 1]).then_inc(residual_made, 1)

                def project(n, s, u):
                    g = head(n, s)
                    act.wait_ge(qk_psum, g + 1)
                    if s:
                        act.wait_ge(stacked[(s - 1) % STACKS], stacked_count(n, s - 1))
                    elif not isinstance(n, int) or n:
                        act.wait_ge(stacked[(KEPT - 1) % STACKS], stacked_count(n - 1, KEPT - 1))
                    nc.scalar.activation(high[:], b_x[:], ACT.Identity, bias=bias[u][:, s:s + 1]).then_inc(high_ready, 1)

                def row(n, s, half):
                    g = head(n, s)
                    act.wait_ge(row_psum, 2 * g + half + 1)
                    nc.scalar.activation(stack[s % STACKS][96:97, 0, half * HALF:(half + 1) * HALF], b_x[96:97],
                                         ACT.Copy).then_inc(row_ready, 1)

                def exponentials(n, s, c):
                    for f in range(2):
                        i = UNITS * head(n, s) + 2 * c + f
                        act.wait_ge(s_psum, i + 1)
                        act.wait_ge(prob_used, i + 1)
                        nc.scalar.activation(prob[(2 * c + f) % 4][:], b_s[f][:], ACT.Exp, scale=SCALE).then_inc(
                            prob_ready, 1)

                def denominators(n, s):
                    g = head(n, s)
                    act.wait_ge(prob_used, UNITS * (g + 1) + 4)
                    act.wait_ge(acc_free, g + 2)
                    for f in range(2):
                        last = nc.scalar.activation(den[2 * HD * f:2 * HD * f + HD],
                                                    b_acc[s % 2][2 * HD * f + HD:2 * HD * (f + 1)], ACT.Copy)
                    last.then_inc(den_ready, 1)

                def turn(n, u, tail=True, prep=True):
                    count = Fills(n, tail, prep)
                    for s in range(KEPT):
                        for c in range(STEPS):
                            if c == 1 and s:
                                denominators(n, s - 1)
                            elif c == 1 and tail:
                                denominators(n - 1, KEPT - 1)
                            if c == 1 and s + 2 < KEPT:
                                project(n, s + 2, u)
                            elif c == 1 and prep:
                                project(n + 1, s + 2 - KEPT, 1 - u)
                            if prep and s == 0:
                                normalise(n + 1, c, count.of(("h", c - 2)) if c >= 2 else count.base)
                            exponentials(n, s, c)
                            for f in fills(s, c, tail, prep):
                                of_before = f[0] in ("out", "turned")
                                take(n - 1 if of_before else n + 1, 1 - u, f, count)
                            if tail and residual_of(s, c) is not None:
                                residual(n - 1, residual_of(s, c))
                            if c in ROW_STEP and s + 1 < KEPT:
                                row(n, s + 1, ROW_STEP.index(c))
                            elif c in ROW_STEP and prep:
                                row(n + 1, 0, ROW_STEP.index(c))

                act.wait_ge(consts, 16 * CONSTS)
                first = Fills(None, False, True)
                normalise(0, 0, None)
                for f in first.order:
                    if f[0] == "h" and f[1] + 1 < TILES:
                        t = f[1] + 1
                        normalise(0, t, first.of(("h", t - 2)) if t >= 2 else None)
                    take(0, 0, f, first)
                project(0, 0, 0)
                for half in range(2):
                    row(0, 0, half)
                project(0, 1, 0)
                turns(act, turn)
                denominators(LAST, KEPT - 1)
                last = Fills(BATCH, True, False)
                residual(LAST, 0)
                for f in last.order:
                    take(LAST, 1, f, last)
                    if f[0] == "out" and f[1] + 1 < TILES:
                        residual(LAST, f[1] + 1)

            @block.tensor
            def _(pe):
                pe.wait_ge(consts, 16 * CONSTS)
                pe.wait_ge(ones_set, 4 + STACKS)

                def fill(n, u, what, count):
                    kind, k = what
                    pe.wait_ge(z_free, count.of(what))
                    if kind == "h":
                        pe.wait_ge(h_ready, TILES * n + k + 1)
                        for o in range(CH):
                            last = nc.tensor.transpose(b_z[:, o * P:(o + 1) * P], h[k % 2][:, o * P:(o + 1) * P], ident[:])
                    elif kind == "logit":
                        pe.wait_ge(mean_ready, n + 1)
                        for o in range(CH):
                            last = nc.tensor.matmul(b_z[:, 0:HEADS], mean_b[:, o], w_r[:, o], start=(o == 0),
                                                    stop=(o == CH - 1))
                    elif kind in ("w", "wbv"):
                        if k == 0:
                            pe.wait_ge(select_ready, n + 1)
                        for i in range(2):
                            g = 2 * k + i
                            for co in range(CH):
                                if g < 3 * CH:
                                    w, ci = divmod(g, CH)
                                    src = w_t[:, w, co, ci * P:(ci + 1) * P]
                                else:
                                    src = b_v[:, co]
                                last = nc.tensor.matmul(b_z[:, i * WIDE:(i + 1) * WIDE], src, select[:, 1, co],
                                                        start=(co == 0), stop=(co == CH - 1))
                    elif kind == "bias":
                        for s in range(KEPT):
                            for co in range(CH):
                                for q in range(4):
                                    last = nc.tensor.matmul(b_z[HD * q:HD * (q + 1), 2 * s:2 * s + 2],
                                                            select[:, 1, co, s * HD:(s + 1) * HD], b_qk[:, co],
                                                            start=(co == 0), stop=(co == CH - 1))
                    elif kind == "wo":
                        for co in range(CH):
                            last = nc.tensor.matmul(b_z[0:LOT, 0:C], select[:, 0, co, k * LOT:(k + 1) * LOT], w_o[:, co],
                                                    start=(co == 0), stop=(co == CH - 1))
                    elif kind == "v":
                        for i in range(2):
                            t = 2 * k + i
                            for ci in range(CH):
                                last = nc.tensor.matmul(b_z[:, i * WIDE:(i + 1) * WIDE], h_t[u][:, ci, t * P:(t + 1) * P],
                                                        w_kept[u][:, 2 * CH + ci], start=(ci == 0), stop=(ci == CH - 1))
                    elif kind == "out":
                        if k == 0:
                            pe.wait_ge(acc_free, KEPT * (n + 1) + 2)
                        for g in range(SIDES):
                            last = nc.tensor.matmul(b_z[:, 0:C], ctx[u][0:LOT, g, k * P:(k + 1) * P], wo_kept[u][0:LOT, g],
                                                    start=(g == 0), stop=(g == SIDES - 1))
                    elif kind == "turned":
                        pe.wait_ge(z_ready, TILES * n + k + 3)
                        for o in range(CH):
                            last = nc.tensor.transpose(b_z[:, o * P:(o + 1) * P], z[k % 2][:, o * P:(o + 1) * P], ident[:])
                    last.then_inc(z_full, 1)

                def project(n, s, u, rows_before=0):
                    g = head(n, s)
                    if not isinstance(g, int) or g:
                        pe.wait_ge(split_done, g)
                        pe.wait_ge(row_ready, rows_before or 2 * (g - 1))
                    for ci in range(CH):
                        for w in range(2):
                            for f in range(2):
                                at = HD * (2 * w + f)
                                last = nc.tensor.matmul(b_x[at:at + HD], w_kept[u][:, CH * w + ci, s * HD:(s + 1) * HD],
                                                        h_t[u][:, ci, f * HALF:(f + 1) * HALF], start=(ci == 0),
                                                        stop=(ci == CH - 1))
                    last.then_inc(qk_psum, 1)

                def next_scores(n, s, t):
                    g, k = head(n, s), s % STACKS
                    if t == 0:
                        pe.wait_ge(stacked[k], stacked_count(n, s))
                    for f in range(2):
                        i = UNITS * g + 2 * t + f
                        pe.wait_ge(part_ready, i + 1)
                        nc.tensor.matmul(b_next[f][:], stack[k][0:96, 0, t * P:(t + 1) * P],
                                         stack[k][0:96, 1, f * HALF:(f + 1) * HALF], start=True, stop=True).then_inc(
                            next_psum, 1)

                def rows_of(n, s, half, first=False):
                    g = head(n, s)
                    pe.wait_ge(top_ready, 2 * g + half + 1)
                    pe.wait_ge(split_done, g + 1 if first else g + 2)
                    if half:
                        pe.wait_ge(row_ready, 2 * g + 1)
                    for t in range(4):
                        at = 4 * half + t
                        last = nc.tensor.matmul(b_x[96:97, t * P:(t + 1) * P], top[:, at:at + 1], ident[:], start=True,
                                                stop=True)
                    last.then_inc(row_psum, 1)

                def scores(n, s, c):
                    k = s % STACKS
                    for f in range(2):
                        i = UNITS * head(n, s) + 2 * c + f
                        pe.wait_ge(prob_ready, i + 1)
                        nc.tensor.matmul(b_s[f][:], stack[k][0:97, 1, c * P:(c + 1) * P],
                                         stack[k][0:97, 0, f * HALF:(f + 1) * HALF], start=True, stop=True).then_inc(
                            s_psum, 1)

                def mix(n, s, u, c):
                    g = head(n, s)
                    if c == 0:
                        pe.wait_ge(acc_free, g + 1)
                    pe.wait_ge(prob_ready, UNITS * g + 2 * c + 4)
                    for f in range(2):
                        at = 2 * HD * f
                        last = nc.tensor.matmul(b_acc[s % 2][at:at + 2 * HD], v[u][:, c, s], prob[(2 * c + f) % 4][:],
                                                start=(c == 0), stop=(c == STEPS - 1))
                        last.then_inc(prob_used, 1)

                def turn(n, u, tail=True, prep=True):
                    count = Fills(n, tail, prep)
                    for s in range(KEPT):
                        following = (n, s + 1) if s + 1 < KEPT else (n + 1, 0)
                        for c in range(STEPS):
                            if s + 1 < KEPT or prep:
                                for t in NEXT_TILES[c]:
                                    next_scores(*following, t)
                            if c:
                                mix(n, s, u, c - 1)
                            elif s:
                                mix(n, s - 1, u, STEPS - 1)
                            elif tail:
                                mix(n - 1, KEPT - 1, 1 - u, STEPS - 1)
                            if c == 0 and s + 2 < KEPT:
                                project(n, s + 2, u)
                            elif c == 0 and prep:
                                project(n + 1, s + 2 - KEPT, 1 - u)
                            elif c == 0:
                                pe.wait_ge(row_ready, 2 * (head(n, s) + 1))
                            scores(n, s, c)
                            for f in fills(s, c, tail, prep):
                                of_before = f[0] in ("out", "turned")
                                fill(n - 1 if of_before else n + 1, 1 - u, f, count)
                            if c in ROW_STEP and (s + 1 < KEPT or prep):
                                rows_of(*following, ROW_STEP.index(c), first=(not prep and s + 1 == KEPT - 1))

                first = Fills(None, False, True)
                for f in first.order:
                    fill(0, 0, f, first)
                project(0, 0, 0)
                for t in range(TILES):
                    next_scores(0, 0, t)
                for half in range(2):
                    rows_of(0, 0, half, first=True)
                project(0, 1, 0, rows_before=2)
                turns(pe, turn)
                mix(LAST, KEPT - 1, 1, STEPS - 1)
                last = Fills(BATCH, True, False)
                for f in last.order:
                    fill(LAST, 1, f, last)


def kernel(**inputs):
    import numpy as _np
    import concourse.bacc as _bacc
    from concourse import mybir as _mybir
    from concourse.bass_utils import run_bass_kernel_spmd as _run

    a = {k: _np.asarray(v) for k, v in inputs.items()}
    ow = a["L0_conv_off_w"].reshape(2 * TAPS, C, TAPS)
    ob = a["L0_conv_off_b"]
    off_w = _np.concatenate([ow[0::2], ow[1::2], a["L0_conv_mask_w"].reshape(TAPS, C, TAPS)])
    off_b = _np.concatenate([ob[0::2], ob[1::2], a["L0_conv_mask_b"]])

    def chunks(w):
        return w.reshape(CH, P, *w.shape[1:]).swapaxes(0, 1)

    arrays = dict(shape_constants())
    arrays["x"] = a["x"]
    arrays["w_off"] = chunks(off_w.transpose(1, 2, 0))
    arrays["b_off"] = _np.tile(off_b, (P, 1))
    arrays["w_conv"] = chunks(a["L0_conv_proj_w"].reshape(C, C, TAPS).transpose(1, 2, 0)).swapaxes(1, 2)
    arrays["gamma"] = chunks(a["L0_conv_gamma"])
    arrays["beta"] = chunks(a["L0_conv_beta"])
    half = _np.concatenate([_np.arange(0, HD, 2), _np.arange(1, HD, 2)])
    order = (_np.arange(HEADS)[:, None] * HD + half).reshape(-1)
    partner = _np.roll(order.reshape(HEADS, HD), HD // 2, axis=1).reshape(-1)
    w = a["L1_attn_w_qkv"]
    arrays["w_qkv"] = chunks(_np.concatenate([w[:, order], w[:, C + order], w[:, 2 * C:]], axis=1))
    arrays["w_proj"] = chunks(a["L1_attn_w_proj"])
    ln = a["L1_attn_w_ln"]
    arrays["w_ln"] = _np.tile(_np.stack([ln[order], ln[partner]]), (P, 1, 1))
    arrays["w_t"] = _np.stack([chunks(a["L1_ffn_W" + k].T) for k in "qkv"], axis=1)
    arrays["w_o"] = chunks(a["L1_ffn_Wo"])
    arrays["w_r"] = chunks(a["L1_ffn_Wr"])
    arrays["b_r"] = _np.tile(a["L1_ffn_br"], (P, 1))
    arrays["b_qk"] = chunks(_np.stack([a["L1_ffn_bq"], a["L1_ffn_bk"]], axis=1))
    arrays["b_v"] = chunks(_np.tile(a["L1_ffn_bv"][:, None], (1, P)))
    arrays["rows"] = _np.tile(_np.stack([a["L1_ffn_bo"], a["L1_ffn_ln_g"], a["L1_ffn_ln_b"]]), (P, 1, 1))
    arrays["b_conv"] = chunks(a["L0_conv_proj_b"])

    nc = _bacc.Bacc("TRN2", target_bir_lowering=False, num_devices=1)
    io, fed = {}, {}
    for name, v in arrays.items():
        v = _np.ascontiguousarray(v)
        fed["in_" + name] = v
        io[name] = nc.dram_tensor("in_" + name, v.shape, _mybir.dt.from_np(v.dtype), kind="ExternalInput").ap()
    io["out"] = nc.dram_tensor("out_0", (BATCH, C, SIDE, SIDE), F32, kind="ExternalOutput").ap()
    build(nc, io)
    r = _run(nc, [fed], core_ids=[0])
    return r.results[0]["out_0"]
```

```python
from contextlib import ExitStack

import numpy as np
import concourse.bass as bass
from concourse import mybir
from concourse.alu_op_type import AluOpType as ALU

ACT = mybir.ActivationFunctionType
AX = mybir.AxisListType
F32 = mybir.dt.float32
BF16 = mybir.dt.bfloat16
U32 = mybir.dt.uint32

P = 128
BATCH, C, SIDE = 8, 384, 32
PIX = SIDE * SIDE
CH = C // P
TAPS = 9
TILES = PIX // P
BLOCKS = BATCH * TILES
GROUP = 4
GROUPS = BLOCKS // GROUP
PADW = SIDE + 2
MAX_OFF = float(SIDE // 4)
GN_GROUPS = 32
CORNERS = 4
CORNER_SHIFT = [0, 1, SIDE, SIDE + 1]
LEAD = SIDE + 1
IMG_ROWS = PIX + LEAD
HEADS, HD = 12, 32
KEPT = 6
ROUND = float(3 * 2 ** 22)

MASKED = -1e30


def shape_constants():
    f = np.float32
    ch = np.arange(C)
    same = (ch[:, None] // (C // GN_GROUPS) == ch[None, :] // (C // GN_GROUPS)).astype(f) / f(C // GN_GROUPS)
    p = np.arange(P)
    tile = np.arange(TILES)
    tap = np.arange(TAPS)
    row = (tile[None, :, None] * (P // SIDE) + p[:, None, None] // SIDE) - 1 + tap[None, None, :] // 3
    col = (p[:, None, None] % SIDE) - 1 + tap[None, None, :] % 3 + 0 * tile[None, :, None]
    pos = np.concatenate([row, col], axis=2).astype(f)
    rows0 = np.tile((np.arange(BATCH) * IMG_ROWS + LEAD).astype(f), (P, 1))
    freq = np.power(f(10000.0), (f(-2.0) * np.arange(0, HD, 2, dtype=f) - f(1.0)) / f(HD), dtype=f)
    ts = p.astype(f)[:, None] * freq[None, :]
    even = np.arange(0, HD, 2)
    channel = np.concatenate([even, even + 1]) % (HD // 2)
    cos, sin = np.cos(ts)[:, channel], np.sin(ts)[:, channel]
    sin = np.where(np.arange(HD) < HD // 2, -sin, sin)
    dim = np.arange(KEPT * HD)
    slot_of = np.where(dim[None, :] % HD == p[:, None] % HD, dim[None, :] // HD, -1)
    head_of = (np.arange(CH)[None, :, None] * P + p[:, None, None]) // HD == np.arange(HEADS)[None, None, :]
    before = np.arange(HEADS)[None, :] < np.arange(HEADS)[:, None]
    quarter = np.arange(P)[:, None] % 32 == np.arange(3 * TAPS)[None, :]
    return {
        "add_quarters": quarter.astype(f),
        "slot_of": slot_of.astype(f),
        "head_of": head_of.astype(f),
        "before": np.tile(before.astype(f), (P, 1, 1)),
        "rot_cos": np.tile(cos, (1, HEADS)).astype(f),
        "rot_sin": np.tile(sin, (1, HEADS)).astype(f),
        "causal": np.where(p[None, :] <= p[:, None], f(0), f(MASKED)).astype(f),
        "ident": np.eye(P, dtype=f),
        "same_group": np.ascontiguousarray(same.reshape(CH, P, C).transpose(1, 0, 2)),
        "tap_pos": pos,
        "table_row0": rows0,
    }


class Chain:

    def __init__(self, eng, sem, base):
        self.eng, self.sem, self.base, self.n = eng, sem, base, 0

    def step(self, ins, apart=False):
        self.n += 1
        ins.then_inc(self.sem, 1)
        self.eng.wait_ge(self.sem, self.base + self.n)
        if apart:
            self.eng.nop(nofuse=True)


def build(nc, io):
    x_img = io["x"].rearrange("b (o p) h w -> b p o (h w)", p=P)
    out_img = io["out"].rearrange("b (o p) h w -> b p o (h w)", p=P)
    table = nc.dram_tensor("corner_table", (BATCH * IMG_ROWS, CORNERS * C), F32, kind="Internal").ap()

    tokens = nc.dram_tensor("tokens", (BLOCKS, P, C), F32, kind="Internal").ap()

    with ExitStack() as whole:
        def sem(name):
            return whole.enter_context(nc.semaphore(name))

        def sb(stack, name, shape, dt=F32):
            return stack.enter_context(nc.sbuf_tensor(name, [P] + shape, dt))

        def bank(stack, name, dt=F32, width=512):
            return stack.enter_context(nc.psum_tensor(name, [P, width], dt))

        ident = sb(whole, "ident", [P])
        neg_half = sb(whole, "neg_half", [BLOCKS])
        token_stats = sb(whole, "token_stats", [BLOCKS, 2])
        token_rstd = sb(whole, "token_rstd", [BLOCKS])
        with ExitStack() as layers:
            y = sb(layers, "y", [BLOCKS, CH, P])
            conv_stats = sb(layers, "conv_stats", [CH, GROUPS, 6])
            with ExitStack() as conv:
                tap_index = sb(conv, "tap_index", [GROUPS + 1, TAPS, GROUP], U32)
                corner_w = sb(conv, "corner_w", [GROUPS, CORNERS, TAPS, GROUP])
                offsets_and_table(nc, io, sem, sb, bank, x_img, table, ident, tap_index, corner_w, neg_half, y)
                deform_conv(nc, io, sem, sb, bank, table, ident, tap_index, corner_w, y, conv_stats)
            batch_norm_gelu(nc, io, sem, sb, bank, x_img, ident, neg_half, y, conv_stats, token_stats, token_rstd)
            block_attention(nc, io, sem, sb, bank, ident, neg_half, y, tokens, token_stats, token_rstd)
        head_attention(nc, io, sem, sb, bank, out_img, tokens, ident, neg_half, token_stats, token_rstd)


def offsets_and_table(nc, io, sem, sb, bank, x_img, table, ident, tap_index, corner_w, neg_half, y):
    NOUT = 3 * TAPS
    QUARTER = 32
    HALF = PIX // 2
    with ExitStack() as mem:
        x_in = [sb(mem, f"a_x{u}", [CH, PIX]) for u in range(2)]
        size = CH * PADW * PADW
        y_flat = y[:].rearrange("p n o q -> p (n o q)")
        xpad = [y_flat[:, u * size:(u + 1) * size].rearrange("p (o h w) -> p o h w", o=CH, h=PADW)
                for u in range(2)]
        tok = [sb(mem, f"a_tok{u}", [TILES, C]) for u in range(2)]
        w_off = sb(mem, "a_w_off", [CH, TAPS, QUARTER])
        add_quarters = sb(mem, "a_add_quarters", [NOUT])
        part = [sb(mem, f"a_part{f}", [HALF]) for f in range(2)]
        b_off = sb(mem, "a_b_off", [NOUT])
        same_group = sb(mem, "a_same_group", [CH, C])
        tap_pos = sb(mem, "a_tap_pos", [TILES, 2 * TAPS])
        table_row0 = sb(mem, "a_table_row0", [BATCH])
        bst = sb(mem, "a_bst", [CH, 2, 6])
        mv = sb(mem, "a_mv", [CH, 2])
        stat = sb(mem, "a_stat", [CH, 2])
        gstat = sb(mem, "a_gstat", [CH, 2])
        gvar = sb(mem, "a_gvar", [CH])
        rstd = sb(mem, "a_rstd", [CH])
        shift = sb(mem, "a_shift", [CH])
        norm_scale = [sb(mem, f"a_ns{u}", [CH]) for u in range(2)]
        norm_shift = [sb(mem, f"a_nb{u}", [CH]) for u in range(2)]
        raw = sb(mem, "a_raw", [TILES, NOUT])
        pos = sb(mem, "a_pos", [TILES, 2 * TAPS])
        base = sb(mem, "a_base", [TILES, 2 * TAPS])
        dist = sb(mem, "a_dist", [2, TILES, 2 * TAPS])
        wgt = sb(mem, "a_wgt", [2, TILES, 2 * TAPS])
        mask = sb(mem, "a_mask", [TILES, TAPS])
        wy = sb(mem, "a_wy", [2, TILES, TAPS])
        row = sb(mem, "a_row", [TILES, TAPS])
        gps = bank(mem, "a_gps")
        cps = [bank(mem, f"a_cps{f}") for f in range(2)]
        offps = [bank(mem, f"a_offps{u}") for u in range(2)]
        tps = [bank(mem, f"a_tps{u}") for u in range(2)]

        consts = sem("a_consts")
        cleared = sem("a_cleared")
        x_loaded = [sem(f"a_x_loaded{u}") for u in range(2)]
        table_written = [sem(f"a_table_written{u}") for u in range(2)]
        stats_ready = sem("a_stats_ready")
        group_ready = sem("a_group_ready")
        var_ready = sem("a_var_ready")
        rstd_ready = sem("a_rstd_ready")
        norm_ready = sem("a_norm_ready")
        padded = sem("a_padded")
        xn_ready = sem("a_xn_ready")
        conv_psum = sem("a_conv_psum")
        part_ready = sem("a_part_ready")
        tp_ready = sem("a_tp_ready")
        tp_free = sem("a_tp_free")
        off_ready = sem("a_off_ready")
        raw_ready = sem("a_raw_ready")
        mask_ready = sem("a_mask_ready")
        fchain = sem("a_fchain")
        bchain = sem("a_bchain")
        gaps_filled = sem("a_gaps_filled")
        NCONST = 7
        GAPS = 2 * (CORNERS - 1)
        img_rows = table.rearrange("(b r) c -> r b c", r=IMG_ROWS)

        with nc.Block() as block:
            @block.sync
            def _(sp):
                def load_x(j, u, first=False):
                    if not first:
                        sp.wait_ge(tp_ready, TILES * (2 * j + u - 1))
                    sp.dma_start(x_in[u][:], x_img[2 * j + u]).then_inc(x_loaded[u], 16)

                sp.dma_start(ident[:], io["ident"]).then_inc(consts, 16)
                sp.dma_start(w_off[:], io["w_off"]).then_inc(consts, 16)
                sp.dma_start(b_off[:], io["b_off"]).then_inc(consts, 16)
                sp.dma_start(add_quarters[:], io["add_quarters"]).then_inc(consts, 16)
                sp.dma_start(same_group[:], io["same_group"]).then_inc(consts, 16)
                sp.dma_start(tap_pos[:], io["tap_pos"]).then_inc(consts, 16)
                sp.dma_start(table_row0[:], io["table_row0"]).then_inc(consts, 16)
                for u in range(2):
                    load_x(0, u, first=True)
                sp.wait_ge(cleared, 5)
                for s, d in enumerate(CORNER_SHIFT):
                    for first, many in ((0, LEAD - d), (LEAD - d + PIX, d)):
                        if many:
                            sp.dma_start(img_rows[first:first + many, :, s * C:(s + 1) * C],
                                         tok[0][0:many]).then_inc(gaps_filled, 16)

                def turn(j, u, more):
                    if more:
                        load_x(j + 1, u)
                    sp.wait_ge(tp_free, TILES * (2 * j + u + 1) + 2)
                    for s, d in enumerate(CORNER_SHIFT):
                        first = (2 * j + u) * IMG_ROWS + LEAD - d
                        dst = table[bass.ds(first, PIX), s * C:(s + 1) * C].rearrange("(t p) c -> p t c", p=P)
                        sp.dma_start(dst, tok[u][:]).then_inc(table_written[u], 16)

                with sp.Fori(0, BATCH // 2 - 1) as j:
                    for u in range(2):
                        turn(j, u, True)
                for u in range(2):
                    turn(BATCH // 2 - 1, u, False)
                for u in range(2):
                    sp.wait_ge(table_written[u], 16 * CORNERS * BATCH // 2 + 1)

            @block.gpsimd
            def _(pool):
                nc.gpsimd.memset(tok[0][:], 0.0).then_inc(cleared, 1)
                nc.gpsimd.memset(neg_half[:], -0.5).then_inc(cleared, 1)
                nc.gpsimd.memset(tap_index[:, GROUPS], 0).then_inc(cleared, 1)
                for u in range(2):
                    nc.gpsimd.memset(xpad[u], 0.0).then_inc(cleared, 1)
                pool.wait_ge(cleared, 5)
                with pool.Fori(0, BATCH) as n:
                    pool.wait_ge(var_ready, n + 1)
                    nc.gpsimd.tensor_tensor(rstd[:], gvar[:], neg_half[:, 0:CH], ALU.pow).then_inc(rstd_ready, 1)

            @block.vector
            def _(dve):
                for u in range(2):
                    dve.sem_inc(table_written[u], 1)
                dve.sem_inc(xn_ready, 2)
                dve.sem_inc(tp_free, 2)
                dve.wait_ge(consts, 16 * NCONST)
                dve.wait_ge(gaps_filled, 16 * GAPS)

                def front(j, u):
                    n = 2 * j + u
                    c = Chain(dve, fchain, 7 * n)
                    dve.wait_ge(x_loaded[u], 16 * (j + 1))
                    for o in range(CH):
                        for h in range(2):
                            last = nc.vector.bn_stats(bst[:, o, h], x_in[u][:, o, h * 512:(h + 1) * 512])
                    c.step(last, apart=True)
                    for o in range(CH):
                        last = nc.vector.bn_aggr(mv[:, o], bst[:, o])
                    c.step(last)
                    nc.vector.tensor_copy(stat[:, :, 0], mv[:, :, 0])
                    c.step(nc.vector.tensor_tensor(stat[:, :, 1], mv[:, :, 0], mv[:, :, 0], ALU.mult))
                    nc.vector.tensor_tensor(stat[:, :, 1], stat[:, :, 1], mv[:, :, 1], ALU.add).then_inc(stats_ready, 1)
                    dve.wait_ge(group_ready, n + 1)
                    c.step(nc.vector.tensor_copy(gstat[:], gps[:, 0:2 * CH].rearrange("p (o s) -> p o s", s=2)))
                    c.step(nc.vector.tensor_tensor(gvar[:], gstat[:, :, 0], gstat[:, :, 0], ALU.mult))
                    c.step(nc.vector.tensor_tensor(gvar[:], gstat[:, :, 1], gvar[:], ALU.subtract))
                    nc.vector.tensor_scalar(gvar[:], gvar[:], 1e-5, None, ALU.add).then_inc(var_ready, 1)
                    dve.wait_ge(rstd_ready, n + 1)
                    dve.wait_ge(xn_ready, n + 1)
                    c.step(nc.vector.tensor_copy(norm_scale[u][:], rstd[:]))
                    nc.vector.scalar_tensor_tensor(norm_shift[u][:], gstat[:, :, 0], -1.0, rstd[:], ALU.mult,
                                                   ALU.mult).then_inc(norm_ready, 1)
                    assert c.n == 7

                def back(j, u):
                    n = 2 * j + u
                    c = Chain(dve, bchain, 14 * n)
                    dve.wait_ge(table_written[u], 16 * CORNERS * j + 1)
                    for i in range(TILES):
                        dve.wait_ge(tp_ready, TILES * n + i + 1)
                        nc.vector.tensor_copy(tok[u][:, i], tps[i % 2][:, 0:C]).then_inc(tp_free, 1)
                    dve.wait_ge(off_ready, n + 1)
                    c.step(nc.vector.tensor_tensor(
                        raw[:], offps[u][:, 0:TILES * NOUT].rearrange("p (t k) -> p t k", k=NOUT),
                        b_off[:].unsqueeze(1).to_broadcast([P, TILES, NOUT]), ALU.add))
                    dve.sem_inc(raw_ready, 1)
                    c.step(nc.vector.tensor_scalar(pos[:], raw[:, :, 0:2 * TAPS], -MAX_OFF, MAX_OFF, ALU.max, ALU.min))
                    c.step(nc.vector.tensor_tensor(pos[:], pos[:], tap_pos[:], ALU.add))
                    c.step(nc.vector.tensor_scalar(base[:], pos[:], 0.25, SIDE - 1.25, ALU.max, ALU.min))
                    c.step(nc.vector.tensor_scalar(base[:], base[:], -0.5, ROUND, ALU.add, ALU.add))
                    c.step(nc.vector.tensor_scalar(base[:], base[:], -ROUND, None, ALU.add))
                    c.step(nc.vector.tensor_tensor(dist[:, 0], pos[:], base[:], ALU.subtract))
                    c.step(nc.vector.tensor_scalar(dist[:, 1], dist[:, 0], -1.0, None, ALU.add))
                    c.step(nc.vector.tensor_scalar(wgt[:], dist[:], -1.0, 1.0, ALU.mult, ALU.add))
                    flat = "p s t k -> p (s t k)"
                    c.step(nc.vector.scalar_tensor_tensor(wgt[:].rearrange(flat), dist[:].rearrange(flat), 1.0,
                                                          wgt[:].rearrange(flat), ALU.add, ALU.min))
                    c.step(nc.vector.tensor_scalar(wgt[:], wgt[:], 0.0, None, ALU.max))
                    c.step(nc.vector.scalar_tensor_tensor(row[:], base[:, :, 0:TAPS], float(SIDE), base[:, :, TAPS:],
                                                          ALU.mult, ALU.add))
                    halves = "p (g i) k -> p g i k"
                    for g in range(2):
                        nc.vector.tensor_scalar(
                            tap_index[:, bass.ds(2 * n + g, 1)].rearrange("p g k i -> p (g i) k"),
                            row[:, g * GROUP:(g + 1) * GROUP], table_row0[:, bass.ds(n, 1)], None, ALU.add)
                    dve.wait_ge(mask_ready, n + 1)
                    for a in range(2):
                        last = nc.vector.scalar_tensor_tensor(wy[:, a], wgt[:, a, :, 0:TAPS], 2.0, mask[:],
                                                              ALU.mult, ALU.mult)
                    c.step(last)
                    for g in range(2):
                        for a in range(2):
                            for b in range(2):
                                rows = slice(g * GROUP, (g + 1) * GROUP)
                                last = nc.vector.tensor_tensor(
                                    corner_w[:, bass.ds(2 * n + g, 1), 2 * a + b].rearrange("p g k i -> p (g i) k"),
                                    wy[:, a, rows], wgt[:, b, rows, TAPS:], ALU.mult)
                    c.step(last)
                    assert c.n == 14

                front(0, 0)
                with dve.Fori(0, BATCH // 2 - 1) as j:
                    front(j, 1)
                    back(j, 0)
                    front(j + 1, 0)
                    back(j, 1)
                front(BATCH // 2 - 1, 1)
                back(BATCH // 2 - 1, 0)
                back(BATCH // 2 - 1, 1)

            @block.scalar
            def _(act):
                act.wait_ge(cleared, 5)

                def front(j, u):
                    n = 2 * j + u
                    act.wait_ge(norm_ready, n + 1)
                    for o in range(CH):
                        last = nc.scalar.activation(
                            xpad[u][:, o, 1:1 + SIDE, 1:1 + SIDE], x_in[u][:, o].rearrange("p (h w) -> p h w", w=SIDE),
                            ACT.Identity, bias=norm_shift[u][:, o:o + 1], scale=norm_scale[u][:, o:o + 1])
                    last.then_inc(padded, 1)
                    act.wait_ge(padded, n + 1)
                    for o in range(CH):
                        last = nc.scalar.activation(x_in[u][:, o], x_in[u][:, o], ACT.Identity,
                                                    bias=norm_shift[u][:, o:o + 1], scale=norm_scale[u][:, o:o + 1])
                    last.then_inc(xn_ready, 1)

                def back(n):
                    for f in range(2):
                        act.wait_ge(conv_psum, 2 * n + f + 1)
                        nc.scalar.activation(part[f][:], cps[f][:], ACT.Copy).then_inc(part_ready, 1)
                    act.wait_ge(raw_ready, n + 1)
                    nc.scalar.activation(mask[:], raw[:, :, 2 * TAPS:], ACT.Sigmoid).then_inc(mask_ready, 1)

                front(0, 0)
                with act.Fori(0, BATCH // 2 - 1) as j:
                    front(j, 1)
                    back(2 * j)
                    front(j + 1, 0)
                    back(2 * j + 1)
                front(BATCH // 2 - 1, 1)
                back(BATCH - 2)
                back(BATCH - 1)

            @block.tensor
            def _(pe):
                pe.wait_ge(consts, 16 * NCONST)

                def front(n):
                    pe.wait_ge(stats_ready, n + 1)
                    for co in range(CH):
                        for ci in range(CH):
                            last = nc.tensor.matmul(gps[:, 2 * co:2 * co + 2], same_group[:, ci, co * P:(co + 1) * P],
                                                    stat[:, ci, :], start=(ci == 0), stop=(ci == CH - 1))
                    last.then_inc(group_ready, 1)

                def back(j, u):
                    n = 2 * j + u
                    pe.wait_ge(xn_ready, n + 3)
                    for f in range(2):
                        for i in range(TAPS * CH):
                            t, o = divmod(i, CH)
                            q = QUARTER * (i % 4)
                            top = t // 3 + f * SIDE // 2
                            last = nc.tensor.matmul(cps[f][q:q + QUARTER], w_off[:, o, t, :],
                                                    xpad[u][:, o, top:top + SIDE // 2, t % 3:t % 3 + SIDE],
                                                    start=(i < 4), stop=(i >= TAPS * CH - 4))
                        last.then_inc(conv_psum, 1)
                    for i in range(TILES):
                        pe.wait_ge(tp_free, TILES * n + i + 1)
                        for o in range(CH):
                            last = nc.tensor.transpose(tps[i % 2][:, o * P:(o + 1) * P],
                                                       x_in[u][:, o, P * i:P * (i + 1)], ident[:])
                        last.then_inc(tp_ready, 1)
                    pe.wait_ge(part_ready, 2 * n + 2)
                    for i in range(TILES):
                        at = P * (i % (TILES // 2))
                        last = nc.tensor.matmul(offps[u][:, i * NOUT:(i + 1) * NOUT],
                                                part[i // (TILES // 2)][:, at:at + P], add_quarters[:],
                                                start=True, stop=True)
                    last.then_inc(off_ready, 1)

                front(0)
                with pe.Fori(0, BATCH // 2 - 1) as j:
                    front(2 * j + 1)
                    back(j, 0)
                    front(2 * j + 2)
                    back(j, 1)
                front(BATCH - 1)
                back(BATCH // 2 - 1, 0)
                back(BATCH // 2 - 1, 1)


def deform_conv(nc, io, sem, sb, bank, table, ident, tap_index, corner_w, y, conv_stats):
    STEPS = 2 * TAPS
    TURN = STEPS * GROUP
    SLOTS = 4
    with ExitStack() as mem:
        w_conv = sb(mem, "b_w", [TAPS, CH, C])
        b_conv = sb(mem, "b_b", [CH])
        got = [sb(mem, f"b_got{s}", [CORNERS * C]) for s in range(SLOTS)]
        mix = [sb(mem, f"b_mix{s}", [C]) for s in range(SLOTS)]
        sampled = [sb(mem, f"b_sampled{u}", [CH, GROUP * P]) for u in range(2)]
        index = [sb(mem, f"b_index{g}", [TAPS, GROUP], U32) for g in range(2)]
        weight = sb(mem, "b_weight", [CORNERS, TAPS, GROUP])
        tps = [bank(mem, f"b_tps{u}") for u in range(2)]
        acc = [[bank(mem, f"b_acc{g}{o}") for o in range(CH)] for g in range(2)]

        consts = sem("b_consts")
        index_ready = sem("b_index_ready")
        gathered = [sem(f"b_gathered{s}") for s in range(SLOTS)]
        mixed = sem("b_mixed")
        transposed = sem("b_transposed")
        evacuated = sem("b_evacuated")
        tps_free = sem("b_tps_free")
        sampled_free = sem("b_sampled_free")
        acc_ready = sem("b_acc_ready")
        acc_free = sem("b_acc_free")
        chain = sem("b_chain")
        gchain = sem("b_gchain")

        with nc.Block() as block:
            @block.sync
            def _(sp):
                sp.dma_start(w_conv[:], io["w_conv"]).then_inc(consts, 16)
                sp.dma_start(b_conv[:], io["b_conv"]).then_inc(consts, 16)

            @block.gpsimd
            def _(pool):
                with pool.Fori(0, BATCH) as n:
                    for t in range(TURN):
                        s, i = divmod(t, GROUP)
                        g, k = divmod(s, TAPS)
                        if t % (TURN // 2) == 0:
                            pool.wait_ge(index_ready, 2 * n + g + 1)
                        pool.wait_ge(mixed, TURN * n + t + 1)
                        pool.nop(nofuse=True)
                        nc.gpsimd.indirect_dma_start(
                            out=got[t % SLOTS][:], out_offset=None, in_=table[:, :],
                            in_offset=bass.IndirectOffsetOnAxis(ap=index[g][:, k, i:i + 1], axis=0),
                        ).then_inc(gathered[t % SLOTS], 16)

            @block.vector
            def _(dve):
                dve.sem_inc(transposed, SLOTS)
                dve.sem_inc(tps_free, 2)
                dve.sem_inc(sampled_free, 2)
                dve.sem_inc(acc_free, 2)
                dve.sem_inc(mixed, SLOTS)
                dve.wait_ge(consts, 32)
                nc.vector.tensor_copy(index[0][:], tap_index[:, 0]).then_inc(index_ready, 1)

                def take(n, g, is_last=False):
                    c = Chain(dve, gchain, 6 * n + (2, 4 if is_last else 5)[g])
                    dve.wait_ge(acc_ready, 2 * n + g + 1)
                    b0 = TILES * n + GROUP * g
                    for o in range(CH):
                        last = nc.vector.tensor_scalar(
                            y[:, bass.ds(b0, GROUP), o], acc[g][o][:].rearrange("p (b q) -> p b q", q=P),
                            b_conv[:, o:o + 1], None, ALU.add)
                    c.step(last)
                    dve.sem_inc(acc_free, 1)
                    for o in range(CH):
                        last = nc.vector.bn_stats(conv_stats[:, o, bass.ds(2 * n + g, 1)], y[:, bass.ds(b0, GROUP), o])
                    c.step(last)

                def turn(n, first=False):
                    for t in range(TURN):
                        s, i = divmod(t, GROUP)
                        g, k = divmod(s, TAPS)
                        if t % (TURN // 2) == 0:
                            dve.wait_ge(mixed, TURN * n + t + SLOTS)
                            nc.vector.tensor_copy(index[1 - g][:], tap_index[:, bass.ds(2 * n + g + 1, 1)]).then_inc(
                                index_ready, 1)
                            nc.vector.tensor_copy(weight[:], corner_w[:, bass.ds(2 * n + g, 1)]).then_inc(gchain, 1)
                            dve.wait_ge(gchain, 6 * n + ((1, 2) if first else (-1, 2))[g])
                        if k == 2 and i == 0:
                            if g == 1:
                                take(n, 0)
                            elif not first:
                                take(n - 1, 1)
                        c = Chain(dve, chain, 3 * (TURN * n + t))
                        dve.wait_ge(gathered[t % SLOTS], 16 * (TURN // SLOTS * n + t // SLOTS + 1))
                        dve.wait_ge(transposed, TURN * n + t + 1)
                        src, dst = got[t % SLOTS], mix[t % SLOTS]
                        c.step(nc.vector.tensor_scalar(dst[:], src[:, 0:C], weight[:, 0, k, i:i + 1], None, ALU.mult))
                        for q in range(1, CORNERS):
                            ins = nc.vector.scalar_tensor_tensor(dst[:], src[:, q * C:(q + 1) * C],
                                                                 weight[:, q, k, i:i + 1], dst[:], ALU.mult, ALU.add)
                            if q < CORNERS - 1:
                                c.step(ins)
                        ins.then_inc(mixed, 1)

                turn(0, first=True)
                with dve.Fori(1, BATCH) as n:
                    turn(n)
                take(BATCH - 1, 1, is_last=True)

            @block.scalar
            def _(act):
                with act.Fori(0, BATCH) as n:
                    for t in range(TURN):
                        s, i = divmod(t, GROUP)
                        if i == 0:
                            act.wait_ge(sampled_free, STEPS * n + s + 1)
                        act.wait_ge(transposed, TURN * n + t + SLOTS + 1)
                        nc.scalar.activation(sampled[s % 2][:, :, i * P:(i + 1) * P],
                                             tps[t % 2][:, 0:C].rearrange("p (o q) -> p o q", q=P),
                                             ACT.Copy).then_inc(evacuated, 1)
                        act.wait_ge(evacuated, TURN * n + t + 1)
                        act.sem_inc(tps_free, 1)

            @block.tensor
            def _(pe):
                pe.wait_ge(consts, 32)

                def product(n, s, i):
                    g, k = divmod(s, TAPS)
                    if i == 0:
                        if k == 0:
                            pe.wait_ge(acc_free, 2 * n + g + 1)
                        pe.wait_ge(evacuated, GROUP * (STEPS * n + s + 1))
                    pairs = [(co, ci) for co in range(CH) for ci in range(CH)]
                    for co, ci in pairs[i * CH * CH // GROUP:(i + 1) * CH * CH // GROUP]:
                        last = nc.tensor.matmul(acc[g][co][:], w_conv[:, k, ci, co * P:(co + 1) * P],
                                                sampled[s % 2][:, ci], start=(k == 0 and ci == 0),
                                                stop=(k == TAPS - 1 and ci == CH - 1))
                    if i == GROUP - 1:
                        if k == TAPS - 1:
                            last.then_inc(acc_ready, 1)
                            pe.wait_ge(acc_ready, 2 * n + g + 1)
                            pe.sem_inc(sampled_free, 1)
                        else:
                            last.then_inc(sampled_free, 1)

                def turn(n, first=False):
                    for s in range(STEPS):
                        for i in range(GROUP):
                            t = s * GROUP + i
                            pe.wait_ge(mixed, TURN * n + t + SLOTS + 1)
                            pe.wait_ge(tps_free, TURN * n + t + 1)
                            for o in range(CH):
                                last = nc.tensor.transpose(tps[t % 2][:, o * P:(o + 1) * P],
                                                           mix[t % SLOTS][:, o * P:(o + 1) * P], ident[:])
                            last.then_inc(transposed, 1)
                            if s:
                                product(n, s - 1, i)
                            elif not first:
                                product(n - 1, STEPS - 1, i)

                turn(0, first=True)
                with pe.Fori(1, BATCH) as n:
                    turn(n)
                for i in range(GROUP):
                    product(BATCH - 1, STEPS - 1, i)


def batch_norm_gelu(nc, io, sem, sb, bank, x_img, ident, neg_half, y, conv_stats, token_stats, token_rstd):
    WIDE = GROUP * P
    with ExitStack() as mem:
        x_in = [sb(mem, f"c_x{u}", [CH, WIDE]) for u in range(2)]
        act_out = [sb(mem, f"c_act{u}", [CH, WIDE]) for u in range(2)]
        gamma = sb(mem, "c_gamma", [CH])
        beta = sb(mem, "c_beta", [CH])
        mv = sb(mem, "c_mv", [CH, 2])
        var = sb(mem, "c_var", [CH])
        rstd = sb(mem, "c_rstd", [CH])
        scale = sb(mem, "c_scale", [CH])
        shift = sb(mem, "c_shift", [CH])
        tst = sb(mem, "c_tst", [GROUP, 6])
        tmv = sb(mem, "c_tmv", [GROUP, 2])
        tvar = sb(mem, "c_tvar", [BLOCKS])
        tps = [bank(mem, f"c_tps{i}") for i in range(2 * GROUP)]

        consts = sem("c_consts")
        x_loaded = [sem(f"c_x_loaded{u}") for u in range(2)]
        x_free = sem("c_x_free")
        var_ready = sem("c_var_ready")
        rstd_ready = sem("c_rstd_ready")
        coef_ready = sem("c_coef_ready")
        act_ready = sem("c_act_ready")
        summed = sem("c_summed")
        transposed = sem("c_transposed")
        tps_free = sem("c_tps_free")
        chain = sem("c_chain")
        lchain = sem("c_lchain")
        token_var = sem("c_token_var")
        token_done = sem("c_token_done")

        with nc.Block() as block:
            @block.sync
            def _(sp):
                sp.dma_start(gamma[:], io["gamma"]).then_inc(consts, 16)
                sp.dma_start(beta[:], io["beta"]).then_inc(consts, 16)
                with sp.Fori(0, BATCH) as n:
                    for u in range(2):
                        sp.wait_ge(x_free, 2 * n + u + 1)
                        sp.dma_start(x_in[u][:], x_img[n, :, :, u * WIDE:(u + 1) * WIDE]).then_inc(x_loaded[u], 16)

            @block.gpsimd
            def _(pool):
                pool.wait_ge(var_ready, 1)
                nc.gpsimd.tensor_tensor(rstd[:], var[:], neg_half[:, 0:CH], ALU.pow).then_inc(rstd_ready, 1)
                with pool.Fori(0, BATCH) as n:
                    for u in range(2):
                        pool.wait_ge(act_ready, 2 * n + u + 1)
                        pool.wait_ge(x_loaded[u], 16 * (n + 1))
                        nc.gpsimd.tensor_tensor(x_in[u][:], x_in[u][:], act_out[u][:], ALU.add).then_inc(summed, 1)
                pool.wait_ge(token_var, 1)
                nc.gpsimd.tensor_tensor(token_rstd[:], tvar[:], neg_half[:], ALU.pow).then_inc(token_done, 1)

            @block.vector
            def _(dve):
                dve.sem_inc(x_free, 2)
                dve.sem_inc(summed, 2)
                dve.sem_inc(tps_free, 2 * GROUP)
                dve.wait_ge(consts, 32)
                c = Chain(dve, chain, 0)
                for o in range(CH):
                    last = nc.vector.bn_aggr(mv[:, o], conv_stats[:, o])
                c.step(last)
                nc.vector.tensor_scalar(var[:], mv[:, :, 1], 1e-5, None, ALU.add).then_inc(var_ready, 1)
                dve.wait_ge(rstd_ready, 1)
                c.step(nc.vector.tensor_tensor(scale[:], rstd[:], gamma[:], ALU.mult))
                c.step(nc.vector.tensor_tensor(shift[:], mv[:, :, 0], scale[:], ALU.mult))
                nc.vector.tensor_tensor(shift[:], beta[:], shift[:], ALU.subtract).then_inc(coef_ready, 1)
                with dve.Fori(0, BATCH) as n:
                    for u in range(2):
                        c = Chain(dve, lchain, 3 * (2 * n + u))
                        for i in range(GROUP):
                            count = TILES * n + u * GROUP + i
                            dve.wait_ge(transposed, count + 1)
                            tile = tps[u * GROUP + i][:, 0:C]
                            nc.vector.tensor_copy(y[:, bass.ds(count, 1)].rearrange("p n o q -> p (n o q)"), tile)
                            last = nc.vector.bn_stats(tst[:, i], tile)
                        c.step(last, apart=True)
                        dve.sem_inc(tps_free, GROUP)
                        dve.sem_inc(x_free, 1)
                        for i in range(GROUP):
                            last = nc.vector.bn_aggr(tmv[:, i], tst[:, i])
                        c.step(last)
                        c.step(nc.vector.tensor_copy(token_stats[:, bass.ds(TILES * n + u * GROUP, GROUP)], tmv[:]))
                nc.vector.tensor_scalar(tvar[:], token_stats[:, :, 1], 1e-5, None, ALU.add).then_inc(token_var, 1)

            @block.scalar
            def _(act):
                act.wait_ge(coef_ready, 1)
                with act.Fori(0, BATCH) as n:
                    for u in range(2):
                        act.wait_ge(summed, 2 * n + u + 1)
                        act.nop(nofuse=True)
                        for o in range(CH):
                            last = nc.scalar.activation(
                                act_out[u][:, o].rearrange("p (b q) -> p b q", q=P),
                                y[:, bass.ds(TILES * n + u * GROUP, GROUP), o], ACT.Gelu,
                                bias=shift[:, o:o + 1], scale=scale[:, o:o + 1])
                        last.then_inc(act_ready, 1)

            @block.tensor
            def _(pe):
                with pe.Fori(0, BATCH) as n:
                    for u in range(2):
                        pe.wait_ge(summed, 2 * n + u + 3)
                        for i in range(GROUP):
                            count = TILES * n + u * GROUP + i
                            pe.wait_ge(tps_free, count + 1)
                            for o in range(CH):
                                last = nc.tensor.transpose(tps[u * GROUP + i][:, o * P:(o + 1) * P],
                                                           x_in[u][:, o, i * P:(i + 1) * P], ident[:])
                            last.then_inc(transposed, 1)


def block_attention(nc, io, sem, sb, bank, ident, neg_half, y, tokens, token_stats, token_rstd):
    F32R = mybir.dt.float32r
    SCALE = 1.0 / float(np.sqrt(np.float32(HD)))
    with ExitStack() as mem:
        w_qkv = sb(mem, "d_w_qkv", [CH, 3 * C])
        w_proj = sb(mem, "d_w_proj", [CH, C])
        rot_a = sb(mem, "d_rot_a", [C])
        rot_b = sb(mem, "d_rot_b", [C])
        w_ln = sb(mem, "d_w_ln", [2, C])
        ident_lo = sb(mem, "d_ident_lo", [P], BF16)
        causal = sb(mem, "d_causal", [P])
        causal_lo = sb(mem, "d_causal_lo", [CH, P], BF16)
        h = sb(mem, "d_h", [C])
        w_high = sb(mem, "d_w_high", [CH, 3 * C], F32R)
        w_low = sb(mem, "d_w_low", [CH, 3 * C], F32R)
        h_high = sb(mem, "d_h_high", [CH, P], F32R)
        h_low = sb(mem, "d_h_low", [CH, P], F32R)
        v = [sb(mem, f"d_v{u}", [C]) for u in range(2)]
        square = sb(mem, "d_square", [2, C])
        ssq = sb(mem, "d_ssq", [2])
        ms = sb(mem, "d_ms", [2])
        rqk = sb(mem, "d_rqk", [2])
        part_a = sb(mem, "d_part_a", [2, C])
        part_b = sb(mem, "d_part_b", [2, C])
        qk = sb(mem, "d_qk", [2, C])
        q_t = sb(mem, "d_q_t", [CH, P])
        k_t = sb(mem, "d_k_t", [CH, P])
        top = sb(mem, "d_top", [HEADS])
        neg_top = sb(mem, "d_neg_top", [HEADS])
        prob = sb(mem, "d_prob", [HEADS, P])
        psum = sb(mem, "d_psum", [HEADS])
        prob_t = sb(mem, "d_prob_t", [HEADS, P])
        inv = sb(mem, "d_inv", [HEADS])
        mixed = sb(mem, "d_mixed", [C])
        mixed_t = sb(mem, "d_mixed_t", [CH, P])
        tst = sb(mem, "d_tst", [6])
        tmv = sb(mem, "d_tmv", [1, 2])
        tvar = sb(mem, "d_tvar", [BLOCKS])
        b_ht, b_q, b_k, b_v = [bank(mem, f"d_front{i}") for i in range(4)]
        b_s = [bank(mem, f"d_back{i}") for i in range(4)]

        consts = sem("d_consts")
        tables = sem("d_tables")
        w_split = sem("d_w_split")
        h_ready = sem("d_h_ready")
        ht_psum = sem("d_ht_psum")
        ht_high = sem("d_ht_high")
        ht_ready = sem("d_ht_ready")
        qk_psum = sem("d_qk_psum")
        v_psum = sem("d_v_psum")
        squared = sem("d_squared")
        v_ready = sem("d_v_ready")
        ms_ready = sem("d_ms_ready")
        rqk_ready = sem("d_rqk_ready")
        parts = sem("d_parts")
        rotated = sem("d_rotated")
        qkt_psum = sem("d_qkt_psum")
        qkt_ready = sem("d_qkt_ready")
        s_psum = sem("d_s_psum")
        top_ready = sem("d_top_ready")
        prob_ready = sem("d_prob_ready")
        inv_ready = sem("d_inv_ready")
        pt_psum = sem("d_pt_psum")
        pt_ready = sem("d_pt_ready")
        av_psum = sem("d_av_psum")
        mixed_ready = sem("d_mixed_ready")
        mt_psum = sem("d_mt_psum")
        mt_ready = sem("d_mt_ready")
        out_psum = sem("d_out_psum")
        out_done = sem("d_out_done")
        stored = sem("d_stored")
        fchain = sem("d_fchain")
        bchain = sem("d_bchain")
        mchain = sem("d_mchain")
        token_var = sem("d_token_var")
        token_done = sem("d_token_done")
        CONSTS = 6
        END = BLOCKS - 1
        HALVES = [[4 * c + r for c in range(CH) for r in pair] for pair in ((0, 1), (2, 3))]
        ORDER = HALVES[0] + HALVES[1]

        def turns(eng, turn):
            turn(0, 0, False, 2)
            with eng.Fori(0, (BLOCKS - 4) // 2) as j:
                turn(2 * j + 1, 1, True, 2)
                turn(2 * j + 2, 0, True, 2)
            turn(END - 2, 1, True, 2)
            turn(END - 1, 0, True, 1)
            turn(END, 1, True, 0)

        with nc.Block() as block:
            @block.sync
            def _(sp):
                sp.dma_start(w_qkv[:], io["w_qkv"]).then_inc(consts, 16)
                sp.dma_start(w_proj[:], io["w_proj"]).then_inc(consts, 16)
                sp.dma_start(rot_a[:], io["rot_cos"]).then_inc(consts, 16)
                sp.dma_start(rot_b[:], io["rot_sin"]).then_inc(consts, 16)
                sp.dma_start(w_ln[:], io["w_ln"]).then_inc(consts, 16)
                sp.dma_start(causal[:], io["causal"]).then_inc(consts, 16)
                with sp.Fori(0, BLOCKS) as n:
                    sp.wait_ge(out_done, n + 2)
                    sp.dma_start(tokens[n], y[:, bass.ds(n, 1)].rearrange("p n o q -> p (n o q)")).then_inc(stored, 16)
                sp.wait_ge(stored, 16 * BLOCKS)

            @block.gpsimd
            def _(pool):
                pool.wait_ge(consts, 16 * CONSTS)
                nc.gpsimd.tensor_tensor(rot_a[:], rot_a[:], w_ln[:, 0], ALU.mult).then_inc(tables, 1)
                nc.gpsimd.tensor_tensor(rot_b[:], rot_b[:], w_ln[:, 1], ALU.mult).then_inc(tables, 1)
                nc.gpsimd.tensor_copy(ident_lo[:], ident[:]).then_inc(tables, 1)
                for c in range(CH):
                    nc.gpsimd.tensor_copy(causal_lo[:, c], causal[:]).then_inc(tables, 1)
                with pool.Fori(0, BLOCKS) as n:
                    pool.wait_ge(ms_ready, n + 1)
                    nc.gpsimd.tensor_tensor(rqk[:], ms[:], neg_half[:, 0:2], ALU.pow).then_inc(rqk_ready, 1)
                    for w in range(2):
                        pool.wait_ge(parts, 2 * n + w + 1)
                        nc.gpsimd.tensor_tensor(qk[:, w], part_a[:, w], part_b[:, w], ALU.add).then_inc(rotated, 1)
                pool.wait_ge(token_var, 1)
                nc.gpsimd.tensor_tensor(token_rstd[:], tvar[:], neg_half[:], ALU.pow).then_inc(token_done, 1)

            @block.vector
            def _(dve):
                dve.sem_inc(qkt_ready, 2)
                dve.sem_inc(mt_ready, 2)
                dve.sem_inc(out_done, 1)
                dve.wait_ge(tables, 3 + CH)

                def norm(n):
                    blk = bass.ds(n, 1)
                    if not isinstance(n, int) or n:
                        dve.wait_ge(ht_psum, n)
                    nc.vector.tensor_scalar(h[:], y[:, blk].rearrange("p n o q -> p (n o q)"),
                                            token_stats[:, blk, 0], token_rstd[:, blk], ALU.subtract,
                                            ALU.mult).then_inc(h_ready, 1)

                def low(n):
                    dve.wait_ge(ht_high, n + 1)
                    nc.vector.tensor_tensor(h_low[:], b_ht[:, 0:C].rearrange("p (o q) -> p o q", q=P), h_high[:],
                                            ALU.subtract).then_inc(ht_ready, 1)

                def rotate(n):
                    dve.wait_ge(squared, n + 1)
                    nc.vector.tensor_scalar(ms[:], ssq[:], 1.0 / C, 1e-6, ALU.mult, ALU.add).then_inc(ms_ready, 1)
                    dve.wait_ge(rqk_ready, n + 1)
                    half = "p (h s d) -> p h s d"
                    for w, src in enumerate((b_q, b_k)):
                        nc.vector.scalar_tensor_tensor(part_a[:, w], src[:, 0:C], rqk[:, w:w + 1], rot_a[:],
                                                       ALU.mult, ALU.mult)
                        s4 = src[:, 0:C].rearrange(half, s=2, d=HD // 2)
                        o4 = part_b[:, w].rearrange(half, s=2, d=HD // 2)
                        b4 = rot_b[:].rearrange(half, s=2, d=HD // 2)
                        for side in range(2):
                            last = nc.vector.scalar_tensor_tensor(o4[:, :, side], s4[:, :, 1 - side], rqk[:, w:w + 1],
                                                                  b4[:, :, side], ALU.mult, ALU.mult)
                        last.then_inc(parts, 1)

                def maxima(n):
                    dve.wait_ge(s_psum, n + 1)
                    by_bank = "p (c r) -> p c r"
                    for half, pair in enumerate(((0, 1), (2, 3))):
                        for r in pair:
                            last = nc.vector.tensor_reduce(top[:, r::4],
                                                           b_s[r][:, 0:C].rearrange("p (c k) -> p c k", k=P),
                                                           AX.X, ALU.max)
                        last.then_inc(mchain, 1)
                        dve.wait_ge(mchain, 2 * n + half + 1)
                        both = slice(pair[0], pair[1] + 1)
                        nc.vector.tensor_scalar(neg_top[:].rearrange(by_bank, r=4)[:, :, both],
                                                top[:].rearrange(by_bank, r=4)[:, :, both], -SCALE, None,
                                                ALU.mult).then_inc(top_ready, 1)

                def inverse(n):
                    dve.wait_ge(prob_ready, 2 * n + 2)
                    if not isinstance(n, int) or n:
                        dve.wait_ge(mixed_ready, n)
                    nc.vector.reciprocal(inv[:], psum[:]).then_inc(inv_ready, 1)

                def divide(n):
                    dve.wait_ge(av_psum, n + 1)
                    dve.wait_ge(inv_ready, n + 1)
                    hd = "p (h d) -> p h d"
                    nc.vector.tensor_tensor(mixed[:].rearrange(hd, d=HD), b_s[3][:, 0:C].rearrange(hd, d=HD),
                                            inv[:].unsqueeze(2).to_broadcast([P, HEADS, HD]),
                                            ALU.mult).then_inc(mixed_ready, 1)

                def add(n):
                    blk = bass.ds(n, 1)
                    dve.wait_ge(out_psum, n + 1)
                    tok = y[:, blk].rearrange("p n o q -> p (n o q)")
                    nc.vector.tensor_tensor(tok, tok, b_v[:, 0:C], ALU.add).then_inc(bchain, 1)
                    dve.wait_ge(bchain, n + 1)
                    dve.sem_inc(out_done, 1)

                def statistics(n):
                    blk = bass.ds(n, 1)
                    tok = y[:, blk].rearrange("p n o q -> p (n o q)")
                    c = Chain(dve, fchain, 3 * n)
                    c.step(nc.vector.bn_stats(tst[:], tok), apart=True)
                    c.step(nc.vector.bn_aggr(tmv[:, 0], tst[:]))
                    c.step(nc.vector.tensor_copy(token_stats[:, blk], tmv[:]))

                def turn(i, u, project, later):
                    if later == 2:
                        low(i + 2)
                    inverse(i)
                    if project:
                        add(i - 1)
                    divide(i)
                    if project:
                        statistics(i - 1)
                    if later:
                        maxima(i + 1)
                    if later == 2 and (not isinstance(i, int) or i + 3 < BLOCKS):
                        norm(i + 3)
                    if later == 2:
                        rotate(i + 2)

                norm(0)
                dve.wait_ge(w_split, CH)
                for o in range(CH):
                    nc.vector.tensor_tensor(w_low[:, o], w_qkv[:, o], w_high[:, o], ALU.subtract).then_inc(w_split, 1)
                low(0)
                norm(1)
                low(1)
                rotate(0)
                norm(2)
                maxima(0)
                rotate(1)
                turns(dve, turn)
                add(END)
                statistics(END)
                nc.vector.tensor_scalar(tvar[:], token_stats[:, :, 1], 1e-5, None, ALU.add).then_inc(token_var, 1)

            @block.scalar
            def _(act):
                def three(out, src):
                    return nc.scalar.activation(out, src[:, 0:C].rearrange("p (o q) -> p o q", q=P), ACT.Copy)

                def copy_prob(n):
                    act.wait_ge(pt_psum, n + 1)
                    for q in range(CH):
                        nc.scalar.activation(prob_t[:, 4 * q:4 * q + 4], b_s[q][:].rearrange("p (h k) -> p h k", k=P),
                                             ACT.Copy).then_inc(pt_ready, 1)

                def copy_h(n):
                    act.wait_ge(ht_psum, n + 1)
                    three(h_high[:], b_ht).then_inc(ht_high, 1)

                def copy_qk(n):
                    act.wait_ge(qkt_psum, n + 1)
                    three(q_t[:], b_ht)
                    three(k_t[:], b_s[0]).then_inc(qkt_ready, 1)

                def copy_mixed(n):
                    act.wait_ge(mt_psum, n + 1)
                    three(mixed_t[:], b_v).then_inc(mt_ready, 1)

                def exponentials(n):
                    for half, heads in enumerate(HALVES):
                        act.wait_ge(top_ready, 2 * n + half + 1)
                        for head in heads:
                            c, r = divmod(head, 4)
                            last = nc.scalar.activation(prob[:, head], b_s[r][:, c * P:(c + 1) * P], ACT.Exp,
                                                        bias=neg_top[:, head:head + 1], scale=SCALE,
                                                        accum_out=psum[:, head:head + 1])
                        last.then_inc(prob_ready, 1)

                def squares(n):
                    act.wait_ge(qk_psum, n + 1)
                    for w, src in enumerate((b_q, b_k)):
                        last = nc.scalar.activation(square[:, w], src[:, 0:C], ACT.Square, accum_out=ssq[:, w:w + 1])
                    last.then_inc(squared, 1)

                def copy_v(n, u):
                    act.wait_ge(v_psum, n + 1)
                    nc.scalar.activation(v[u][:], b_v[:, 0:C], ACT.Copy).then_inc(v_ready, 1)

                def turn(i, u, project, later):
                    if later == 2:
                        copy_h(i + 2)
                    copy_prob(i)
                    if later:
                        copy_qk(i + 1)
                    copy_mixed(i)
                    if later:
                        exponentials(i + 1)
                    if later == 2:
                        squares(i + 2)
                        copy_v(i + 2, u)

                act.wait_ge(consts, 16 * CONSTS)
                for o in range(CH):
                    nc.scalar.activation(w_high[:, o], w_qkv[:, o], ACT.Copy).then_inc(w_split, 1)
                copy_h(0)
                squares(0)
                copy_v(0, 0)
                copy_h(1)
                copy_qk(0)
                exponentials(0)
                squares(1)
                copy_v(1, 1)
                turns(act, turn)

            @block.tensor
            def _(pe):
                pe.wait_ge(tables, 3 + CH)

                def three(dst, src):
                    for o in range(CH):
                        last = nc.tensor.transpose(dst[:, o * P:(o + 1) * P], src[:, o * P:(o + 1) * P], ident[:])
                    return last

                def turn_h(n):
                    pe.wait_ge(h_ready, n + 1)
                    pe.wait_ge(qkt_ready, n + 1)
                    three(b_ht, h).then_inc(ht_psum, 1)

                def make_qkv(n):
                    pe.wait_ge(ht_ready, n + 1)
                    for w, dst in enumerate((b_q, b_k, b_v)):
                        if w == 2:
                            pe.wait_ge(mt_ready, n + 1)
                        for i, (a, b) in enumerate(((h_high, w_high), (h_high, w_low), (h_low, w_high))):
                            for o in range(CH):
                                last = nc.tensor.matmul(dst[:, 0:C], a[:, o], b[:, o, w * C:(w + 1) * C],
                                                        start=(i == 0 and o == 0), stop=(i == 2 and o == CH - 1))
                        if w:
                            last.then_inc((qk_psum, v_psum)[w - 1], 1)

                def turn_qk(n, last=False):
                    pe.wait_ge(rotated, 2 * n + 1)
                    pe.wait_ge(ht_ready, n + 1 if last else n + 2)
                    three(b_ht, qk[:, 0])
                    pe.wait_ge(rotated, 2 * n + 2)
                    three(b_s[0], qk[:, 1]).then_inc(qkt_psum, 1)

                def scores(n):
                    pe.wait_ge(qkt_ready, n + 3)
                    for c in range(CH):
                        for r in range(4):
                            rows = slice(HD * r, HD * (r + 1))
                            nc.tensor.matmul(b_s[r][:, c * P:(c + 1) * P], q_t[rows, c], k_t[rows, c],
                                             start=(c == 0), stop=False, skip_group_check=True)
                    for r in range(4):
                        last = nc.tensor.matmul(b_s[r][:, 0:C], ident_lo[:], causal_lo[:].rearrange("p c k -> p (c k)"),
                                                start=False, stop=True, skip_group_check=True)
                    last.then_inc(s_psum, 1)

                def turn_prob(n):
                    for j, head in enumerate(ORDER):
                        if j % (HEADS // 2) == 0:
                            pe.wait_ge(prob_ready, 2 * n + j // (HEADS // 2) + 1)
                        last = nc.tensor.transpose(b_s[j // 4][:, j % 4 * P:(j % 4 + 1) * P], prob[:, head], ident[:])
                    last.then_inc(pt_psum, 1)

                def mix(n, u):
                    for j, head in enumerate(ORDER):
                        if j % 4 == 0:
                            pe.wait_ge(pt_ready, CH * n + j // 4 + 1)
                        d = slice(head * HD, (head + 1) * HD)
                        last = nc.tensor.matmul(b_s[3][:, d], prob_t[:, j], v[u][:, d], start=True, stop=True)
                    last.then_inc(av_psum, 1)

                def turn_mixed(n):
                    pe.wait_ge(mixed_ready, n + 1)
                    pe.wait_ge(out_done, n + 1)
                    three(b_v, mixed).then_inc(mt_psum, 1)

                def project(n, newest_v):
                    pe.wait_ge(mt_ready, n + 3)
                    pe.wait_ge(v_ready, newest_v + 1)
                    for o in range(CH):
                        last = nc.tensor.matmul(b_v[:, 0:C], mixed_t[:, o], w_proj[:, o], start=(o == 0),
                                                stop=(o == CH - 1))
                    last.then_inc(out_psum, 1)

                def turn(i, u, before, later):
                    if later == 2:
                        turn_h(i + 2)
                    turn_prob(i)
                    if before:
                        project(i - 1, i + 1 if later else END)
                    mix(i, u)
                    if later:
                        turn_qk(i + 1, last=(later == 1))
                    if not before:
                        pe.wait_ge(v_ready, 2)
                    turn_mixed(i)
                    if later:
                        scores(i + 1)
                    if later == 2:
                        make_qkv(i + 2)

                turn_h(0)
                pe.wait_ge(w_split, 2 * CH)
                make_qkv(0)
                turn_h(1)
                turn_qk(0)
                scores(0)
                pe.wait_ge(v_ready, 1)
                make_qkv(1)
                turns(pe, turn)
                project(END, END)


def head_attention(nc, io, sem, sb, bank, out_img, tokens, ident, neg_half, token_stats, token_rstd):
    WIDE = KEPT * HD
    SIDES = 2
    LOT = WIDE // SIDES
    SCALE = 1.0 / float(np.sqrt(np.float32(HD)))
    HALF = PIX // 2
    STEPS = TILES
    LAST = BATCH - 1
    STACKS = 3
    UNITS = 2 * STEPS
    F32R = mybir.dt.float32r
    NEXT_TILES = [[0], [1, 2], [3], [4], [5], [6], [7], []]
    ROW_STEP = [4, 7]
    PREP = [("w", 0), ("w", 1), ("w", 2), ("bias", 0), ("w", 3), ("wbv", 4), ("v", 0), ("v", 1),
            ("v", 2), ("v", 3), ("wo", 0), ("wo", 1)]

    def fills(s, c, tail, prep):
        out = []
        if tail and c in (0, 4) and 1 <= s <= 4:
            out.append(("out", 2 * (s - 1) + c // 4))
        if tail and c in (3, 7):
            k = 2 * (s - 1) + (c + 1) // 4 - 2
            if 0 <= k < TILES:
                out.append(("turned", k))
        if prep and s == 0:
            out.append(("h", c))
        if prep and s == 1 and c == 5:
            out.append(("logit", 0))
        if prep and 2 <= s <= 4 and c % 4 in (1, 2):
            out.append(PREP[4 * (s - 2) + 2 * (c // 4) + c % 4 - 1])
        return out

    def residual_of(s, c):
        k = 2 * s if c == 7 else 2 * s - 1
        return k if c in (3, 7) and 0 <= k < TILES else None

    def ordered(tail, prep):
        return [f for s in range(KEPT) for c in range(STEPS) for f in fills(s, c, tail, prep)]

    PREPS, BOTH, TAILS = (len(ordered(*kind)) for kind in ((False, True), (True, True), (True, False)))

    class Fills:

        def __init__(self, n, tail, prep):
            if n is None:
                self.base = 0
            elif tail:
                self.base = 2 * PREPS + BOTH * (n - 1)
                if isinstance(n, int) and n == BATCH:
                    self.base += TAILS - BOTH
            else:
                self.base = PREPS
            self.order = ordered(tail, prep)

        def of(self, fill):
            return self.base + self.order.index(fill) + 1

    with ExitStack() as mem:
        w_t = sb(mem, "e_w_t", [3, CH, C])
        w_o = sb(mem, "e_w_o", [CH, C])
        w_r = sb(mem, "e_w_r", [CH, HEADS])
        b_r = sb(mem, "e_b_r", [HEADS])
        b_qk = sb(mem, "e_b_qk", [CH, 2])
        b_v = sb(mem, "e_b_v", [CH, P])
        rows = sb(mem, "e_rows", [3, C])
        slot_of = sb(mem, "e_slot_of", [WIDE])
        head_of = sb(mem, "e_head_of", [CH, HEADS])
        before = sb(mem, "e_before", [HEADS, HEADS])
        tok = sb(mem, "e_tok", [TILES, C])
        img_mean = sb(mem, "e_img_mean", [TILES])
        img_rstd = sb(mem, "e_img_rstd", [TILES])
        img_shift = sb(mem, "e_img_shift", [TILES])
        minus_one = sb(mem, "e_minus_one", [TILES])
        h = [sb(mem, f"e_h{t}", [C]) for t in range(2)]
        h_t = [sb(mem, f"e_h_t{u}", [CH, PIX]) for u in range(2)]
        mean_h = sb(mem, "e_mean_h", [CH])
        mean_b = sb(mem, "e_mean_b", [CH, P])
        logit = sb(mem, "e_logit", [HEADS])
        beats = sb(mem, "e_beats", [HEADS, HEADS])
        ties = sb(mem, "e_ties", [HEADS, HEADS])
        rank = sb(mem, "e_rank", [HEADS])
        keep = sb(mem, "e_keep", [HEADS])
        by_ch = sb(mem, "e_by_ch", [2, CH, HEADS])
        ch_rank = sb(mem, "e_ch_rank", [2, CH])
        select = sb(mem, "e_select", [2, CH, WIDE])
        w_kept = [sb(mem, f"e_w_kept{u}", [3 * CH, WIDE]) for u in range(2)]
        wo_kept = [sb(mem, f"e_wo_kept{u}", [SIDES, C]) for u in range(2)]
        bias = [sb(mem, f"e_bias{u}", [KEPT]) for u in range(2)]
        bv_kept = sb(mem, "e_bv_kept", [WIDE])
        v = [sb(mem, f"e_v{u}", [TILES, KEPT, 2 * HD]) for u in range(2)]
        high = sb(mem, "e_high", [HALF], F32R)
        low = sb(mem, "e_low", [HALF], F32R)
        stack = [sb(mem, f"e_stack{i}", [2, PIX], F32R) for i in range(STACKS)]
        part_top = sb(mem, "e_part_top", [TILES, 2])
        top = sb(mem, "e_top", [TILES])
        prob = [sb(mem, f"e_prob{i}", [HALF]) for i in range(4)]
        den = sb(mem, "e_den", [HALF])
        ctx = [sb(mem, f"e_ctx{u}", [SIDES, PIX]) for u in range(2)]
        t_tok = [sb(mem, f"e_t_tok{i}", [C]) for i in range(2)]
        t_mean = sb(mem, "e_t_mean", [TILES])
        t_rstd = sb(mem, "e_t_rstd", [TILES])
        t_shift = sb(mem, "e_t_shift", [TILES])
        hb = [sb(mem, f"e_hb{i}", [C]) for i in range(2)]
        z = [sb(mem, f"e_z{i}", [C]) for i in range(2)]
        tst = sb(mem, "e_tst", [6])
        tmv = [sb(mem, f"e_tmv{i}", [2]) for i in range(2)]
        zvar = [sb(mem, f"e_zvar{i}", [1]) for i in range(2)]
        zrstd = [sb(mem, f"e_zrstd{i}", [1]) for i in range(2)]
        fin = [sb(mem, f"e_fin{i}", [CH, P]) for i in range(2)]
        b_next = [bank(mem, f"e_next{f}") for f in range(2)]
        b_s = [bank(mem, f"e_s{f}") for f in range(2)]
        b_acc = [bank(mem, f"e_acc{i}") for i in range(2)]
        b_x = bank(mem, "e_x")
        b_z = bank(mem, "e_z")

        consts = sem("e_consts")
        ones_set = sem("e_ones_set")
        tok_loaded = sem("e_tok_loaded")
        img_stats = sem("e_img_stats")
        h_ready = sem("e_h_ready")
        z_full = sem("e_z_full")
        z_free = sem("e_z_free")
        mean_ready = sem("e_mean_ready")
        select_ready = sem("e_select_ready")
        qk_psum = sem("e_qk_psum")
        high_ready = sem("e_high_ready")
        split_done = sem("e_split_done")
        stacked = [sem(f"e_stacked{i}") for i in range(STACKS)]
        next_psum = sem("e_next_psum")
        part_ready = sem("e_part_ready")
        top_ready = sem("e_top_ready")
        row_psum = sem("e_row_psum")
        row_ready = sem("e_row_ready")
        s_psum = sem("e_s_psum")
        prob_ready = sem("e_prob_ready")
        prob_used = sem("e_prob_used")
        den_ready = sem("e_den_ready")
        inverted = sem("e_inverted")
        acc_free = sem("e_acc_free")
        t_tok_loaded = [sem(f"e_t_tok_loaded{i}") for i in range(2)]
        t_stats = sem("e_t_stats")
        residual_made = sem("e_residual_made")
        hb_ready = sem("e_hb_ready")
        zvar_ready = sem("e_zvar_ready")
        zrstd_ready = sem("e_zrstd_ready")
        znorm_ready = sem("e_znorm_ready")
        z_ready = sem("e_z_ready")
        fin_ready = sem("e_fin_ready")
        written = [sem(f"e_written{i}") for i in range(2)]
        pchain = sem("e_pchain")
        tchain = sem("e_tchain")
        zchain = sem("e_zchain")
        rchain = sem("e_rchain")
        CONSTS = 10
        STACK_DMA = 16 * 12
        img_tokens = tokens.rearrange("(b t) p c -> b p t c", t=TILES)

        def head(n, s):
            return KEPT * n + s

        def stacked_count(n, s):
            return STACK_DMA * (2 * n + s // STACKS + 1)

        def turns(eng, turn):
            turn(0, 0, tail=False)
            with eng.Fori(0, BATCH // 2 - 1) as j:
                turn(2 * j + 1, 1)
                turn(2 * j + 2, 0)
            turn(LAST, 1, prep=False)

        with nc.Block() as block:
            @block.sync
            def _(sp):
                def load_image(n):
                    sp.dma_start(tok[:], img_tokens[n]).then_inc(tok_loaded, 16)

                def stack_up(n, s):
                    g, k = head(n, s), s % STACKS
                    sp.wait_ge(split_done, g + 1)
                    sp.nop(nofuse=True)
                    if not isinstance(g, int) or g >= STACKS:
                        sp.wait_ge(s_psum, UNITS * (g - STACKS + 1))
                        sp.nop(nofuse=True)

                    for w, order in enumerate(((high, high, low), (high, low, high))):
                        for at, src in enumerate(order):
                            for f in range(2):
                                part = slice(HD * (2 * w + f), HD * (2 * w + f + 1))
                                sp.dma_start(
                                    stack[k][HD * at:HD * (at + 1), w, f * HALF:(f + 1) * HALF].bitcast(F32),
                                    src[part].bitcast(F32)).then_inc(stacked[k], 16)

                def load_tile(n, k):
                    sp.wait_ge(z_ready, TILES * n + k + 1)
                    sp.nop(nofuse=True)
                    sp.dma_start(t_tok[k % 2][:], img_tokens[n, :, k]).then_inc(t_tok_loaded[k % 2], 16)

                def store(n, k):
                    sp.wait_ge(fin_ready, TILES * n + k + 1)
                    sp.nop(nofuse=True)
                    sp.dma_start(out_img[n, :, :, k * P:(k + 1) * P], fin[k % 2][:]).then_inc(written[k % 2], 16)

                def turn(n, tail=True, prep=True, load=True):
                    for s in range(KEPT):
                        if tail and s == 0:
                            load_tile(n - 1, 0)
                            load_tile(n - 1, 1)
                        if tail and 2 <= s <= 4:
                            load_tile(n - 1, 2 * s - 1)
                        if s + 2 < KEPT or prep:
                            stack_up(n if s + 2 < KEPT else n + 1, (s + 2) % KEPT)
                        if tail and s >= 2:
                            store(n - 1, 2 * s - 3)
                        if tail and 1 <= s <= 3:
                            load_tile(n - 1, 2 * s)
                        if tail and 1 <= s <= 4:
                            store(n - 1, 2 * s - 2)
                        if load and s == 1:
                            sp.wait_ge(h_ready, TILES * (n + 2))
                            sp.nop(nofuse=True)
                            load_image(n + 2)

                for dst, name in ((w_t, "w_t"), (w_o, "w_o"), (w_r, "w_r"), (b_r, "b_r"), (b_qk, "b_qk"), (b_v, "b_v"),
                                  (rows, "rows"), (slot_of, "slot_of"), (head_of, "head_of"), (before, "before")):
                    sp.dma_start(dst[:], io[name]).then_inc(consts, 16)
                load_image(0)
                sp.wait_ge(h_ready, TILES)
                load_image(1)
                stack_up(0, 0)
                stack_up(0, 1)
                turn(0, tail=False)
                with sp.Fori(1, LAST - 1) as n:
                    turn(n)
                turn(LAST - 1, load=False)
                turn(LAST, prep=False, load=False)
                load_tile(LAST, 0)
                load_tile(LAST, 1)
                for k in range(TILES):
                    if k + 2 < TILES:
                        load_tile(LAST, k + 2)
                    store(LAST, k)
                for i in range(2):
                    sp.wait_ge(written[i], 16 * (BLOCKS // 2 + 1))

            @block.gpsimd
            def _(pool):
                for u in range(2):
                    nc.gpsimd.memset(v[u][:], 1.0).then_inc(ones_set, 1)

                def statistics(n, counter, mean, rstd, shift):
                    blk = bass.ds(TILES * n, TILES)
                    c = Chain(pool, counter, 4 * n)
                    pool.nop(nofuse=True)
                    c.step(nc.gpsimd.tensor_copy(mean[:], token_stats[:, blk, 0]), apart=True)
                    c.step(nc.gpsimd.tensor_copy(rstd[:], token_rstd[:, blk]))
                    c.step(nc.gpsimd.tensor_tensor(shift[:], mean[:], rstd[:], ALU.mult))
                    nc.gpsimd.tensor_tensor(shift[:], shift[:], minus_one[:], ALU.mult).then_inc(counter, 1)

                def image_statistics(n):
                    if not isinstance(n, int) or n:
                        pool.wait_ge(h_ready, TILES * n)
                    statistics(n, img_stats, img_mean, img_rstd, img_shift)

                def tail_statistics(n):
                    if not isinstance(n, int) or n:
                        pool.wait_ge(residual_made, TILES * n)
                    statistics(n, t_stats, t_mean, t_rstd, t_shift)

                def add_bias(n, k):
                    pool.wait_ge(residual_made, TILES * n + k + 1)
                    nc.gpsimd.tensor_tensor(hb[k % 2][:], hb[k % 2][:], rows[:, 0], ALU.add).then_inc(hb_ready, 1)

                def root(n, k):
                    pool.wait_ge(zvar_ready, TILES * n + k + 1)
                    nc.gpsimd.tensor_tensor(zrstd[k % 2][:], zvar[k % 2][:], neg_half[:, 0:1], ALU.pow).then_inc(
                        zrstd_ready, 1)

                def finish(n, k):
                    i = k % 2
                    c = Chain(pool, zchain, 2 * (TILES * n + k))
                    pool.wait_ge(znorm_ready, TILES * n + k + 1)
                    c.step(nc.gpsimd.tensor_tensor(z[i][:], z[i][:], rows[:, 1], ALU.mult))
                    c.step(nc.gpsimd.tensor_tensor(z[i][:], z[i][:], rows[:, 2], ALU.add))
                    nc.gpsimd.tensor_tensor(z[i][:], z[i][:], t_tok[i][:], ALU.add).then_inc(z_ready, 1)

                def turn(n, u, tail=True, prep=True):
                    if prep:
                        image_statistics(n + 1)
                    if tail:
                        tail_statistics(n - 1)
                    for s in range(KEPT):
                        for c in range(STEPS):
                            if tail and 1 <= s <= 4 and c in (1, 5):
                                root(n - 1, 2 * (s - 1) + c // 4)
                            if tail and 1 <= s <= 4 and c in (2, 6):
                                finish(n - 1, 2 * (s - 1) + c // 4)
                            if tail and residual_of(s, c) is not None:
                                add_bias(n - 1, residual_of(s, c))

                nc.gpsimd.memset(minus_one[:], -1.0).then_inc(ones_set, 1)
                nc.gpsimd.memset(den[:], 1.0).then_inc(ones_set, 1)
                pool.wait_ge(ones_set, 4)
                pool.wait_ge(consts, 16 * CONSTS)
                image_statistics(0)
                turns(pool, turn)
                tail_statistics(LAST)
                add_bias(LAST, 0)
                for k in range(TILES):
                    root(LAST, k)
                    finish(LAST, k)
                    if k + 1 < TILES:
                        add_bias(LAST, k + 1)

            @block.vector
            def _(dve):
                dve.sem_inc(z_free, 1)
                dve.sem_inc(part_ready, 2)
                dve.sem_inc(prob_ready, 2)
                dve.sem_inc(prob_used, 4)
                dve.sem_inc(acc_free, 2)
                dve.sem_inc(z_ready, 2)
                for i in range(2):
                    dve.sem_inc(written[i], 16)
                dve.wait_ge(consts, 16 * CONSTS)
                dve.wait_ge(ones_set, 4)
                for i in range(STACKS):
                    nc.vector.tensor_scalar(stack[i][96:97, 1], v[0][96:97].rearrange("p t k d -> p (t k d)")[:, 0:PIX],
                                            -1.0, None, ALU.mult).then_inc(ones_set, 1)
                dve.wait_ge(ones_set, 4 + STACKS)

                def router(n, count):
                    c = Chain(dve, pchain, 11 * n)
                    dve.wait_ge(z_full, count.of(("logit", 0)))
                    c.step(nc.vector.tensor_tensor(logit[:], b_z[:, 0:HEADS], b_r[:], ALU.add))
                    dve.sem_inc(z_free, 1)
                    square = [P, HEADS, HEADS]
                    mine = logit[:].unsqueeze(2).to_broadcast(square)
                    other = logit[:].unsqueeze(1).to_broadcast(square)
                    nc.vector.tensor_tensor(beats[:], other, mine, ALU.is_gt)
                    c.step(nc.vector.tensor_tensor(ties[:], other, mine, ALU.is_equal))
                    c.step(nc.vector.tensor_tensor(ties[:], ties[:], before[:], ALU.mult))
                    c.step(nc.vector.tensor_tensor(beats[:], beats[:], ties[:], ALU.add))
                    c.step(nc.vector.reduce_sum(rank[:], beats[:], AX.X))
                    c.step(nc.vector.tensor_scalar(keep[:], rank[:], KEPT - 0.5, None, ALU.is_lt))
                    c.step(nc.vector.tensor_tensor(keep[:], keep[:], logit[:], ALU.add))
                    c.step(nc.vector.tensor_tensor(keep[:], keep[:], logit[:], ALU.subtract))
                    wide = [P, CH, HEADS]
                    nc.vector.tensor_tensor(by_ch[:, 0], head_of[:], rank[:].unsqueeze(1).to_broadcast(wide), ALU.mult)
                    c.step(nc.vector.tensor_tensor(by_ch[:, 1], head_of[:], keep[:].unsqueeze(1).to_broadcast(wide),
                                                   ALU.mult))
                    c.step(nc.vector.reduce_sum(ch_rank[:], by_ch[:], AX.X))
                    for o in range(CH):
                        nc.vector.tensor_scalar(select[:, 0, o], slot_of[:], ch_rank[:, 0, o:o + 1], None, ALU.is_equal)
                        last = nc.vector.tensor_scalar(select[:, 1, o], slot_of[:], ch_rank[:, 0, o:o + 1],
                                                       ch_rank[:, 1, o:o + 1], ALU.is_equal, ALU.mult)
                    c.step(last)
                    dve.sem_inc(select_ready, 1)
                    assert c.n == 11

                def mean(n, u, count):
                    dve.wait_ge(z_free, count.of(("h", TILES - 1)) + 1)
                    nc.vector.reduce_sum(mean_h[:], h_t[u][:], AX.X).then_inc(rchain, 1)
                    dve.wait_ge(rchain, n + 1)
                    nc.vector.tensor_scalar(mean_b[:], mean_h[:].unsqueeze(2).to_broadcast([P, CH, P]), 1.0 / PIX, None,
                                            ALU.mult).then_inc(mean_ready, 1)

                def take(n, u, fill, count):
                    kind, k = fill
                    if kind == "bias":
                        dve.wait_ge(z_full, count.of(fill))
                        for w in range(2):
                            part = slice(2 * HD * w, 2 * HD * (w + 1))
                            last = nc.vector.tensor_copy(
                                bias[u][part], b_z[part, 0:2 * KEPT].rearrange("p (s w) -> p s w", w=2)[:, :, w])
                        last.then_inc(z_free, 1)
                    elif kind == "v":
                        dve.wait_ge(z_full, count.of(fill))
                        nc.vector.tensor_tensor(
                            v[u][:, 2 * k:2 * k + 2, :, 0:HD],
                            b_z[:, 0:2 * WIDE].rearrange("p (t s d) -> p t s d", t=2, d=HD),
                            bv_kept[:].rearrange("p (s d) -> p s d", d=HD).unsqueeze(1).to_broadcast([P, 2, KEPT, HD]),
                            ALU.add).then_inc(z_free, 1)
                    elif kind == "logit":
                        router(n, count)
                    elif kind == "out":
                        i = k % 2
                        dve.wait_ge(hb_ready, TILES * n + k + 1)
                        dve.wait_ge(z_full, count.of(fill))
                        c = Chain(dve, tchain, 3 * (TILES * n + k))
                        c.step(nc.vector.tensor_tensor(z[i][:], b_z[:, 0:C], hb[i][:], ALU.add))
                        dve.sem_inc(z_free, 1)
                        c.step(nc.vector.bn_stats(tst[:], z[i][:]), apart=True)
                        c.step(nc.vector.bn_aggr(tmv[i][:], tst[:]))
                        nc.vector.tensor_scalar(zvar[i][:], tmv[i][:, 1:2], 1e-12, None, ALU.add).then_inc(zvar_ready, 1)

                def norm(n, k):
                    i = k % 2
                    dve.wait_ge(zrstd_ready, TILES * n + k + 1)
                    nc.vector.tensor_scalar(z[i][:], z[i][:], tmv[i][:, 0:1], zrstd[i][:], ALU.subtract,
                                            ALU.mult).then_inc(znorm_ready, 1)

                def split(n, s, u):
                    g = head(n, s)
                    dve.wait_ge(high_ready, g + 1)
                    nc.vector.scalar_tensor_tensor(low[:], b_x[:], bias[u][:, s:s + 1], high[:], ALU.add,
                                                   ALU.subtract).then_inc(split_done, 1)

                def maxima(n, s, t):
                    g = head(n, s)
                    if t % 4 == 0:
                        half = t // 4
                        if s or not isinstance(n, int) or n:
                            dve.wait_ge(top_ready, 2 * g + half - 1)
                    for f in range(2):
                        i = UNITS * g + 2 * t + f
                        dve.wait_ge(next_psum, i + 1)
                        nc.vector.reduce_max(part_top[:, t, f:f + 1], b_next[f][:], AX.X).then_inc(part_ready, 1)

                def join(n, s, half):
                    g = head(n, s)
                    dve.wait_ge(part_ready, UNITS * g + 8 * (half + 1) + 2)
                    part = slice(4 * half, 4 * half + 4)
                    nc.vector.reduce_max(top[:, part], part_top[:, part], AX.X).then_inc(top_ready, 1)

                def invert(n, s, piece):
                    if piece == 0:
                        dve.wait_ge(den_ready, head(n, s) + 1)
                    part = den[0:96, piece * P:(piece + 1) * P]
                    nc.vector.reciprocal(part, part).then_inc(inverted, 1)

                def divide(n, s, u):
                    g = head(n, s)
                    dve.wait_ge(inverted, 4 * (g + 1))
                    to = slice(HD * (s % 3), HD * (s % 3 + 1))
                    for f in range(2):
                        part = slice(2 * HD * f, 2 * HD * f + HD)
                        last = nc.vector.tensor_tensor(ctx[u][to, s // 3, f * HALF:(f + 1) * HALF],
                                                       b_acc[s % 2][part], den[part], ALU.mult)
                    last.then_inc(acc_free, 1)

                def turn(n, u, tail=True, prep=True):
                    count = Fills(n, tail, prep)
                    for s in range(KEPT):
                        for c in range(STEPS):
                            if s + 1 < KEPT or prep:
                                at = (n, s + 1) if s + 1 < KEPT else (n + 1, 0)
                                for t in NEXT_TILES[c]:
                                    maxima(*at, t)
                                if c in ROW_STEP:
                                    join(*at, ROW_STEP.index(c))
                            if c == 1 and s + 2 < KEPT:
                                split(n, s + 2, u)
                            elif c == 1 and prep:
                                split(n + 1, s + 2 - KEPT, 1 - u)
                            if s or tail:
                                before = (n, s - 1) if s else (n - 1, KEPT - 1)
                                if 3 <= c < 7:
                                    invert(*before, c - 3)
                                elif c == 7:
                                    divide(*before, u if s else 1 - u)
                            if tail and 1 <= s <= 4 and c in (2, 6):
                                norm(n - 1, 2 * (s - 1) + c // 4)
                            for f in fills(s - (c == 0), (c - 1) % STEPS, tail, prep):
                                of_before = f[0] in ("out", "turned")
                                take(n - 1 if of_before else n + 1, 1 - u, f, count)
                            if prep and s == 1 and c == 0:
                                mean(n + 1, 1 - u, count)

                first = Fills(None, False, True)
                for f in first.order:
                    if f[0] == "logit":
                        mean(0, 0, first)
                    take(0, 0, f, first)
                split(0, 0, 0)
                for t in range(TILES):
                    maxima(0, 0, t)
                    if t % 4 == 3:
                        join(0, 0, t // 4)
                split(0, 1, 0)
                turns(dve, turn)
                for piece in range(4):
                    invert(LAST, KEPT - 1, piece)
                divide(LAST, KEPT - 1, 1)
                last = Fills(BATCH, True, False)
                for f in last.order:
                    take(LAST, 1, f, last)
                    if f[0] == "out":
                        norm(LAST, f[1])

            @block.scalar
            def _(act):
                def take(n, u, fill, count):
                    kind, k = fill
                    if kind in ("h", "w", "wbv", "wo", "turned"):
                        act.wait_ge(z_full, count.of(fill))
                    if kind == "h":
                        nc.scalar.activation(h_t[u][:, :, k * P:(k + 1) * P],
                                             b_z[:, 0:C].rearrange("p (o q) -> p o q", q=P), ACT.Copy).then_inc(z_free, 1)
                    elif kind == "w":
                        nc.scalar.activation(w_kept[u][:, 2 * k:2 * k + 2],
                                             b_z[:, 0:2 * WIDE].rearrange("p (g k) -> p g k", g=2),
                                             ACT.Copy).then_inc(z_free, 1)
                    elif kind == "wbv":
                        nc.scalar.activation(w_kept[u][:, 2 * k], b_z[:, 0:WIDE], ACT.Copy)
                        nc.scalar.activation(bv_kept[:], b_z[:, WIDE:2 * WIDE], ACT.Copy).then_inc(z_free, 1)
                    elif kind == "wo":
                        nc.scalar.activation(wo_kept[u][0:LOT, k], b_z[0:LOT, 0:C], ACT.Copy).then_inc(z_free, 1)
                    elif kind == "turned":
                        act.wait_ge(written[k % 2], 16 * (TILES // 2 * n + k // 2 + 1))
                        nc.scalar.activation(fin[k % 2][:], b_z[:, 0:C].rearrange("p (o q) -> p o q", q=P),
                                             ACT.Copy).then_inc(fin_ready, 1)
                        act.wait_ge(fin_ready, TILES * n + k + 1)
                        act.sem_inc(z_free, 1)

                def normalise(n, t, z_of):
                    if t == 0:
                        act.wait_ge(tok_loaded, 16 * (n + 1))
                        act.wait_ge(img_stats, 4 * (n + 1))
                    if z_of is not None:
                        act.wait_ge(z_full, z_of)
                    nc.scalar.activation(h[t % 2][:], tok[:, t], ACT.Identity, bias=img_shift[:, t:t + 1],
                                         scale=img_rstd[:, t:t + 1]).then_inc(h_ready, 1)

                def residual(n, k):
                    i = k % 2
                    act.wait_ge(t_stats, 4 * (n + 1))
                    act.wait_ge(t_tok_loaded[i], 16 * (TILES // 2 * n + k // 2 + 1))
                    act.wait_ge(z_ready, TILES * n + k + 1)
                    nc.scalar.activation(hb[i][:], t_tok[i][:], ACT.Identity, bias=t_shift[:, k:k + 1],
                                         scale=t_rstd[:, k:k + 1]).then_inc(residual_made, 1)

                def project(n, s, u):
                    g = head(n, s)
                    act.wait_ge(qk_psum, g + 1)
                    if s:
                        act.wait_ge(stacked[(s - 1) % STACKS], stacked_count(n, s - 1))
                    elif not isinstance(n, int) or n:
                        act.wait_ge(stacked[(KEPT - 1) % STACKS], stacked_count(n - 1, KEPT - 1))
                    nc.scalar.activation(high[:], b_x[:], ACT.Identity, bias=bias[u][:, s:s + 1]).then_inc(high_ready, 1)

                def row(n, s, half):
                    g = head(n, s)
                    act.wait_ge(row_psum, 2 * g + half + 1)
                    nc.scalar.activation(stack[s % STACKS][96:97, 0, half * HALF:(half + 1) * HALF], b_x[96:97],
                                         ACT.Copy).then_inc(row_ready, 1)

                def exponentials(n, s, c):
                    for f in range(2):
                        i = UNITS * head(n, s) + 2 * c + f
                        act.wait_ge(s_psum, i + 1)
                        act.wait_ge(prob_used, i + 1)
                        nc.scalar.activation(prob[(2 * c + f) % 4][:], b_s[f][:], ACT.Exp, scale=SCALE).then_inc(
                            prob_ready, 1)

                def denominators(n, s):
                    g = head(n, s)
                    act.wait_ge(prob_used, UNITS * (g + 1) + 4)
                    act.wait_ge(acc_free, g + 2)
                    for f in range(2):
                        last = nc.scalar.activation(den[2 * HD * f:2 * HD * f + HD],
                                                    b_acc[s % 2][2 * HD * f + HD:2 * HD * (f + 1)], ACT.Copy)
                    last.then_inc(den_ready, 1)

                def turn(n, u, tail=True, prep=True):
                    count = Fills(n, tail, prep)
                    for s in range(KEPT):
                        for c in range(STEPS):
                            if c == 2 and s:
                                denominators(n, s - 1)
                            elif c == 2 and tail:
                                denominators(n - 1, KEPT - 1)
                            if c == 1 and s + 2 < KEPT:
                                project(n, s + 2, u)
                            elif c == 1 and prep:
                                project(n + 1, s + 2 - KEPT, 1 - u)
                            if prep and s == 0:
                                normalise(n + 1, c, count.of(("h", c - 2)) if c >= 2 else count.base)
                            exponentials(n, s, c)
                            for f in fills(s, c, tail, prep):
                                of_before = f[0] in ("out", "turned")
                                take(n - 1 if of_before else n + 1, 1 - u, f, count)
                            if tail and residual_of(s, c) is not None:
                                residual(n - 1, residual_of(s, c))
                            if c in ROW_STEP and s + 1 < KEPT:
                                row(n, s + 1, ROW_STEP.index(c))
                            elif c in ROW_STEP and prep:
                                row(n + 1, 0, ROW_STEP.index(c))

                act.wait_ge(consts, 16 * CONSTS)
                first = Fills(None, False, True)
                normalise(0, 0, None)
                for f in first.order:
                    if f[0] == "h" and f[1] + 1 < TILES:
                        t = f[1] + 1
                        normalise(0, t, first.of(("h", t - 2)) if t >= 2 else None)
                    take(0, 0, f, first)
                project(0, 0, 0)
                for half in range(2):
                    row(0, 0, half)
                project(0, 1, 0)
                turns(act, turn)
                denominators(LAST, KEPT - 1)
                last = Fills(BATCH, True, False)
                residual(LAST, 0)
                for f in last.order:
                    take(LAST, 1, f, last)
                    if f[0] == "out" and f[1] + 1 < TILES:
                        residual(LAST, f[1] + 1)

            @block.tensor
            def _(pe):
                pe.wait_ge(consts, 16 * CONSTS)
                pe.wait_ge(ones_set, 4 + STACKS)

                def fill(n, u, what, count):
                    kind, k = what
                    pe.wait_ge(z_free, count.of(what))
                    if kind == "h":
                        pe.wait_ge(h_ready, TILES * n + k + 1)
                        for o in range(CH):
                            last = nc.tensor.transpose(b_z[:, o * P:(o + 1) * P], h[k % 2][:, o * P:(o + 1) * P], ident[:])
                    elif kind == "logit":
                        pe.wait_ge(mean_ready, n + 1)
                        for o in range(CH):
                            last = nc.tensor.matmul(b_z[:, 0:HEADS], mean_b[:, o], w_r[:, o], start=(o == 0),
                                                    stop=(o == CH - 1))
                    elif kind in ("w", "wbv"):
                        if k == 0:
                            pe.wait_ge(select_ready, n + 1)
                        for i in range(2):
                            g = 2 * k + i
                            for co in range(CH):
                                if g < 3 * CH:
                                    w, ci = divmod(g, CH)
                                    src = w_t[:, w, co, ci * P:(ci + 1) * P]
                                else:
                                    src = b_v[:, co]
                                last = nc.tensor.matmul(b_z[:, i * WIDE:(i + 1) * WIDE], src, select[:, 1, co],
                                                        start=(co == 0), stop=(co == CH - 1))
                    elif kind == "bias":
                        for s in range(KEPT):
                            for co in range(CH):
                                for q in range(4):
                                    last = nc.tensor.matmul(b_z[HD * q:HD * (q + 1), 2 * s:2 * s + 2],
                                                            select[:, 1, co, s * HD:(s + 1) * HD], b_qk[:, co],
                                                            start=(co == 0), stop=(co == CH - 1))
                    elif kind == "wo":
                        for co in range(CH):
                            last = nc.tensor.matmul(b_z[0:LOT, 0:C], select[:, 0, co, k * LOT:(k + 1) * LOT], w_o[:, co],
                                                    start=(co == 0), stop=(co == CH - 1))
                    elif kind == "v":
                        for i in range(2):
                            t = 2 * k + i
                            for ci in range(CH):
                                last = nc.tensor.matmul(b_z[:, i * WIDE:(i + 1) * WIDE], h_t[u][:, ci, t * P:(t + 1) * P],
                                                        w_kept[u][:, 2 * CH + ci], start=(ci == 0), stop=(ci == CH - 1))
                    elif kind == "out":
                        if k == 0:
                            pe.wait_ge(acc_free, KEPT * (n + 1) + 2)
                        for g in range(SIDES):
                            last = nc.tensor.matmul(b_z[:, 0:C], ctx[u][0:LOT, g, k * P:(k + 1) * P], wo_kept[u][0:LOT, g],
                                                    start=(g == 0), stop=(g == SIDES - 1))
                    elif kind == "turned":
                        pe.wait_ge(z_ready, TILES * n + k + 3)
                        for o in range(CH):
                            last = nc.tensor.transpose(b_z[:, o * P:(o + 1) * P], z[k % 2][:, o * P:(o + 1) * P], ident[:])
                    last.then_inc(z_full, 1)

                def project(n, s, u, rows_before=0):
                    g = head(n, s)
                    if not isinstance(g, int) or g:
                        pe.wait_ge(split_done, g)
                        pe.wait_ge(row_ready, rows_before or 2 * (g - 1))
                    for ci in range(CH):
                        for w in range(2):
                            for f in range(2):
                                at = HD * (2 * w + f)
                                last = nc.tensor.matmul(b_x[at:at + HD], w_kept[u][:, CH * w + ci, s * HD:(s + 1) * HD],
                                                        h_t[u][:, ci, f * HALF:(f + 1) * HALF], start=(ci == 0),
                                                        stop=(ci == CH - 1))
                    last.then_inc(qk_psum, 1)

                def next_scores(n, s, t):
                    g, k = head(n, s), s % STACKS
                    if t == 0:
                        pe.wait_ge(stacked[k], stacked_count(n, s))
                    for f in range(2):
                        i = UNITS * g + 2 * t + f
                        pe.wait_ge(part_ready, i + 1)
                        nc.tensor.matmul(b_next[f][:], stack[k][0:96, 0, t * P:(t + 1) * P],
                                         stack[k][0:96, 1, f * HALF:(f + 1) * HALF], start=True, stop=True).then_inc(
                            next_psum, 1)

                def rows_of(n, s, half, first=False):
                    g = head(n, s)
                    pe.wait_ge(top_ready, 2 * g + half + 1)
                    pe.wait_ge(split_done, g + 1 if first else g + 2)
                    if half:
                        pe.wait_ge(row_ready, 2 * g + 1)
                    for t in range(4):
                        at = 4 * half + t
                        last = nc.tensor.matmul(b_x[96:97, t * P:(t + 1) * P], top[:, at:at + 1], ident[:], start=True,
                                                stop=True)
                    last.then_inc(row_psum, 1)

                def scores(n, s, c):
                    k = s % STACKS
                    for f in range(2):
                        i = UNITS * head(n, s) + 2 * c + f
                        pe.wait_ge(prob_ready, i + 1)
                        nc.tensor.matmul(b_s[f][:], stack[k][0:97, 1, c * P:(c + 1) * P],
                                         stack[k][0:97, 0, f * HALF:(f + 1) * HALF], start=True, stop=True).then_inc(
                            s_psum, 1)

                def mix(n, s, u, c):
                    g = head(n, s)
                    if c == 0:
                        pe.wait_ge(acc_free, g + 1)
                    pe.wait_ge(prob_ready, UNITS * g + 2 * c + 4)
                    for f in range(2):
                        at = 2 * HD * f
                        last = nc.tensor.matmul(b_acc[s % 2][at:at + 2 * HD], v[u][:, c, s], prob[(2 * c + f) % 4][:],
                                                start=(c == 0), stop=(c == STEPS - 1))
                        last.then_inc(prob_used, 1)

                def turn(n, u, tail=True, prep=True):
                    count = Fills(n, tail, prep)
                    for s in range(KEPT):
                        following = (n, s + 1) if s + 1 < KEPT else (n + 1, 0)
                        for c in range(STEPS):
                            if s + 1 < KEPT or prep:
                                for t in NEXT_TILES[c]:
                                    next_scores(*following, t)
                            if c >= 2:
                                mix(n, s, u, c - 2)
                            elif s:
                                mix(n, s - 1, u, STEPS + c - 2)
                            elif tail:
                                mix(n - 1, KEPT - 1, 1 - u, STEPS + c - 2)
                            if c == 0 and s + 2 < KEPT:
                                project(n, s + 2, u)
                            elif c == 0 and prep:
                                project(n + 1, s + 2 - KEPT, 1 - u)
                            elif c == 0:
                                pe.wait_ge(row_ready, 2 * (head(n, s) + 1))
                            scores(n, s, c)
                            for f in fills(s, c, tail, prep):
                                of_before = f[0] in ("out", "turned")
                                fill(n - 1 if of_before else n + 1, 1 - u, f, count)
                            if c in ROW_STEP and (s + 1 < KEPT or prep):
                                rows_of(*following, ROW_STEP.index(c), first=(not prep and s + 1 == KEPT - 1))

                first = Fills(None, False, True)
                for f in first.order:
                    fill(0, 0, f, first)
                project(0, 0, 0)
                for t in range(TILES):
                    next_scores(0, 0, t)
                for half in range(2):
                    rows_of(0, 0, half, first=True)
                project(0, 1, 0, rows_before=2)
                turns(pe, turn)
                mix(LAST, KEPT - 1, 1, STEPS - 2)
                mix(LAST, KEPT - 1, 1, STEPS - 1)
                last = Fills(BATCH, True, False)
                for f in last.order:
                    fill(LAST, 1, f, last)


def kernel(**inputs):
    import numpy as _np
    import concourse.bacc as _bacc
    from concourse import mybir as _mybir
    from concourse.bass_utils import run_bass_kernel_spmd as _run

    a = {k: _np.asarray(v) for k, v in inputs.items()}
    ow = a["L0_conv_off_w"].reshape(2 * TAPS, C, TAPS)
    ob = a["L0_conv_off_b"]
    off_w = _np.concatenate([ow[0::2], ow[1::2], a["L0_conv_mask_w"].reshape(TAPS, C, TAPS)])
    off_b = _np.concatenate([ob[0::2], ob[1::2], a["L0_conv_mask_b"]])

    def chunks(w):
        return w.reshape(CH, P, *w.shape[1:]).swapaxes(0, 1)

    arrays = dict(shape_constants())
    arrays["x"] = a["x"]
    w_off = chunks(off_w.transpose(1, 2, 0))
    arrays["w_off"] = _np.concatenate([w_off, _np.zeros_like(w_off[..., :32 - 3 * TAPS])], axis=-1)
    arrays["b_off"] = _np.tile(off_b, (P, 1))
    arrays["w_conv"] = chunks(a["L0_conv_proj_w"].reshape(C, C, TAPS).transpose(1, 2, 0)).swapaxes(1, 2)
    arrays["gamma"] = chunks(a["L0_conv_gamma"])
    arrays["beta"] = chunks(a["L0_conv_beta"])
    half = _np.concatenate([_np.arange(0, HD, 2), _np.arange(1, HD, 2)])
    order = (_np.arange(HEADS)[:, None] * HD + half).reshape(-1)
    partner = _np.roll(order.reshape(HEADS, HD), HD // 2, axis=1).reshape(-1)
    w = a["L1_attn_w_qkv"]
    arrays["w_qkv"] = chunks(_np.concatenate([w[:, order], w[:, C + order], w[:, 2 * C:]], axis=1))
    arrays["w_proj"] = chunks(a["L1_attn_w_proj"])
    ln = a["L1_attn_w_ln"]
    arrays["w_ln"] = _np.tile(_np.stack([ln[order], ln[partner]]), (P, 1, 1))
    arrays["w_t"] = _np.stack([chunks(a["L1_ffn_W" + k].T) for k in "qkv"], axis=1)
    arrays["w_o"] = chunks(a["L1_ffn_Wo"])
    arrays["w_r"] = chunks(a["L1_ffn_Wr"])
    arrays["b_r"] = _np.tile(a["L1_ffn_br"], (P, 1))
    arrays["b_qk"] = chunks(_np.stack([a["L1_ffn_bq"], a["L1_ffn_bk"]], axis=1))
    arrays["b_v"] = chunks(_np.tile(a["L1_ffn_bv"][:, None], (1, P)))
    arrays["rows"] = _np.tile(_np.stack([a["L1_ffn_bo"], a["L1_ffn_ln_g"], a["L1_ffn_ln_b"]]), (P, 1, 1))
    arrays["b_conv"] = chunks(a["L0_conv_proj_b"])

    nc = _bacc.Bacc("TRN2", target_bir_lowering=False, num_devices=1)
    io, fed = {}, {}
    for name, v in arrays.items():
        v = _np.ascontiguousarray(v)
        fed["in_" + name] = v
        io[name] = nc.dram_tensor("in_" + name, v.shape, _mybir.dt.from_np(v.dtype), kind="ExternalInput").ap()
    io["out"] = nc.dram_tensor("out_0", (BATCH, C, SIDE, SIDE), F32, kind="ExternalOutput").ap()
    build(nc, io)
    r = _run(nc, [fed], core_ids=[0])
    return r.results[0]["out_0"]
```
